# Optimizing a Trainium2 kernel written in Bass

```python
import numpy as np
import jax
import jax.numpy as jnp

def _softmax(x, axis=-1):
    return jax.nn.softmax(x, axis=axis)

def _gelu(x):
    return jax.nn.gelu(x, approximate=True)

def _silu(x):
    return jax.nn.silu(x)

def _sigmoid(x):
    return jax.nn.sigmoid(x)

def _layernorm(x, axis=-1, eps=1e-05):
    m = jnp.mean(x, axis=axis, keepdims=True)
    v = jnp.var(x, axis=axis, keepdims=True)
    return (x - m) / jnp.sqrt(v + eps)

def _scatter_add(tgt, idx, src, axis=0):
    return tgt.at[idx].add(src)

def _segment_sum(src, seg, n):
    return jax.ops.segment_sum(src, seg, n)
kernel_name = 'mk_decoder_postln_d1_seqx_r4_5b04f4'

def setup_inputs(seed: int=0):
    np.random.seed(seed)
    _w = jnp.asarray

    def _rec_inputs():
        import jax
        import jax.numpy as jnp
        _rk = jax.random.key(seed)
        x = 7.22e-05 + 1 * jax.random.normal(jax.random.fold_in(_rk, 1), (4, 512, 512), jnp.float32)
        _lenS = 512 - jax.random.randint(jax.random.fold_in(_rk, 7), (4,), 0, max(1, 512 // 4) + 1, jnp.int32)
        _lenS2 = 64 - jax.random.randint(jax.random.fold_in(_rk, 8), (4,), 0, max(1, 64 // 4) + 1, jnp.int32)
        _ctx_1024P = jax.random.normal(jax.random.fold_in(_rk, 11), (4, 16, 256), jnp.float32)
        _ctx_1024c = jax.random.dirichlet(jax.random.fold_in(_rk, 511), 0.3 * jnp.ones((16,), jnp.float32), (4, 64))
        _ctx_1024t = jnp.einsum('bsk,bkd->bsd', _ctx_1024c, _ctx_1024P)
        _ctx_1024t = _ctx_1024t * jax.lax.rsqrt(jnp.mean(jnp.square(_ctx_1024t)) + 1e-12) * 0.953939
        ctx_1024 = -0.000673644 + 1.00013 * (_ctx_1024t + 0.3 * jax.random.normal(jax.random.fold_in(_rk, 611), (4, 64, 256), jnp.float32))
        return (x, ctx_1024)
    x, ctx_1024 = _rec_inputs()

    def _L0_attn_setup():
        import jax, jax.numpy as jnp
        import numpy as np
        EPS = 1.1920929e-07

        def _rms(x):
            return x * jax.lax.rsqrt(jnp.mean(x * x, axis=-1, keepdims=True) + EPS)
        key = jax.random.key(seed)
        k0, k1, k2, k3 = jax.random.split(key, 4)
        B, S, D, DFF = (4, 512, 512, 2048)
        x = jax.random.normal(k0, (B, S, D), dtype=jnp.float32)
        w_qkv = jax.random.normal(k1, (3 * D, D), dtype=jnp.float32) * 0.02
        w_swiglu = jax.random.normal(k2, (2 * DFF, D), dtype=jnp.float32) * 0.02
        w_out = jax.random.normal(k3, (D, DFF), dtype=jnp.float32) * 0.02
        return {'x': x, 'w_qkv': w_qkv, 'w_swiglu': w_swiglu, 'w_out': w_out}
    _L0_attn_all = _L0_attn_setup()
    _L0_attn_in = {k: v for k, v in _L0_attn_all.items() if k in ('w_qkv', 'w_swiglu', 'w_out')}
    del _L0_attn_all

    def _L0_xattn_setup():
        import jax, jax.numpy as jnp
        import numpy as np
        B, S1, S2, DCA = (2, 512, 256, 16)
        QDIM, KDIM, H = (512, 256, 16)
        HD = QDIM // H
        SCALE = HD ** (-0.5)
        EPS = 1e-06
        DCA_WEIGHT = 1.0

        def _ln(t, w, b):
            m = jnp.mean(t, axis=-1, keepdims=True)
            v = jnp.var(t, axis=-1, keepdims=True)
            return (t - m) * jax.lax.rsqrt(v + EPS) * w + b

        def _attn(q, k, v):
            s = jnp.einsum('bhqd,bhkd->bhqk', q, k) * SCALE
            p = jax.nn.softmax(s, axis=-1)
            return jnp.einsum('bhqk,bhkd->bhqd', p, v)
        key = jax.random.key(seed)
        ks = jax.random.split(key, 8)
        w = lambda k, shape: jax.random.normal(k, shape, jnp.float32) * 0.02
        return {'x': jax.random.normal(ks[0], (B, S1, QDIM), jnp.float32), 'y': jax.random.normal(ks[1], (B, S2 + DCA, KDIM), jnp.float32), 'Wq': w(ks[2], (QDIM, QDIM)), 'bq': jnp.zeros((QDIM,), jnp.float32), 'Wk': w(ks[3], (KDIM, QDIM)), 'bk': jnp.zeros((QDIM,), jnp.float32), 'Wv': w(ks[4], (KDIM, QDIM)), 'bv': jnp.zeros((QDIM,), jnp.float32), 'Wkv_dca': w(ks[5], (KDIM, 2 * QDIM)), 'bkv_dca': jnp.zeros((2 * QDIM,), jnp.float32), 'qn_w': jnp.ones((HD,), jnp.float32), 'qn_b': jnp.zeros((HD,), jnp.float32), 'kn_w': jnp.ones((HD,), jnp.float32), 'kn_b': jnp.zeros((HD,), jnp.float32), 'kn_dca_w': jnp.ones((HD,), jnp.float32), 'kn_dca_b': jnp.zeros((HD,), jnp.float32), 'Wo': w(ks[6], (QDIM, QDIM)), 'bo': jnp.zeros((QDIM,), jnp.float32)}
    _L0_xattn_all = _L0_xattn_setup()
    _L0_xattn_in = {k: v for k, v in _L0_xattn_all.items() if k in ('Wq', 'bq', 'Wk', 'bk', 'Wv', 'bv', 'Wkv_dca', 'bkv_dca', 'qn_w', 'qn_b', 'kn_w', 'kn_b', 'kn_dca_w', 'kn_dca_b', 'Wo', 'bo')}
    del _L0_xattn_all

    def _L0_ffn_setup():
        import jax, jax.numpy as jnp
        import numpy as np
        B, S, D_IN, D_OUT, E = (4, 256, 512, 512, 32)
        MASK_DENSITY = 0.3
        THRESH = 0.5
        key = jax.random.key(seed)
        k_x, k_w, k_m, k_r = jax.random.split(key, 4)
        x = jax.random.normal(k_x, (B, S, D_IN), dtype=jnp.float32)
        bound = np.sqrt(1.0 / D_IN) * np.sqrt(3.0)
        weight = jax.random.uniform(k_w, (D_OUT, D_IN), minval=-bound, maxval=bound, dtype=jnp.float32)
        scale = jnp.ones((D_OUT,), dtype=jnp.float32)
        expert_masks = (jax.random.uniform(k_m, (E, D_OUT, D_IN)) < MASK_DENSITY).astype(jnp.float32)
        router_w = 0.01 * jax.random.normal(k_r, (E, D_IN), dtype=jnp.float32)
        return {'x': x, 'weight': weight, 'scale': scale, 'expert_masks': expert_masks, 'router_w': router_w}
    _L0_ffn_all = _L0_ffn_setup()
    _L0_ffn_in = {k: v for k, v in _L0_ffn_all.items() if k in ('weight', 'scale', 'expert_masks', 'router_w')}
    del _L0_ffn_all
    return {'x': x, 'ctx_1024': ctx_1024, 'L0_attn_w_qkv': _L0_attn_in['w_qkv'], 'L0_attn_w_swiglu': _L0_attn_in['w_swiglu'], 'L0_attn_w_out': _L0_attn_in['w_out'], 'L0_xattn_Wq': _L0_xattn_in['Wq'], 'L0_xattn_bq': _L0_xattn_in['bq'], 'L0_xattn_Wk': _L0_xattn_in['Wk'], 'L0_xattn_bk': _L0_xattn_in['bk'], 'L0_xattn_Wv': _L0_xattn_in['Wv'], 'L0_xattn_bv': _L0_xattn_in['bv'], 'L0_xattn_Wkv_dca': _L0_xattn_in['Wkv_dca'], 'L0_xattn_bkv_dca': _L0_xattn_in['bkv_dca'], 'L0_xattn_qn_w': _L0_xattn_in['qn_w'], 'L0_xattn_qn_b': _L0_xattn_in['qn_b'], 'L0_xattn_kn_w': _L0_xattn_in['kn_w'], 'L0_xattn_kn_b': _L0_xattn_in['kn_b'], 'L0_xattn_kn_dca_w': _L0_xattn_in['kn_dca_w'], 'L0_xattn_kn_dca_b': _L0_xattn_in['kn_dca_b'], 'L0_xattn_Wo': _L0_xattn_in['Wo'], 'L0_xattn_bo': _L0_xattn_in['bo'], 'L0_ffn_weight': _L0_ffn_in['weight'], 'L0_ffn_scale': _L0_ffn_in['scale'], 'L0_ffn_expert_masks': _L0_ffn_in['expert_masks'], 'L0_ffn_router_w': _L0_ffn_in['router_w']}

def reference(x, ctx_1024, L0_attn_w_qkv, L0_attn_w_swiglu, L0_attn_w_out, L0_xattn_Wq, L0_xattn_bq, L0_xattn_Wk, L0_xattn_bk, L0_xattn_Wv, L0_xattn_bv, L0_xattn_Wkv_dca, L0_xattn_bkv_dca, L0_xattn_qn_w, L0_xattn_qn_b, L0_xattn_kn_w, L0_xattn_kn_b, L0_xattn_kn_dca_w, L0_xattn_kn_dca_b, L0_xattn_Wo, L0_xattn_bo, L0_ffn_weight, L0_ffn_scale, L0_ffn_expert_masks, L0_ffn_router_w):
    import jax
    import jax.numpy as jnp

    def _L0_attn_ref(x, w_qkv, w_swiglu, w_out):
        import jax, jax.numpy as jnp
        import numpy as np
        EPS = 1.1920929e-07

        def _rms(x):
            return x * jax.lax.rsqrt(jnp.mean(x * x, axis=-1, keepdims=True) + EPS)
        qkv = _rms(x) @ w_qkv.T
        q, k, v = jnp.split(qkv, 3, axis=-1)
        q = _rms(q)
        k = _rms(k)
        w = jnp.exp(k)
        kv_cum = jnp.cumsum(w * v, axis=1)
        w_cum = jnp.cumsum(w, axis=1)
        y = jax.nn.sigmoid(q) * (kv_cum / (w_cum + 1e-06))
        uv = y @ w_swiglu.T
        u, g = jnp.split(uv, 2, axis=-1)
        return x + u * jax.nn.silu(g) @ w_out.T

    def _L0_xattn_ref(x, y, Wq, bq, Wk, bk, Wv, bv, Wkv_dca, bkv_dca, qn_w, qn_b, kn_w, kn_b, kn_dca_w, kn_dca_b, Wo, bo):
        import jax, jax.numpy as jnp
        import numpy as np
        B, S1, S2, DCA = (2, 512, 256, 16)
        QDIM, KDIM, H = (512, 256, 16)
        HD = QDIM // H
        SCALE = HD ** (-0.5)
        EPS = 1e-06
        DCA_WEIGHT = 1.0

        def _ln(t, w, b):
            m = jnp.mean(t, axis=-1, keepdims=True)
            v = jnp.var(t, axis=-1, keepdims=True)
            return (t - m) * jax.lax.rsqrt(v + EPS) * w + b

        def _attn(q, k, v):
            s = jnp.einsum('bhqd,bhkd->bhqk', q, k) * SCALE
            p = jax.nn.softmax(s, axis=-1)
            return jnp.einsum('bhqk,bhkd->bhqd', p, v)
        b, s1, _ = x.shape
        y_dca = y[:, -DCA:, :]
        y_main = y[:, :-DCA, :]
        kv_dca = (y_dca @ Wkv_dca + bkv_dca).reshape(b, DCA, 2, H, HD)
        k_dca = _ln(kv_dca[:, :, 0], kn_dca_w, kn_dca_b)
        v_dca = kv_dca[:, :, 1]
        s2 = y_main.shape[1]
        q = _ln((x @ Wq + bq).reshape(b, s1, H, HD), qn_w, qn_b)
        kv = jnp.concatenate([y_main @ Wk + bk, y_main @ Wv + bv], axis=-1)
        kv = kv.reshape(b, s2, H, 2 * HD)
        k = _ln(kv[..., :HD], kn_w, kn_b)
        v = kv[..., HD:]
        qT = q.transpose(0, 2, 1, 3)
        ctx = _attn(qT, k.transpose(0, 2, 1, 3), v.transpose(0, 2, 1, 3))
        ctx = ctx.transpose(0, 2, 1, 3).reshape(b, s1, QDIM)
        ctx_dca = _attn(qT, k_dca.transpose(0, 2, 1, 3), v_dca.transpose(0, 2, 1, 3))
        ctx_dca = ctx_dca.transpose(0, 2, 1, 3).reshape(b, s1, QDIM)
        ctx = ctx + DCA_WEIGHT * ctx_dca
        return ctx @ Wo + bo

    def _L0_ffn_ref(x, weight, scale, expert_masks, router_w):
        import jax, jax.numpy as jnp
        import numpy as np
        B, S, D_IN, D_OUT, E = (4, 256, 512, 512, 32)
        MASK_DENSITY = 0.3
        THRESH = 0.5
        logits = jnp.einsum('bsd,ed->bse', x, router_w)
        probs = jax.nn.softmax(logits, axis=-1)
        top1_w = jnp.max(probs, axis=-1)
        top1_idx = jnp.argmax(probs, axis=-1)
        w_q = jnp.clip(jnp.round(weight / THRESH), -1.0, 1.0)
        w_scaled = w_q * scale[:, None]
        out0 = jnp.zeros((x.shape[0], x.shape[1], weight.shape[0]), dtype=x.dtype)

        def body(out, inputs):
            e_idx, mask_e = inputs
            y = jnp.einsum('bsi,oi->bso', x, w_scaled * mask_e)
            sel = (top1_idx == e_idx)[..., None]
            out = jnp.where(sel, y * top1_w[..., None], out)
            return (out, None)
        out, _ = jax.lax.scan(body, out0, (jnp.arange(E), expert_masks))
        return out
    x = _layernorm(x + _L0_attn_ref(x, L0_attn_w_qkv, L0_attn_w_swiglu, L0_attn_w_out), axis=-1)
    x = _layernorm(x + _L0_xattn_ref(x, ctx_1024, L0_xattn_Wq, L0_xattn_bq, L0_xattn_Wk, L0_xattn_bk, L0_xattn_Wv, L0_xattn_bv, L0_xattn_Wkv_dca, L0_xattn_bkv_dca, L0_xattn_qn_w, L0_xattn_qn_b, L0_xattn_kn_w, L0_xattn_kn_b, L0_xattn_kn_dca_w, L0_xattn_kn_dca_b, L0_xattn_Wo, L0_xattn_bo), axis=-1)
    x = _layernorm(x + _L0_ffn_ref(x, L0_ffn_weight, L0_ffn_scale, L0_ffn_expert_masks, L0_ffn_router_w), axis=-1)
    return x

_drawn_inputs = setup_inputs


def setup_inputs(seed=0):
    import zlib

    import numpy as np

    out = dict(_drawn_inputs(seed))
    spreads = {'L0_xattn_bq': (0.0, 0.67),
     'L0_xattn_bk': (0.0, 0.1),
     'L0_xattn_bv': (0.0, 0.1),
     'L0_xattn_bkv_dca': (0.0, 0.1),
     'L0_xattn_qn_w': (1.0, 0.6),
     'L0_xattn_qn_b': (0.0, 0.8),
     'L0_xattn_kn_w': (1.0, 0.6),
     'L0_xattn_kn_b': (0.0, 0.8),
     'L0_xattn_kn_dca_w': (1.0, 0.6),
     'L0_xattn_kn_dca_b': (0.0, 0.8),
     'L0_xattn_bo': (0.0, 0.1),
     'L0_ffn_scale': (1.0, 0.2)}
    factors = {'L0_attn_w_qkv': 8.0, 'L0_attn_w_swiglu': 8.0, 'L0_attn_w_out': 8.0}
    for name, (base, spread) in spreads.items():
        noise = np.random.default_rng([zlib.crc32(name.encode()), seed]).standard_normal(out[name].shape)
        drawn = base * np.exp(spread * noise) if base else spread * noise
        out[name] = jnp.asarray(drawn.astype(out[name].dtype))
    for name, factor in factors.items():
        out[name] = (out[name] * factor).astype(out[name].dtype)
    return out
```

```python
import numpy as np
import concourse.bass as bass
from concourse import mybir
from contextlib import ExitStack

fp32 = mybir.dt.float32
fp32r = mybir.dt.float32r
bf16 = mybir.dt.bfloat16
i32 = mybir.dt.int32
u32 = mybir.dt.uint32
ALU = mybir.AluOpType
ACT = mybir.ActivationFunctionType
AX = mybir.AxisListType

P = 128
NBATCH = 4
S = 512
T = NBATCH * S
D = 512
DC = D // P
EPS_RMS = 1.1920929e-07
EPS_CUM = 1e-6


def this(i, n, m):
    return n * (i + 1) + m


def last(i, n, m):
    return n * i + m


def stage_qkv(nc, ins, xyh, xyl, scratch, bank):
    xT, wqkvT = ins["xT"], ins["wqkvT"]
    LOADS = [("w", 1), ("x", 0), ("w", 0), ("w", 2), ("x", 1), ("x", 2), ("x", 3)]
    RING = 6
    K, Q, V = 0, 1, 2
    W_OF = {K: 1, Q: 0, V: 2}
    N_PROJ, N_KQ, N_ADD, N_C, N_ROOT, N_STEP = 3 * DC, 2 * DC, 6, 6, 4, 9 * DC

    with ExitStack() as held:
        def sb(name, shape, dtype):
            return held.enter_context(nc.sbuf_tensor(name, shape, dtype))

        def sem(name):
            return held.enter_context(nc.semaphore(name))

        raw = scratch[:, 0:2 * DC, :].rearrange("p (n c) t -> p n c t", c=DC)
        sq = scratch[:, 2 * DC:4 * DC, :]
        wh = sb("a_wh", [P, 3, DC, D], fp32r)
        wl = sb("a_wl", [P, 3, DC, D], fp32r)
        qbuf = sb("a_q", [P, 2 * DC, S], fp32)
        kbuf = sb("a_k", [P, 2 * DC, S], fp32)
        vbuf = sb("a_v", [P, 2, S], fp32)
        wcum = sb("a_wcum", [P, 2, S], fp32)
        kvcum = sb("a_kvcum", [P, 2, S], fp32)
        sqsum = sb("a_sqsum", [P, 2, S], fp32)
        rx = sb("a_r", [P, NBATCH, S], fp32)
        ckq = sb("a_ckq", [P, 2, S], fp32)
        mean_w = sb("a_mean", [P, P], fp32)
        eps = sb("a_eps", [P, 1], fp32)
        raw0_in = sem("a_raw0_in")
        raw1_in = sem("a_raw1_in")
        consts = sem("a_consts")
        hi_made = sem("a_hi_made")
        lo_made = sem("a_lo_made")
        xsq_made = sem("a_xsq_made")
        xsq_add = sem("a_xsq_add")
        x_ms = sem("a_x_ms")
        x_root = sem("a_x_root")
        proj = sem("a_proj")
        kq_read = sem("a_kq_read")
        kq_copied = sem("a_kq_copied")
        sq_add = sem("a_sq_add")
        ms_made = sem("a_ms_made")
        c_scaled = sem("a_c_scaled")
        c_root = sem("a_c_root")
        normed = sem("a_normed")
        exped = sem("a_exped")
        y_steps = sem("a_y_steps")
        block = held.enter_context(nc.Block())
        raw_in = [raw0_in, raw1_in]
        looped = [(proj, N_PROJ), (kq_read, N_KQ), (kq_copied, N_KQ), (sq_add, N_ADD), (ms_made, 2),
                  (c_scaled, N_C), (c_root, N_ROOT), (normed, N_KQ), (exped, N_KQ), (y_steps, N_STEP)]

        def split_target(l):
            kind, n = LOADS[l]
            if kind == "w":
                return wh[:, n], wl[:, n]
            return xyh[:, :, n * S:(n + 1) * S], xyl[:, :, n * S:(n + 1) * S]

        def half(buf, par, c):
            return buf[:, par * DC + c, :]

        def tokens(buf, b, c):
            return buf[:, c, bass.ds(b * S, S)]

        @block.sync
        def _(sp):
            seen = 0
            for l, (kind, n) in enumerate(LOADS):
                if l >= 2:
                    sp.wait_ge(lo_made, l - 1)
                    if LOADS[l - 2][0] == "x":
                        seen += 1
                        sp.wait_ge(xsq_made, seen)
                src = wqkvT[n] if kind == "w" else xT[n]
                sp.dma_start(raw[:, l % 2], src.rearrange("(c p) t -> p c t", p=P)).then_inc(raw_in[l % 2], 16)

        @block.tensor
        def _(pe):
            def mean_square(out, src):
                return nc.tensor.matmul(out[:, :], mean_w[:, :], src, start=True, stop=True)

            pe.wait_ge(consts, 2)
            for n in range(NBATCH):
                pe.wait_ge(xsq_add, 2 * n + 2)
                if n >= 2:
                    pe.wait_ge(x_root, 2 * (n - 2) + 1)
                mean_square(bank[6 + n % 2], sqsum[:, n % 2]).then_inc(x_ms, 1)
            pe.wait_ge(x_root, 2 * NBATCH)
            pe.wait_ge(lo_made, len(LOADS))
            with pe.Fori(0, NBATCH // 2) as pair:
                for par in range(2):
                    b = pair * 2 + par
                    for j in range(N_PROJ):
                        which, c = j // DC, j % DC
                        if j < 2:
                            pe.wait_ge(kq_read, last(b, N_KQ, 7 + j))
                        elif j < RING:
                            pe.wait_ge(y_steps, last(b, N_STEP, 9 * (j - 2) + 1))
                        else:
                            pe.wait_ge(kq_read, this(b, N_KQ, j - RING + 1))
                        out = bank[j % RING][:, :]
                        w, cols = W_OF[which], slice(c * P, (c + 1) * P)
                        for kc in range(DC):
                            xh, xl = tokens(xyh, b, kc), tokens(xyl, b, kc)
                            nc.tensor.matmul(out, wh[:, w, kc, cols], xl, start=kc == 0, stop=False)
                            nc.tensor.matmul(out, wh[:, w, kc, cols], xh, start=False, stop=False)
                            mm = nc.tensor.matmul(out, wl[:, w, kc, cols], xh, start=False, stop=kc == DC - 1)
                        mm.then_inc(proj, 1)
                        if j == DC + 2 or j == 2 * DC + 2:
                            w = j // DC - 1
                            pe.wait_ge(sq_add, this(b, N_ADD, 3 * w + 3))
                            pe.wait_ge(c_scaled, last(b, N_C, 3 * w + 1))
                            mean_square(bank[6 + w], sqsum[:, w]).then_inc(ms_made, 1)

        @block.scalar
        def _(act):
            def root(dst, src, sem, value):
                nc.scalar.activation(dst, src, ACT.Ln, bias=eps[:, 0:1]).then_inc(sem, 1)
                act.wait_ge(sem, value)
                nc.scalar.activation(dst, dst, ACT.Exp, scale=-0.5).then_inc(sem, 1)

            nc.scalar.preload_act_table_set("natural_log_exp_and_others")
            act.wait_ge(consts, 2)
            xs = 0
            for l, (kind, n) in enumerate(LOADS):
                act.wait_ge(raw_in[l % 2], 16 * (l // 2 + 1))
                hi, _ = split_target(l)
                nc.scalar.activation(hi, raw[:, l % 2], ACT.Copy).then_inc(hi_made, 1)
                if kind == "x":
                    if xs:
                        act.wait_ge(xsq_add, 2 * xs)
                    nc.scalar.activation(sq[:, 0:DC, :], raw[:, l % 2], ACT.Square).then_inc(xsq_made, 1)
                    xs += 1
            for n in range(NBATCH):
                act.wait_ge(x_ms, n + 1)
                root(rx[:, n], bank[6 + n % 2][:, :], x_root, 2 * n + 1)
            act.wait_ge(xsq_add, 2 * NBATCH)

            with act.Fori(0, NBATCH // 2) as pair:
                for par in range(2):
                    b = pair * 2 + par
                    for j in range(2 * DC):
                        buf, c = (kbuf, qbuf)[j // DC], j % DC
                        act.wait_ge(proj, this(b, N_PROJ, j + 1))
                        if j == 0:
                            act.wait_ge(sq_add, last(b, N_ADD, 6))
                            act.wait_ge(y_steps, last(b, N_STEP, 1))
                        nc.scalar.activation(half(buf, par, c), bank[j % RING][:, :], ACT.Copy).then_inc(kq_copied, 1)
                        nc.scalar.activation(sq[:, j], bank[j % RING][:, :], ACT.Square).then_inc(kq_read, 1)
                    for w, buf in enumerate((kbuf, qbuf)):
                        act.wait_ge(c_scaled, this(b, N_C, 3 * w + 2))
                        root(ckq[:, w], ckq[:, w], c_root, this(b, N_ROOT, 2 * w + 1))
                        for c in range(DC):
                            act.wait_ge(normed, this(b, N_KQ, DC * w + c + 1))
                            nc.scalar.activation(half(buf, par, c), half(buf, par, c), ACT.Exp,
                                                 scale=(1.0, -1.0)[w]).then_inc(exped, 1)

        @block.gpsimd
        def _(pool):
            nc.gpsimd.memset(mean_w[:, :], 1.0 / D).then_inc(consts, 1)
            nc.gpsimd.memset(eps[:, :], EPS_RMS).then_inc(consts, 1)
            for sem, n in looped:
                pool.sem_inc(sem, n)
            for n in range(NBATCH):
                pool.wait_ge(xsq_made, n + 1)
                if n >= 2:
                    pool.wait_ge(x_ms, n - 1)
                nc.gpsimd.tensor_tensor(sq[:, 0:2], sq[:, 0:2], sq[:, 2:4], ALU.add).then_inc(xsq_add, 1)
                pool.wait_ge(xsq_add, 2 * n + 1)
                nc.gpsimd.tensor_tensor(sqsum[:, n % 2], sq[:, 0], sq[:, 1], ALU.add).then_inc(xsq_add, 1)
            pool.wait_ge(x_ms, NBATCH)
            with pool.Fori(0, NBATCH // 2) as pair:
                for par in range(2):
                    b = pair * 2 + par
                    for w, buf in enumerate((kbuf, qbuf)):
                        for c in range(1, DC):
                            pool.wait_ge(kq_read, this(b, N_KQ, DC * w + c + 1))
                            if c == 1:
                                pool.wait_ge(ms_made, last(b, 2, w + 1))
                            else:
                                pool.wait_ge(sq_add, this(b, N_ADD, 3 * w + c - 1))
                            nc.gpsimd.tensor_tensor(sqsum[:, w], sq[:, DC * w] if c == 1 else sqsum[:, w],
                                                    sq[:, DC * w + c], ALU.add).then_inc(sq_add, 1)
                    for w, buf in enumerate((kbuf, qbuf)):
                        pool.wait_ge(c_scaled, this(b, N_C, 3 * w + 3))
                        for c in range(DC):
                            nc.gpsimd.tensor_tensor(half(buf, par, c), half(buf, par, c), ckq[:, w],
                                                    ALU.mult).then_inc(normed, 1)

        @block.vector
        def _(dve):
            for l in range(len(LOADS)):
                dve.wait_ge(hi_made, l + 1)
                hi, lo = split_target(l)
                nc.vector.tensor_tensor(lo, raw[:, l % 2], hi.bitcast(fp32), ALU.subtract).then_inc(lo_made, 1)
            dve.wait_ge(x_root, 2 * NBATCH)
            with dve.Fori(0, NBATCH // 2) as pair:
                for par in range(2):
                    b = pair * 2 + par
                    r = rx[:, bass.ds(b, 1), :].rearrange("p o t -> p (o t)")
                    for w in range(2):
                        dve.wait_ge(ms_made, this(b, 2, w + 1))
                        dve.wait_ge(normed, last(b, N_KQ, DC * w + DC))
                        nc.vector.tensor_tensor(ckq[:, w], bank[6 + w][:, :], r, ALU.mult).then_inc(c_scaled, 1)
                        dve.wait_ge(c_scaled, this(b, N_C, 3 * w + 1))
                        nc.vector.tensor_tensor(ckq[:, w], ckq[:, w], r, ALU.mult).then_inc(c_scaled, 1)
                        dve.wait_ge(c_root, this(b, N_ROOT, 2 * w + 2))
                        nc.vector.tensor_tensor(ckq[:, w], ckq[:, w], r, ALU.mult).then_inc(c_scaled, 1)
                    for c in range(DC):
                        h = c % 2
                        st = lambda m: this(b, N_STEP, 9 * c + m)
                        expk, expq = half(kbuf, par, c), half(qbuf, par, c)
                        dve.wait_ge(proj, this(b, N_PROJ, 2 * DC + c + 1))
                        nc.vector.tensor_tensor(vbuf[:, h], bank[(2 * DC + c) % RING][:, :], r, ALU.mult).then_inc(y_steps, 1)
                        dve.wait_ge(exped, this(b, N_KQ, c + 1))
                        nc.vector.tensor_tensor_scan(wcum[:, h], expk, expk, EPS_CUM, ALU.add, ALU.bypass).then_inc(y_steps, 1)
                        dve.wait_ge(y_steps, st(1))
                        nc.vector.tensor_tensor(vbuf[:, h], vbuf[:, h], expk, ALU.mult).then_inc(y_steps, 1)
                        dve.wait_ge(y_steps, st(3))
                        nc.vector.tensor_tensor_scan(kvcum[:, h], vbuf[:, h], vbuf[:, h], 0.0, ALU.add, ALU.bypass).then_inc(y_steps, 1)
                        dve.wait_ge(exped, this(b, N_KQ, DC + c + 1))
                        nc.vector.scalar_tensor_tensor(wcum[:, h], expq, 1.0, wcum[:, h], ALU.add, ALU.mult).then_inc(y_steps, 1)
                        dve.wait_ge(y_steps, st(5))
                        nc.vector.reciprocal(wcum[:, h], wcum[:, h]).then_inc(y_steps, 1)
                        dve.wait_ge(y_steps, st(6))
                        nc.vector.tensor_tensor(kvcum[:, h], kvcum[:, h], wcum[:, h], ALU.mult).then_inc(y_steps, 1)
                        dve.wait_ge(proj, this(b, N_PROJ, N_PROJ))
                        dve.wait_ge(y_steps, st(7))
                        nc.vector.tensor_copy(tokens(xyh, b, c), kvcum[:, h]).then_inc(y_steps, 1)
                        dve.wait_ge(y_steps, st(8))
                        nc.vector.tensor_tensor(tokens(xyl, b, c), kvcum[:, h], tokens(xyh, b, c).bitcast(fp32),
                                                ALU.subtract).then_inc(y_steps, 1)


def stage_swiglu(nc, ins, yh, yl, acc, zero_filled, bank):
    x, wsT, woT = ins["x"], ins["wsT"], ins["woT"]
    NE = 8
    FE = 2048 // NE
    FC = FE // P
    STEPS = 2 * NBATCH
    N_UV, N_OUT = FC * STEPS, 4 * STEPS

    with ExitStack() as held:
        def sb(name, shape, dtype):
            return held.enter_context(nc.sbuf_tensor(name, shape, dtype))

        def sem(name):
            return held.enter_context(nc.semaphore(name))

        raw_s = sb("f_raw_s", [P, DC, 2, FE], fp32)
        raw_o = sb("f_raw_o", [P, FC, D], fp32)
        sh = [sb(f"f_sh{i}", [P, DC, 2, FE], fp32r) for i in range(2)]
        sl = [sb(f"f_sl{i}", [P, DC, 2, FE], fp32r) for i in range(2)]
        oh = [sb(f"f_oh{i}", [P, FC, D], fp32r) for i in range(2)]
        ol = [sb(f"f_ol{i}", [P, FC, D], fp32r) for i in range(2)]
        silu = sb("f_silu", [P, FC, S], fp32)
        hf = [sb(f"f_h{i}", [P, FC, S], fp32) for i in range(2)]
        hh = [sb(f"f_hh{i}", [P, FC, S], fp32r) for i in range(2)]
        hl = [sb(f"f_hl{i}", [P, FC, S], fp32r) for i in range(2)]
        x_in, s_in, o_in = sem("f_x_in"), sem("f_s_in"), sem("f_o_in")
        x_doubled = sem("f_x_doubled")
        w_hi, w_lo = sem("f_w_hi"), sem("f_w_lo")
        uv_done, silu_done, h_done = sem("f_uv_done"), sem("f_silu_done"), sem("f_h_done")
        h_hi, h_lo = sem("f_h_hi"), sem("f_h_lo")
        out_done, added = sem("f_out_done"), sem("f_added")
        credit = [(uv_done, N_UV), (silu_done, N_UV), (h_done, N_UV), (h_hi, N_UV), (h_lo, N_UV),
                  (out_done, N_OUT), (added, N_OUT)]
        block = held.enter_context(nc.Block())

        def of(i, n, per, s, m):
            return this(i, n, per * s + m) if s >= 0 else last(i, n, per * (s + STEPS) + m)

        def passes(eng, body):
            with eng.Fori(0, NE // 2 - 1) as i:
                body(i, False)
            body(NE // 2 - 1, True)

        @block.sync
        def _(sp):
            def load(e, free):
                if free is not None:
                    sp.wait_ge(w_lo, free)
                sp.dma_start(raw_s[:, :, :, :], wsT[e] if type(e) is int else
                             wsT[bass.ds(e, 1)].rearrange("o p c u f -> p (o c) u f")).then_inc(s_in, 16)
                sp.dma_start(raw_o[:, :, :], woT[e] if type(e) is int else
                             woT[bass.ds(e, 1)].rearrange("o p c f -> p (o c) f")).then_inc(o_in, 16)

            load(0, None)
            sp.dma_start(acc[:, :, :], x.rearrange("(n p) d -> p n d", p=P)).then_inc(x_in, 16)

            def body(i, final):
                for half in range(1 if final else 2):
                    load(2 * i + half + 1, 2 * (2 * i + half + 1))
            passes(sp, body)
            sp.wait_ge(zero_filled, 16)

        @block.gpsimd
        def _(pool):
            for s, n in credit:
                pool.sem_inc(s, n)

        @block.tensor
        def _(pe):
            def up(i, s):
                w, b = s // NBATCH, s % NBATCH
                for c in range(FC):
                    pe.wait_ge(h_done, of(i, N_UV, FC, s - 1, c + 1))
                    for g in range(2):
                        out = bank[2 * c + g][:, :]
                        cols = slice(c * P, (c + 1) * P)
                        for kc in range(DC):
                            y_hi, y_lo = yh[:, kc, b * S:(b + 1) * S], yl[:, kc, b * S:(b + 1) * S]
                            nc.tensor.matmul(out, sh[w][:, kc, g, cols], y_lo, start=kc == 0, stop=False)
                            nc.tensor.matmul(out, sh[w][:, kc, g, cols], y_hi, start=False, stop=False)
                            mm = nc.tensor.matmul(out, sl[w][:, kc, g, cols], y_hi, start=False, stop=kc == DC - 1)
                    mm.then_inc(uv_done, 1)

            def down(i, s):
                w = s // NBATCH
                pe.wait_ge(h_lo, of(i, N_UV, FC, s, FC))
                for n in range(4):
                    pe.wait_ge(added, of(i, N_OUT, 4, s - 1, n + 1))
                    out = bank[4 + n][:, :]
                    rows = slice(n * P, (n + 1) * P)
                    for c in range(FC):
                        h_h, h_l = hh[s % 2][:, c, rows], hl[s % 2][:, c, rows]
                        nc.tensor.matmul(out, h_h, ol[w][:, c, :], start=c == 0, stop=False)
                        nc.tensor.matmul(out, h_h, oh[w][:, c, :], start=False, stop=False)
                        mm = nc.tensor.matmul(out, h_l, oh[w][:, c, :], start=False, stop=c == FC - 1)
                    mm.then_inc(out_done, 1)

            def body(i, final):
                for s in range(STEPS):
                    if s % NBATCH == 0:
                        pe.wait_ge(w_lo, 4 * i + 2 * (s // NBATCH) + 2)
                    up(i, s)
                    if s >= 1:
                        down(i, s - 1)
                down(i, STEPS - 1)
            passes(pe, body)

        def fetched(i, s, final):
            return s % NBATCH == 1 and not (final and s // NBATCH == 1)

        @block.scalar
        def _(act):
            def split_hi(e, w):
                act.wait_ge(s_in, 16 * e + 16)
                nc.scalar.activation(sh[w][:, :, :, :], raw_s[:, :, :, :], ACT.Copy).then_inc(w_hi, 1)
                act.wait_ge(o_in, 16 * e + 16)
                nc.scalar.activation(oh[w][:, :, :], raw_o[:, :, :], ACT.Copy).then_inc(w_hi, 1)

            split_hi(0, 0)

            def body(i, final):
                for s in range(STEPS):
                    for c in range(FC):
                        act.wait_ge(uv_done, of(i, N_UV, FC, s, c + 1))
                        act.wait_ge(h_done, of(i, N_UV, FC, s - 1, c + 1))
                        nc.scalar.activation(silu[:, c], bank[2 * c + 1][:, :], ACT.Silu).then_inc(silu_done, 1)
                    act.wait_ge(out_done, of(i, N_OUT, 4, s - 2, 4))
                    for c in range(FC):
                        act.wait_ge(h_done, of(i, N_UV, FC, s, c + 1))
                        nc.scalar.activation(hh[s % 2][:, c], hf[s % 2][:, c], ACT.Copy).then_inc(h_hi, 1)
                    if fetched(i, s, final):
                        w = s // NBATCH
                        act.wait_ge(out_done, of(i, N_OUT, 4, 4 * w - 1, 4))
                        split_hi(2 * i + w + 1, 1 - w)
            passes(act, body)

        @block.vector
        def _(dve):
            def split_lo(e, w):
                dve.wait_ge(w_hi, 2 * e + 1)
                nc.vector.tensor_tensor(sl[w][:, :, :, :], raw_s[:, :, :, :], sh[w][:, :, :, :].bitcast(fp32),
                                        ALU.subtract).then_inc(w_lo, 1)
                dve.wait_ge(w_hi, 2 * e + 2)
                nc.vector.tensor_tensor(ol[w][:, :, :], raw_o[:, :, :], oh[w][:, :, :].bitcast(fp32),
                                        ALU.subtract).then_inc(w_lo, 1)

            def add(i, s):
                for n in range(4):
                    a = acc[:, (s % NBATCH) * 4 + n, :]
                    dve.wait_ge(out_done, of(i, N_OUT, 4, s, n + 1))
                    nc.vector.tensor_tensor(a, bank[4 + n][:, :], a, ALU.add).then_inc(added, 1)

            split_lo(0, 0)
            dve.wait_ge(x_in, 16)
            nc.vector.tensor_scalar(acc[:, :, :], acc[:, :, :], 2.0, None, ALU.mult).then_inc(x_doubled, 1)
            dve.wait_ge(x_doubled, 1)

            def body(i, final):
                for s in range(STEPS):
                    for c in range(FC):
                        dve.wait_ge(silu_done, of(i, N_UV, FC, s, c + 1))
                        nc.vector.tensor_tensor(hf[s % 2][:, c], bank[2 * c][:, :], silu[:, c], ALU.mult).then_inc(h_done, 1)
                    for c in range(FC):
                        dve.wait_ge(h_hi, of(i, N_UV, FC, s, c + 1))
                        nc.vector.tensor_tensor(hl[s % 2][:, c], hf[s % 2][:, c], hh[s % 2][:, c].bitcast(fp32),
                                                ALU.subtract).then_inc(h_lo, 1)
                    if fetched(i, s, final):
                        split_lo(2 * i + s // NBATCH + 1, 1 - s // NBATCH)
                    if s >= 1:
                        add(i, s - 1)
                add(i, STEPS - 1)
            passes(dve, body)


H, HD = 16, 32
HC = P // HD
KM, KD = 48, 16
KT = KM + KD
CK = 256 // P
SCALE = HD ** -0.5
EPS_HEAD = 1e-6
EPS_LN = 1e-5


def stage_context(nc, ins, kT, vrows, head_mean, biases, wqh, wql, woh, wol, bank):
    with ExitStack() as held:
        def sb(name, shape, dtype):
            return held.enter_context(nc.sbuf_tensor(name, shape, dtype))

        def sem(name):
            return held.enter_context(nc.semaphore(name))

        wq = sb("c_wq", [P, DC, D], fp32)
        wo = sb("c_wo", [P, DC, D], fp32)
        wk = sb("c_wk", [P, 2, CK, D], fp32)
        wv = sb("c_wv", [P, 2, CK, D], fp32)
        ctx = sb("c_ctx", [P, CK, NBATCH, KT], fp32)
        ctx2 = sb("c_ctx2", [P, 2, CK, NBATCH, 2, KT], fp32)
        bv = sb("c_bv", [1, 2, D], fp32)
        kinds = sb("c_kinds", [1, 2, 2, KT], fp32)
        gsum = sb("c_gsum", [P, 4, 8 * H], fp32)
        kc = sb("c_kc", [P, DC, NBATCH * KT], fp32)
        ksq = sb("c_ksq", [P, DC, NBATCH * KT], fp32)
        rstd = sb("c_rstd", [P, DC, NBATCH * KT], fp32)
        bias_c = sb("c_bias_c", [P, 3, DC], fp32)
        eps = sb("c_eps", [P, 1], fp32)
        w_in, b_in, q_in, o_in = sem("c_w_in"), sem("c_b_in"), sem("c_q_in"), sem("c_o_in")
        consts, zeroed, placed = sem("c_consts"), sem("c_zeroed"), sem("c_placed")
        summed, centred = sem("c_summed"), sem("c_centred")
        bias_mean, bias_done = sem("c_bias_mean"), sem("c_bias_done")
        k_proj, k_biased, k_sq, k_var = sem("c_k_proj"), sem("c_k_biased"), sem("c_k_sq"), sem("c_k_var")
        k_root, k_steps = sem("c_k_root"), sem("c_k_steps")
        v_proj, v_copied = sem("c_v_proj"), sem("c_v_copied")
        q_hi, q_lo = sem("c_q_hi"), sem("c_q_lo")
        block = held.enter_context(nc.Block())
        SPANS = [(0, KM), (KM, KT)]

        @block.sync
        def _(sp):
            for n, name in enumerate(("wk_main", "wk_last")):
                sp.dma_start(wk[:, n], ins[name].rearrange("(c p) n -> p c n", p=P)).then_inc(w_in, 16)
            sp.dma_start(ctx[:, :, :, :], ins["ctxT"].rearrange("(c p) b k -> p c b k", p=P)).then_inc(w_in, 16)
            for n, name in enumerate(("wv_main", "wv_last")):
                sp.dma_start(wv[:, n], ins[name].rearrange("(c p) n -> p c n", p=P)).then_inc(w_in, 16)
            sp.dma_start(wq[:, :, :], ins["wq"].rearrange("(c p) n -> p c n", p=P)).then_inc(q_in, 16)
            sp.dma_start(wo[:, :, :], ins["wo"].rearrange("(c p) n -> p c n", p=P)).then_inc(o_in, 16)

        @block.gpsimd
        def _(pool):
            nc.gpsimd.memset(head_mean[:, :], 0.0).then_inc(zeroed, 1)
            nc.gpsimd.memset(kinds[:, :, :, :], 0.0).then_inc(zeroed, 1)
            nc.gpsimd.memset(ctx2[:, :, :, :, :, :], 0.0).then_inc(zeroed, 1)
            nc.gpsimd.memset(eps[:, :], EPS_HEAD).then_inc(consts, 1)
            pool.wait_ge(zeroed, 3)
            for h in range(HC):
                rows = slice(h * HD, (h + 1) * HD)
                pool.wait_ge(consts, 1 + h)
                nc.gpsimd.memset(head_mean[rows, rows], 1.0 / HD).then_inc(consts, 1)
            for n, (a, z) in enumerate(SPANS):
                pool.wait_ge(consts, 1 + HC + n)
                nc.gpsimd.memset(kinds[:, n, :, a:z], 1.0).then_inc(consts, 1)
            pool.wait_ge(w_in, 80)
            pool.wait_ge(consts, 1 + HC + 2)
            for n, (a, z) in enumerate(SPANS):
                for half in range(2):
                    nc.gpsimd.tensor_copy(ctx2[:, n, :, :, half, a:z], ctx[:, :, :, a:z]).then_inc(placed, 1)

        @block.scalar
        def _(act):
            act.dma_start(biases[:, :, :], ins["biases"]).then_inc(b_in, 16)
            act.dma_start(bv[:, :, :], ins["bv"]).then_inc(b_in, 16)
            nc.scalar.preload_act_table_set("natural_log_exp_and_others")
            for c in range(DC):
                act.wait_ge(k_biased, 2 * c + 2)
                nc.scalar.activation(ksq[:, c], kc[:, c], ACT.Square).then_inc(k_sq, 1)
            for c in range(DC):
                act.wait_ge(k_var, c + 1)
                nc.scalar.activation(rstd[:, c], bank[4 + c % 2][:, 0:NBATCH * KT], ACT.Ln,
                                     bias=eps[:, 0:1]).then_inc(k_root, 1)
            act.wait_ge(k_root, DC)
            nc.scalar.activation(rstd[:, :, :], rstd[:, :, :], ACT.Exp, scale=-0.5).then_inc(k_root, 1)
            for b in range(NBATCH):
                act.wait_ge(v_proj, b + 1)
                nc.scalar.activation(vrows[:, b], bank[6 + b % 2][:, :], ACT.Copy).then_inc(v_copied, 1)
            act.wait_ge(centred, 3)
            nc.scalar.activation(wqh[:, :, :], wq[:, :, :], ACT.Copy).then_inc(q_hi, 1)
            act.wait_ge(o_in, 16)
            nc.scalar.activation(woh[:, :, :], wo[:, :, :], ACT.Copy).then_inc(q_hi, 1)

        @block.vector
        def _(dve):
            def centre(n, w, chunks):
                v = w.rearrange("p c (h d) -> p (c h) d", d=HD)
                g = gsum[:, n, 0:chunks * H]
                nc.vector.tensor_reduce(g, v, AX.X, ALU.add).then_inc(summed, 1)
                dve.wait_ge(summed, 2 * n + 1)
                nc.vector.tensor_scalar(g, g, 1.0 / HD, None, ALU.mult).then_inc(summed, 1)
                dve.wait_ge(summed, 2 * n + 2)
                nc.vector.tensor_tensor(v, v, g.unsqueeze(2).broadcast_to([P, chunks * H, HD]),
                                        ALU.subtract).then_inc(centred, 1)

            dve.wait_ge(w_in, 80)
            centre(0, wk[:, 0], CK)
            centre(1, wk[:, 1], CK)
            dve.wait_ge(bias_mean, 1)
            nc.vector.tensor_tensor(bias_c[:, :, :], biases[:, 0:3, :], bank[3][:, 0:3 * DC].rearrange(
                "p (n c) -> p n c", n=3), ALU.subtract).then_inc(bias_done, 1)
            dve.wait_ge(bias_done, 1)
            for c in range(DC):
                src = bank[c % 2][:, 0:NBATCH * KT].rearrange("p (b k) -> p b k", k=KT)
                dst = kc[:, c].rearrange("p (b k) -> p b k", k=KT)
                dve.wait_ge(k_proj, c + 1)
                for n, (a, z) in enumerate(SPANS):
                    nc.vector.tensor_scalar(dst[:, :, a:z], src[:, :, a:z], bias_c[:, 1 + n, c:c + 1], None,
                                            ALU.add).then_inc(k_biased, 1)
            nc.vector.tensor_copy(biases[:, 0, :], bias_c[:, 0, :]).then_inc(bias_done, 1)
            dve.wait_ge(k_root, DC + 1)
            dve.wait_ge(k_biased, 2 * DC)
            nc.vector.tensor_tensor(kc[:, :, :], kc[:, :, :], rstd[:, :, :], ALU.mult).then_inc(k_steps, 1)
            dve.wait_ge(k_steps, 1)
            src = kc[:, :, :].rearrange("p c (b k) -> p (c b) k", k=KT)
            dst = kT[:, :, :].rearrange("p c (b k) -> p (c b) k", k=KT)
            for n, (a, z) in enumerate(SPANS):
                nc.vector.tensor_scalar(dst[:, :, a:z], src[:, :, a:z], biases[:, 3 + n, 0:1],
                                        biases[:, 3 + n, 1:2], ALU.mult, ALU.add).then_inc(k_steps, 1)
            dve.wait_ge(k_steps, 3)
            nc.vector.tensor_scalar(kT[:, :, :], kT[:, :, :], SCALE, None, ALU.mult).then_inc(k_steps, 1)
            dve.wait_ge(q_in, 16)
            centre(2, wq[:, :, :], DC)
            for n, (hi, lo, w) in enumerate(((wqh, wql, wq), (woh, wol, wo))):
                dve.wait_ge(q_hi, n + 1)
                nc.vector.tensor_tensor(lo[:, :, :], w[:, :, :], hi[:, :, :].bitcast(fp32),
                                        ALU.subtract).then_inc(q_lo, 1)

        @block.tensor
        def _(pe):
            pe.wait_ge(consts, 1 + HC + 2)
            pe.wait_ge(b_in, 32)
            nc.tensor.matmul(bank[3][:, 0:3 * DC], head_mean[:, :], biases[:, 0:3, :].rearrange("p n c -> p (n c)"),
                             start=True, stop=True).then_inc(bias_mean, 1)
            pe.wait_ge(w_in, 80)
            for c in range(DC):
                out = bank[c % 2][:, 0:NBATCH * KT].rearrange("p (b k) -> p b k", k=KT)
                for n, (a, z) in enumerate(SPANS):
                    pe.wait_ge(centred, n + 1)
                    if c >= 2:
                        pe.wait_ge(k_biased, 2 * (c - 1))
                    for i in range(CK):
                        mm = nc.tensor.matmul(out[:, :, a:z], wk[:, n, i, c * P:(c + 1) * P], ctx[:, i, :, a:z],
                                              start=i == 0, stop=i == CK - 1)
                mm.then_inc(k_proj, 1)
            for c in range(DC):
                pe.wait_ge(k_sq, c + 1)
                if c >= 2:
                    pe.wait_ge(k_root, c - 1)
                nc.tensor.matmul(bank[4 + c % 2][:, 0:NBATCH * KT], head_mean[:, :], ksq[:, c],
                                 start=True, stop=True).then_inc(k_var, 1)
            pe.wait_ge(placed, 4)
            for b in range(NBATCH):
                if b >= 2:
                    pe.wait_ge(v_copied, b - 1)
                out = bank[6 + b % 2][:, :]
                for n in range(2):
                    nc.tensor.matmul(out, kinds[0:1, n].rearrange("o h k -> o (h k)"), bv[0:1, n],
                                     start=n == 0, stop=False)
                    for i in range(CK):
                        mm = nc.tensor.matmul(out, ctx2[:, n, i, b].rearrange("p h k -> p (h k)"), wv[:, n, i],
                                              start=False, stop=n == 1 and i == CK - 1)
                mm.then_inc(v_proj, 1)


def stage_cross(nc, ins, acc, logits, kT, vrows, head_mean, biases, identity, wqh, wql, woh, wol, bank):
    PAIRS = H // 2
    NT = S // P
    NE = 32
    SPANS = [(0, KM), (KM, KT)]

    def one(i):
        return bank[i // 2][:, i % 2, :]

    with ExitStack() as held:
        def sb(name, shape, dtype=fp32):
            return held.enter_context(nc.sbuf_tensor(name, shape, dtype))

        def sem(name):
            return held.enter_context(nc.semaphore("x_" + name))

        xb = sb("x_x", [P, NT, D])
        xth, xtl = sb("x_xth", [P, DC, S], fp32r), sb("x_xtl", [P, DC, S], fp32r)
        cth, ctl = xth, xtl
        qc = sb("x_qc", [P, DC, S])
        qsq = sb("x_qsq", [P, 2, S])
        rs = sb("x_rs", [P, 2, S])
        qh, ql = sb("x_qh", [P, DC, S], fp32r), sb("x_ql", [P, DC, S], fp32r)
        kh, kl = sb("x_kh", [P, DC, HC, KT], fp32r), sb("x_kl", [P, DC, HC, KT], fp32r)
        vh, vl = sb("x_vh", [P, PAIRS, P], fp32r), sb("x_vl", [P, PAIRS, P], fp32r)
        pf = sb("x_p", [P, 2, H, KT])
        pth, ptl = sb("x_pth", [P, PAIRS, S], fp32r), sb("x_ptl", [P, PAIRS, S], fp32r)
        mx, den = sb("x_mx", [P, 2, H, 2]), sb("x_den", [P, 2, H, 2])
        stats, moments = sb("x_stats", [P, NT, 6]), sb("x_moments", [P, NT, 2])
        rstd = sb("x_rstd", [P, NT])
        bo = sb("x_bo", [P, D])
        router = sb("x_router", [P, DC, NE])
        eps = sb("x_eps", [P, 2])
        io_in, consts, zeroed = sem("in"), sem("consts"), sem("zeroed")
        names = dict(stat=2 * NT, stat_seen=2, moment=2 * NT, root=4, x1=NT, t1=DC, x1_hi=DC, x1_lo=DC, k_hi=HC, k_lo=HC,
                     v_hi=4, v_lo=4, q=DC, q_b=DC, q_sq=DC, var=DC, q_root=2 * DC, q_n=DC, q_aff=DC, q_hi=DC,
                     q_lo=DC, sc=NT, mx=2 * NT, sub=2 * NT, ex=NT, sm=2 * NT, rc=NT, nm=2 * NT, pt=NT,
                     p_hi=NT, p_lo=NT, pv=DC, c_hi=DC, c_lo=DC, bo=NT, wo=NT, res=NT, x2=NT, kept=1,
                     t2=DC, xt=DC, lg=1, lg_out=1)
        s = {k: sem(k) for k in names}
        block = held.enter_context(nc.Block())

        def at(b, name, m):
            return this(b, names[name], m)

        def before(b, name):
            return last(b, names[name], names[name])

        HALVES = [(half, j) for half in range(2) for j in range(2)]

        def values_at(t, half, j):
            g = 2 * j + half
            return t[half * KT:(half + 1) * KT, j::2, g * HD:(g + 1) * HD]

        def values_of(b, half, j):
            v = vrows[half * KT:(half + 1) * KT, bass.ds(b, 1), :]
            return v.rearrange("p o (c g d) -> p (o c) g d", g=HC, d=HD)[:, :, 2 * j + half, :]

        def keys_of(b, h):
            return kT[h * HD:(h + 1) * HD, :, bass.ds(b * KT, KT)]

        @block.sync
        def _(sp):
            sp.dma_start(bo[:, :], ins["bo"].broadcast_to([P, D])).then_inc(io_in, 16)
            sp.dma_start(router[:, :, :], ins["routerT"].rearrange("(c p) e -> p c e", p=P)).then_inc(io_in, 16)

        @block.gpsimd
        def _(pool):
            nc.gpsimd.memset(eps[:, 0:1], EPS_LN).then_inc(consts, 1)
            nc.gpsimd.memset(eps[:, 1:2], EPS_HEAD).then_inc(consts, 1)
            for t in (kh, kl):
                nc.gpsimd.memset(t[:, :, :, :].bitcast(fp32), 0.0).then_inc(zeroed, 1)
            for t in (vh, vl):
                nc.gpsimd.memset(t[:, :, :].bitcast(fp32), 0.0).then_inc(zeroed, 1)
            for name, n in names.items():
                pool.sem_inc(s[name], n)
            pool.wait_ge(io_in, 32)
            with pool.Fori(0, NBATCH) as b:
                for n in range(NT):
                    pool.wait_ge(s["t1"], at(b, "t1", DC))
                    nc.gpsimd.tensor_tensor(xb[:, n], xb[:, n], bo[:, :], ALU.add).then_inc(s["bo"], 1)
                for c in range(DC):
                    pool.wait_ge(s["q_root"], at(b, "q_root", 2 * c + 2))
                    nc.gpsimd.tensor_tensor(qc[:, c], qc[:, c], rs[:, c % 2], ALU.mult).then_inc(s["q_n"], 1)

        @block.scalar
        def _(act):
            nc.scalar.preload_act_table_set("natural_log_exp_and_others")
            act.wait_ge(zeroed, 4)
            act.wait_ge(consts, 2)
            with act.Fori(0, NBATCH) as b:
                def roots(m):
                    act.wait_ge(s["moment"], at(b, "moment", m * NT))
                    nc.scalar.activation(rstd[:, :], moments[:, :, 1], ACT.Ln, bias=eps[:, 0:1]).then_inc(s["root"], 1)
                    act.wait_ge(s["root"], at(b, "root", 2 * m - 1))
                    nc.scalar.activation(rstd[:, :], rstd[:, :], ACT.Exp, scale=-0.5).then_inc(s["root"], 1)

                def q_root(c):
                    act.wait_ge(s["var"], at(b, "var", c + 1))
                    if c >= 2:
                        act.wait_ge(s["q_n"], at(b, "q_n", c - 1))
                    nc.scalar.activation(rs[:, c % 2], one(6 + c % 2), ACT.Ln, bias=eps[:, 1:2]).then_inc(s["q_root"], 1)
                    act.wait_ge(s["q_root"], at(b, "q_root", 2 * c + 1))
                    nc.scalar.activation(rs[:, c % 2], rs[:, c % 2], ACT.Exp, scale=-0.5).then_inc(s["q_root"], 1)

                roots(1)
                act.wait_ge(s["sc"], before(b, "sc"))
                act.wait_ge(s["pv"], before(b, "pv"))
                act.wait_ge(consts, 2)
                for h in range(HC):
                    nc.scalar.activation(kh[h * HD:(h + 1) * HD, :, h, :], keys_of(b, h), ACT.Copy).then_inc(s["k_hi"], 1)
                for half, j in HALVES:
                    nc.scalar.activation(values_at(vh, half, j), values_of(b, half, j), ACT.Copy).then_inc(s["v_hi"], 1)
                for c in range(DC):
                    act.wait_ge(s["t1"], at(b, "t1", c + 1))
                    nc.scalar.activation(xth[:, c], one(c), ACT.Copy).then_inc(s["x1_hi"], 1)
                act.wait_ge(s["lg"], before(b, "lg"))
                for c in range(DC):
                    act.wait_ge(s["q"], at(b, "q", c + 1))
                    nc.scalar.activation(qc[:, c], one(4 + c % 2), ACT.Identity, bias=biases[:, 0, c:c + 1]).then_inc(s["q_b"], 1)
                    nc.scalar.activation(qsq[:, c % 2], one(4 + c % 2), ACT.Square, bias=biases[:, 0, c:c + 1]).then_inc(s["q_sq"], 1)
                    if c >= 1:
                        q_root(c - 1)
                q_root(DC - 1)
                for c in range(DC):
                    act.wait_ge(s["q_aff"], at(b, "q_aff", c + 1))
                    nc.scalar.activation(qh[:, c], qc[:, c], ACT.Copy).then_inc(s["q_hi"], 1)

                def p_hi(n):
                    act.wait_ge(s["pt"], at(b, "pt", n + 1))
                    nc.scalar.activation(pth[:, :, n * P:(n + 1) * P], bank[2 + n % 2][:, :, :].rearrange(
                        "p a (j t) -> p (a j) t", t=P), ACT.Copy).then_inc(s["p_hi"], 1)
                for n in range(NT):
                    act.wait_ge(s["sub"], at(b, "sub", 2 * n + 2))
                    nc.scalar.activation(pf[:, n % 2], pf[:, n % 2], ACT.Exp).then_inc(s["ex"], 1)
                    if n >= 1:
                        p_hi(n - 1)
                p_hi(NT - 1)
                for c in range(DC):
                    act.wait_ge(s["pv"], at(b, "pv", c + 1))
                    nc.scalar.activation(cth[:, c], one(c), ACT.Copy).then_inc(s["c_hi"], 1)
                roots(2)
                act.wait_ge(s["x2"], at(b, "x2", NT))
                act.wait_ge(consts, 2)
                nc.scalar.activation(acc[:, bass.ds(b * NT, NT), :], xb[:, :, :], ACT.Copy).then_inc(s["kept"], 1)
                for c in range(DC):
                    act.wait_ge(s["t2"], at(b, "t2", c + 1))
                    nc.scalar.activation(qc[:, c], one(c), ACT.Copy).then_inc(s["xt"], 1)

        @block.vector
        def _(dve):
            dve.wait_ge(zeroed, 4)
            with dve.Fori(0, NBATCH) as b:
                def norm(src, dst, m):
                    for n in range(NT):
                        nc.vector.bn_stats(stats[:, n], src(n)).then_inc(s["stat"], 1)
                    dve.wait_ge(s["stat"], at(b, "stat", m * NT))
                    dve.sem_inc(s["stat_seen"], 1)
                    for n in range(NT):
                        dve.wait_ge(zeroed, 4)
                        nc.vector.bn_aggr(moments[:, n], stats[:, n]).then_inc(s["moment"], 1)
                    dve.wait_ge(s["root"], at(b, "root", 2 * m))
                    for n in range(NT):
                        nc.vector.tensor_scalar(dst(n), src(n), moments[:, n, 0:1], rstd[:, n:n + 1],
                                                ALU.subtract, ALU.mult).then_inc(s[("x1", "x2")[m - 1]], 1)

                def rows(n):
                    return acc[:, bass.ds(b * NT + n, 1), :].rearrange("p o d -> p (o d)")

                dve.wait_ge(s["kept"], before(b, "kept"))
                dve.wait_ge(s["t2"], before(b, "t2"))
                dve.wait_ge(zeroed, 4)
                norm(rows, lambda n: xb[:, n], 1)
                for h in range(HC):
                    dve.wait_ge(s["k_hi"], at(b, "k_hi", h + 1))
                    nc.vector.tensor_tensor(kl[h * HD:(h + 1) * HD, :, h, :], keys_of(b, h),
                                            kh[h * HD:(h + 1) * HD, :, h, :].bitcast(fp32), ALU.subtract).then_inc(s["k_lo"], 1)
                for n, (half, j) in enumerate(HALVES):
                    dve.wait_ge(s["v_hi"], at(b, "v_hi", n + 1))
                    nc.vector.tensor_tensor(values_at(vl, half, j), values_of(b, half, j),
                                            values_at(vh, half, j).bitcast(fp32), ALU.subtract).then_inc(s["v_lo"], 1)
                for c in range(DC):
                    dve.wait_ge(s["x1_hi"], at(b, "x1_hi", c + 1))
                    nc.vector.tensor_tensor(xtl[:, c], one(c), xth[:, c].bitcast(fp32), ALU.subtract).then_inc(s["x1_lo"], 1)
                for c in range(DC):
                    dve.wait_ge(s["q_n"], at(b, "q_n", c + 1))
                    nc.vector.tensor_scalar(qc[:, c], qc[:, c], biases[:, 5, 0:1], biases[:, 5, 1:2],
                                            ALU.mult, ALU.add).then_inc(s["q_aff"], 1)
                for c in range(DC):
                    dve.wait_ge(s["q_hi"], at(b, "q_hi", c + 1))
                    nc.vector.tensor_tensor(ql[:, c], qc[:, c], qh[:, c].bitcast(fp32), ALU.subtract).then_inc(s["q_lo"], 1)

                def scores(n):
                    return bank[n % 2][:, :, :].rearrange("p a (h k) -> p (a h) k", k=KT)

                def minus_max(n):
                    dve.wait_ge(s["sc"], at(b, "sc", n + 1))
                    for i, (a, z) in enumerate(SPANS):
                        nc.vector.tensor_reduce(mx[:, n % 2, :, i], scores(n)[:, :, a:z], AX.X, ALU.max).then_inc(s["mx"], 1)
                    for i, (a, z) in enumerate(SPANS):
                        dve.wait_ge(s["mx"], at(b, "mx", 2 * n + i + 1))
                        nc.vector.tensor_tensor(pf[:, n % 2, :, a:z], scores(n)[:, :, a:z],
                                                mx[:, n % 2, :, i:i + 1].broadcast_to([P, H, z - a]),
                                                ALU.subtract).then_inc(s["sub"], 1)

                def normalise(n):
                    dve.wait_ge(s["ex"], at(b, "ex", n + 1))
                    for i, (a, z) in enumerate(SPANS):
                        nc.vector.tensor_reduce(den[:, n % 2, :, i], pf[:, n % 2, :, a:z], AX.X, ALU.add).then_inc(s["sm"], 1)
                    dve.wait_ge(s["sm"], at(b, "sm", 2 * n + 2))
                    nc.vector.reciprocal(den[:, n % 2], den[:, n % 2]).then_inc(s["rc"], 1)
                    dve.wait_ge(s["rc"], at(b, "rc", n + 1))
                    for i, (a, z) in enumerate(SPANS):
                        nc.vector.tensor_tensor(pf[:, n % 2, :, a:z], pf[:, n % 2, :, a:z],
                                                den[:, n % 2, :, i:i + 1].broadcast_to([P, H, z - a]),
                                                ALU.mult).then_inc(s["nm"], 1)

                def p_lo(n):
                    dve.wait_ge(s["p_hi"], at(b, "p_hi", n + 1))
                    nc.vector.tensor_tensor(ptl[:, :, n * P:(n + 1) * P], bank[2 + n % 2][:, :, :].rearrange(
                        "p a (j t) -> p (a j) t", t=P), pth[:, :, n * P:(n + 1) * P].bitcast(fp32),
                        ALU.subtract).then_inc(s["p_lo"], 1)

                for n in range(NT + 1):
                    if n < NT:
                        if n >= 2:
                            dve.wait_ge(s["pt"], at(b, "pt", n - 1))
                        minus_max(n)
                    if n >= 1:
                        normalise(n - 1)
                    if n >= 2:
                        p_lo(n - 2)
                p_lo(NT - 1)
                for c in range(DC):
                    dve.wait_ge(s["c_hi"], at(b, "c_hi", c + 1))
                    nc.vector.tensor_tensor(ctl[:, c], one(c), cth[:, c].bitcast(fp32), ALU.subtract).then_inc(s["c_lo"], 1)
                for n in range(NT):
                    dve.wait_ge(s["bo"], at(b, "bo", NT))
                    dve.wait_ge(s["wo"], at(b, "wo", n + 1))
                    nc.vector.tensor_tensor(xb[:, n], one(4 + n), xb[:, n], ALU.add).then_inc(s["res"], 1)
                dve.wait_ge(s["res"], at(b, "res", NT))
                dve.wait_ge(zeroed, 4)
                norm(lambda n: xb[:, n], lambda n: xb[:, n], 2)
                dve.wait_ge(s["lg"], at(b, "lg", 1))
                nc.vector.tensor_copy(logits[:, bass.ds(b * NT, NT), :],
                                      one(4)[:, 0:NT * NE].rearrange("p (n e) -> p n e", e=NE)).then_inc(s["lg_out"], 1)

        @block.tensor
        def _(pe):
            def product(out, lh, ll, rh, rl, first, stop):
                nc.tensor.matmul(out, lh, rl, start=first, stop=False)
                nc.tensor.matmul(out, lh, rh, start=False, stop=False)
                return nc.tensor.matmul(out, ll, rh, start=False, stop=stop)

            pe.wait_ge(zeroed, 4)
            pe.wait_ge(consts, 2)
            with pe.Fori(0, NBATCH) as b:
                pe.wait_ge(s["x1"], at(b, "x1", NT))
                for c in range(DC):
                    for n in range(NT):
                        mm = nc.tensor.transpose(one(c)[:, n * P:(n + 1) * P], xb[:, n, c * P:(c + 1) * P], identity[:, :])
                    mm.then_inc(s["t1"], 1)

                def variance(c):
                    pe.wait_ge(s["q_sq"], at(b, "q_sq", c + 1))
                    if c >= 2:
                        pe.wait_ge(s["q_root"], at(b, "q_root", 2 * c - 3))
                    nc.tensor.matmul(one(6 + c % 2), head_mean[:, :], qsq[:, c % 2], start=True, stop=True).then_inc(s["var"], 1)

                pe.wait_ge(s["x1_lo"], at(b, "x1_lo", DC))
                for c in range(DC):
                    if c >= 2:
                        pe.wait_ge(s["q_sq"], at(b, "q_sq", c - 1))
                    for kc in range(DC):
                        cols = slice(c * P, (c + 1) * P)
                        mm = product(one(4 + c % 2), wqh[:, kc, cols], wql[:, kc, cols], xth[:, kc], xtl[:, kc],
                                     kc == 0, kc == DC - 1)
                    mm.then_inc(s["q"], 1)
                    if c >= 1:
                        variance(c - 1)
                variance(DC - 1)

                def turn(n):
                    pe.wait_ge(s["nm"], at(b, "nm", 2 * n + 2))
                    if n >= 2:
                        pe.wait_ge(s["p_lo"], at(b, "p_lo", n - 1))
                    for j in range(PAIRS):
                        mm = nc.tensor.transpose(bank[2 + n % 2][:, j // 4, (j % 4) * P:(j % 4 + 1) * P],
                                                 pf[:, n % 2, 2 * j:2 * j + 2, :].rearrange("p h k -> p (h k)"), identity[:, :])
                    mm.then_inc(s["pt"], 1)

                pe.wait_ge(s["k_lo"], at(b, "k_lo", HC))
                pe.wait_ge(s["q_lo"], at(b, "q_lo", DC))
                for n in range(NT):
                    if n >= 2:
                        pe.wait_ge(s["sub"], at(b, "sub", 2 * n - 2))
                    for c in range(DC):
                        toks = slice(n * P, (n + 1) * P)
                        out = bank[n % 2][:, c // 2, (c % 2) * HC * KT:(c % 2 + 1) * HC * KT]
                        keys = [k[:, c].rearrange("p h k -> p (h k)") for k in (kh, kl)]
                        mm = product(out, qh[:, c, toks], ql[:, c, toks], *keys, True, True)
                    mm.then_inc(s["sc"], 1)
                    if n >= 1:
                        turn(n - 1)
                turn(NT - 1)
                pe.wait_ge(s["v_lo"], at(b, "v_lo", 4))
                pe.wait_ge(s["p_lo"], at(b, "p_lo", NT))
                for c in range(DC):
                    for j in (2 * c, 2 * c + 1):
                        mm = product(one(c), vh[:, j], vl[:, j], pth[:, j], ptl[:, j], j == 2 * c, j == 2 * c + 1)
                    mm.then_inc(s["pv"], 1)
                pe.wait_ge(s["c_lo"], at(b, "c_lo", DC))
                for n in range(NT):
                    for c in range(DC):
                        toks = slice(n * P, (n + 1) * P)
                        mm = product(one(4 + n), cth[:, c, toks], ctl[:, c, toks], woh[:, c], wol[:, c],
                                     c == 0, c == DC - 1)
                    mm.then_inc(s["wo"], 1)
                pe.wait_ge(s["x2"], at(b, "x2", NT))
                for c in range(DC):
                    for n in range(NT):
                        mm = nc.tensor.transpose(one(c)[:, n * P:(n + 1) * P], xb[:, n, c * P:(c + 1) * P], identity[:, :])
                    mm.then_inc(s["t2"], 1)
                pe.wait_ge(s["xt"], at(b, "xt", DC))
                for n in range(NT):
                    for c in range(DC):
                        mm = nc.tensor.matmul(one(4)[:, n * NE:(n + 1) * NE], qc[:, c, n * P:(n + 1) * P], router[:, c],
                                              start=c == 0, stop=c == DC - 1)
                mm.then_inc(s["lg"], 1)


NE = 32
NT = T // P
NSLOT = NT + NE - 1

def stage_route(nc, acc, logits, pos, top, tile_expert, sorted_x, bank):
    with ExitStack() as held:
        def sb(name, shape, dtype=fp32):
            return held.enter_context(nc.sbuf_tensor("r_" + name, shape, dtype))

        def sem(name):
            return held.enter_context(nc.semaphore("r_" + name))

        mx, den, best = sb("mx", [P, NT]), sb("den", [P, NT]), sb("best", [P, NT])
        ex = sb("ex", [P, NT, NE])
        eq = sb("eq", [P, NT, NE])
        onehot = sb("onehot", [P, NT, NE])
        onehot_b = sb("onehot_b", [P, NT, NE], bf16)
        below = sb("below", [P, P], bf16)
        ones = sb("ones", [P, P], bf16)
        rev = sb("rev", [P, NE])
        marks = sb("marks", [P, NT])
        steps = sb("steps", [P, NSLOT])
        total, run_a, run_b = sb("total", [P, NT, NE]), sb("run_a", [P, NT, NE]), sb("run_b", [P, NT, NE])
        over = sb("over", [P, NE, NT])
        tiles, end, base = sb("tiles", [P, NE]), sb("end", [P, NE]), sb("base", [P, NE])
        done = sb("done", [P, NSLOT, NE])
        expert_f = sb("expert_f", [P, NSLOT])
        pos_f = sb("pos_f", [P, NT])
        consts, steps_done, exps, counted, placed = (sem("consts"), sem("steps"), sem("exps"), sem("counted"),
                                                     sem("placed"))
        ready, scattered = sem("ready"), sem("scattered")
        block = held.enter_context(nc.Block())
        N_CONST = 7

        @block.gpsimd
        def _(pool):
            nc.gpsimd.memset(ones[:, :], 1.0).then_inc(consts, 1)
            nc.gpsimd.memset(below[:, :], 1.0).then_inc(consts, 1)
            nc.gpsimd.iota(rev[:, :], pattern=[[-1, NE]], base=NE, channel_multiplier=0,
                           allow_small_or_imprecise_dtypes=True).then_inc(consts, 1)
            nc.gpsimd.iota(marks[:, :], pattern=[[P, NT]], base=0, channel_multiplier=0,
                           allow_small_or_imprecise_dtypes=True).then_inc(consts, 1)
            nc.gpsimd.iota(steps[:, :], pattern=[[1, NSLOT]], base=0, channel_multiplier=0,
                           allow_small_or_imprecise_dtypes=True).then_inc(consts, 1)
            pool.wait_ge(consts, 5)
            nc.gpsimd.affine_select(out=below[:, :], in_=below[:, :], compare_op=ALU.is_gt, fill=0.0, base=0,
                                    pattern=[[1, P]], channel_multiplier=-1).then_inc(consts, 2)
            pool.wait_ge(ready, 1)
            for n in range(NT):
                nc.gpsimd.indirect_dma_start(
                    out=sorted_x, out_offset=bass.IndirectOffsetOnAxis(ap=pos[:, n:n + 1], axis=0),
                    in_=acc[:, n, :], in_offset=None).then_inc(scattered, 16)
            pool.wait_ge(scattered, 16 * NT)

        @block.scalar
        def _(act):
            act.wait_ge(exps, 1)
            nc.scalar.activation(ex[:, :, :], ex[:, :, :], ACT.Exp).then_inc(exps, 1)

        @block.tensor
        def _(pe):
            pe.wait_ge(consts, N_CONST)
            pe.wait_ge(placed, 1)
            flat = onehot_b[:, :, :].rearrange("p n e -> p (n e)")
            nc.tensor.matmul(bank[0][:, :], below[:, :], flat, start=True, stop=True).then_inc(counted, 1)
            nc.tensor.matmul(bank[1][:, :], ones[:, :], flat, start=True, stop=True).then_inc(counted, 1)

        @block.vector
        def _(dve):
            count = [0]

            def step(ins):
                count[0] += 1
                ins.then_inc(steps_done, 1)
                dve.wait_ge(steps_done, count[0])

            def over_experts(t):
                return t[:, :].unsqueeze(2).broadcast_to([P, NT, NE])

            def over_tiles(t):
                return t[:, :].unsqueeze(1).broadcast_to([P, NT, NE])

            v = nc.vector
            step(v.tensor_reduce(mx[:, :], logits[:, :, :], AX.X, ALU.max))
            v.tensor_tensor(ex[:, :, :], logits[:, :, :], over_experts(mx), ALU.subtract).then_inc(exps, 1)
            dve.wait_ge(consts, N_CONST)
            step(v.tensor_tensor(eq[:, :, :], logits[:, :, :], over_experts(mx), ALU.is_equal))
            step(v.tensor_tensor(eq[:, :, :], eq[:, :, :], over_tiles(rev), ALU.mult))
            step(v.tensor_reduce(best[:, :], eq[:, :, :], AX.X, ALU.max))
            step(v.tensor_tensor(onehot[:, :, :], eq[:, :, :], over_experts(best), ALU.is_equal))
            v.tensor_copy(onehot_b[:, :, :], onehot[:, :, :]).then_inc(placed, 1)
            dve.wait_ge(exps, 2)
            step(v.tensor_reduce(den[:, :], ex[:, :, :], AX.X, ALU.add))
            step(v.reciprocal(top[:, :], den[:, :]))
            dve.wait_ge(counted, 2)
            step(v.tensor_copy(total[:, :, :], bank[1][:, :].rearrange("p (n e) -> p n e", e=NE)))
            src, dst = total, run_a
            k = 1
            while k < NT:
                v.tensor_copy(dst[:, 0:k], src[:, 0:k]).then_inc(steps_done, 1)
                count[0] += 1
                step(v.tensor_tensor(dst[:, k:NT], src[:, k:NT], src[:, 0:NT - k], ALU.add))
                src, dst = dst, (run_b if dst is run_a else run_a)
                k *= 2
            each = src[:, NT - 1, :].unsqueeze(2).broadcast_to([P, NE, NT])
            step(v.tensor_tensor(over[:, :, :], each, marks[:, :].unsqueeze(1).broadcast_to([P, NE, NT]), ALU.is_gt))
            step(v.tensor_reduce(tiles[:, :], over[:, :, :], AX.X, ALU.add))
            step(v.tensor_tensor_scan(end[:, :], tiles[:, :], tiles[:, :], 0.0, ALU.add, ALU.bypass))
            step(v.tensor_tensor(base[:, :], end[:, :], tiles[:, :], ALU.subtract))
            step(v.tensor_scalar(base[:, :], base[:, :], float(P), None, ALU.mult))
            step(v.tensor_tensor(src[:, :, :], src[:, :, :], total[:, :, :], ALU.subtract))
            step(v.tensor_tensor(src[:, :, :], src[:, :, :], over_tiles(base), ALU.add))
            step(v.tensor_tensor(src[:, :, :], bank[0][:, :].rearrange("p (n e) -> p n e", e=NE), src[:, :, :], ALU.add))
            step(v.tensor_tensor(src[:, :, :], src[:, :, :], onehot[:, :, :], ALU.mult))
            step(v.tensor_reduce(pos_f[:, :], src[:, :, :], AX.X, ALU.add))
            step(v.tensor_copy(pos[:, :], pos_f[:, :]))
            step(v.tensor_tensor(done[:, :, :], end[:, :].unsqueeze(1).broadcast_to([P, NSLOT, NE]),
                                 steps[:, :].unsqueeze(2).broadcast_to([P, NSLOT, NE]), ALU.is_le))
            step(v.tensor_reduce(expert_f[:, :], done[:, :, :], AX.X, ALU.add))
            step(v.tensor_scalar(expert_f[:, :], expert_f[:, :], float(NE - 1), None, ALU.min))
            v.tensor_copy(tile_expert[:, :], expert_f[0:1, :]).then_inc(ready, 1)

def stage_experts(nc, ins, tile_expert, identity, sorted_x, sorted_y, bank):
    maskT, w_ffnT = ins["maskT"], ins["w_ffnT"]

    with ExitStack() as held:
        def sb(name, shape, dtype=fp32):
            return held.enter_context(nc.sbuf_tensor("e_" + name, shape, dtype))

        def sem(name):
            return held.enter_context(nc.semaphore("e_" + name))

        ternary, low = sb("ternary", [P, DC, D]), sb("low", [P, DC, D])
        m = [sb(f"m{i}", [P, DC, D]) for i in range(2)]
        wh = [sb(f"wh{i}", [P, DC, D], fp32r) for i in range(2)]
        wl = [sb(f"wl{i}", [P, DC, D], fp32r) for i in range(2)]
        xs = [sb(f"xs{i}", [P, D]) for i in range(2)]
        xth = [sb(f"xth{i}", [P, D], fp32r) for i in range(2)]
        xtl = [sb(f"xtl{i}", [P, D], fp32r) for i in range(2)]
        ys = [sb(f"ys{i}", [P, D]) for i in range(2)]
        t_in, t_steps = sem("t_in"), sem("t_steps")
        m_in, x_in, y_out = ([sem(f"{k}{i}") for i in range(2)] for k in ("m_in", "x_in", "y_out"))
        names = dict(masked=1, w_hi=1, w_lo=1, w_lo2=1, turned=1, x_hi=1, x_lo=1, y=1, y_read=1)
        s = {k: sem(k) for k in names}
        block = held.enter_context(nc.Block())
        HALF = DC // 2

        def passes(eng, body):
            with eng.Fori(0, NSLOT // 2) as i:
                for par in range(2):
                    body(i * 2 + par, par)
            if NSLOT % 2:
                body(NSLOT - 1, (NSLOT - 1) % 2)

        def through(t):
            return t + 3

        def freed(t):
            return t + 1

        @block.sync
        def _(sp):
            sp.dma_start(m[0][:, :, :], w_ffnT.rearrange("(c p) n -> p c n", p=P)).then_inc(t_in, 16)
            sp.wait_ge(t_steps, 2)

            def body(t, par):
                e = sp.value_load(tile_expert[0:1, bass.ds(t, 1)], min_val=0, max_val=NE - 1)
                sp.wait_ge(s["w_lo"], freed(t))
                sp.wait_ge(s["w_lo2"], freed(t))
                sp.dma_start(m[par][:, :, :], maskT[bass.ds(e, 1)].rearrange("o (c p) n -> p (o c) n", p=P)
                             ).then_inc(m_in[par], 16)
                sp.wait_ge(s["turned"], freed(t))
                sp.dma_start(xs[par][:, :], sorted_x[bass.ds(t * P, P), :]).then_inc(x_in[par], 16)
            passes(sp, body)

        @block.gpsimd
        def _(pool):
            for k in names:
                pool.sem_inc(s[k], 2)

            def body(t, par):
                pool.wait_ge(s["w_hi"], through(t))
                nc.gpsimd.tensor_tensor(wl[par][:, HALF:DC], m[par][:, HALF:DC], wh[par][:, HALF:DC].bitcast(fp32),
                                        ALU.subtract).then_inc(s["w_lo2"], 1)
            passes(pool, body)

        @block.scalar
        def _(act):
            def body(t, par):
                act.wait_ge(s["masked"], through(t))
                act.wait_ge(s["y"], freed(t))
                nc.scalar.activation(wh[par][:, :, :], m[par][:, :, :], ACT.Copy).then_inc(s["w_hi"], 1)
                act.wait_ge(s["turned"], through(t))
                nc.scalar.activation(xth[par][:, :], bank[par][:, :], ACT.Copy).then_inc(s["x_hi"], 1)
                act.wait_ge(s["y"], through(t))
                act.wait_ge(y_out[par], 16 * (t // 2) + 16)
                nc.scalar.activation(ys[par][:, :], bank[2 + par][:, :], ACT.Copy).then_inc(s["y_read"], 1)
                act.wait_ge(s["y_read"], through(t))
                act.dma_start(sorted_y[bass.ds(t * P, P), :] if type(t) is not int else
                              sorted_y[t * P:(t + 1) * P, :], ys[par][:, :]).then_inc(y_out[par], 16)

            for o in y_out:
                act.sem_inc(o, 16)
            passes(act, body)
            for par in range(2):
                act.wait_ge(y_out[par], 16 * ((NSLOT + 1 - par) // 2 + 1))

        @block.vector
        def _(dve):
            dve.wait_ge(t_in, 16)
            nc.vector.tensor_scalar(low[:, :, :], m[0][:, :, :], -0.25, None, ALU.is_lt).then_inc(t_steps, 1)
            nc.vector.tensor_scalar(ternary[:, :, :], m[0][:, :, :], 0.25, None, ALU.is_gt).then_inc(t_steps, 1)
            dve.wait_ge(t_steps, 2)
            nc.vector.tensor_tensor(ternary[:, :, :], ternary[:, :, :], low[:, :, :], ALU.subtract).then_inc(t_steps, 1)
            dve.wait_ge(t_steps, 3)

            def body(t, par):
                dve.wait_ge(m_in[par], 16 * (t // 2) + 16)
                nc.vector.tensor_tensor(m[par][:, :, :], m[par][:, :, :], ternary[:, :, :], ALU.mult).then_inc(s["masked"], 1)
                dve.wait_ge(s["w_hi"], through(t))
                nc.vector.tensor_tensor(wl[par][:, 0:HALF], m[par][:, 0:HALF], wh[par][:, 0:HALF].bitcast(fp32),
                                        ALU.subtract).then_inc(s["w_lo"], 1)
                dve.wait_ge(s["x_hi"], through(t))
                nc.vector.tensor_tensor(xtl[par][:, :], bank[par][:, :], xth[par][:, :].bitcast(fp32),
                                        ALU.subtract).then_inc(s["x_lo"], 1)
            passes(dve, body)

        @block.tensor
        def _(pe):
            def body(t, par):
                pe.wait_ge(x_in[par], 16 * (t // 2) + 16)
                pe.wait_ge(s["x_lo"], freed(t))
                for c in range(DC):
                    mm = nc.tensor.transpose(bank[par][:, c * P:(c + 1) * P], xs[par][:, c * P:(c + 1) * P], identity[:, :])
                mm.then_inc(s["turned"], 1)
                pe.wait_ge(s["x_lo"], through(t))
                pe.wait_ge(s["w_lo"], through(t))
                pe.wait_ge(s["w_lo2"], through(t))
                pe.wait_ge(s["y_read"], freed(t))
                out = bank[2 + par][:, :]
                for c in range(DC):
                    cols = slice(c * P, (c + 1) * P)
                    nc.tensor.matmul(out, xth[par][:, cols], wl[par][:, c], start=c == 0, stop=False)
                    nc.tensor.matmul(out, xth[par][:, cols], wh[par][:, c], start=False, stop=False)
                    mm = nc.tensor.matmul(out, xtl[par][:, cols], wh[par][:, c], start=False, stop=c == DC - 1)
                mm.then_inc(s["y"], 1)
            passes(pe, body)

def stage_last(nc, ins, out, acc, pos, top, sorted_y):
    RING = 4

    with ExitStack() as held:
        def sb(name, shape, dtype=fp32):
            return held.enter_context(nc.sbuf_tensor("l_" + name, shape, dtype))

        def sem(name):
            return held.enter_context(nc.semaphore("l_" + name))

        y = [sb(f"y{i}", [P, D]) for i in range(RING)]
        scale = sb("scale", [P, D])
        stats, moments, rstd, eps = (sb("stats", [P, NT, 6]), sb("moments", [P, NT, 2]), sb("rstd", [P, NT]),
                                     sb("eps", [P, 1]))
        scale_in, eps_set = sem("scale_in"), sem("eps_set")
        y_in = [sem(f"y_in{i}") for i in range(RING)]
        scaled, summed, stat, moment, root, normed, out_done = (
            sem(k) for k in ("scaled", "summed", "stat", "moment", "root", "normed", "out_done"))
        block = held.enter_context(nc.Block())

        @block.gpsimd
        def _(pool):
            nc.gpsimd.memset(eps[:, :], EPS_LN).then_inc(eps_set, 1)

            def gather(n):
                if n >= RING:
                    pool.wait_ge(summed, n - RING + 1)
                nc.gpsimd.indirect_dma_start(
                    out=y[n % RING][:, :], out_offset=None, in_=sorted_y,
                    in_offset=bass.IndirectOffsetOnAxis(ap=pos[:, n:n + 1], axis=0)).then_inc(y_in[n % RING], 16)

            for n in range(RING - 1):
                gather(n)
            pool.wait_ge(scale_in, 16)
            for n in range(NT):
                if n + RING - 1 < NT:
                    gather(n + RING - 1)
                pool.wait_ge(y_in[n % RING], 16 * (n // RING + 1))
                nc.gpsimd.tensor_tensor(y[n % RING][:, :], y[n % RING][:, :], scale[:, :], ALU.mult).then_inc(scaled, 1)

        @block.vector
        def _(dve):
            def finish(n):
                dve.wait_ge(root, 2 * n + 2)
                nc.vector.tensor_scalar(acc[:, n], acc[:, n], moments[:, n, 0:1], rstd[:, n:n + 1],
                                        ALU.subtract, ALU.mult).then_inc(normed, 1)
            for n in range(NT):
                dve.wait_ge(scaled, n + 1)
                nc.vector.scalar_tensor_tensor(acc[:, n], y[n % RING][:, :], top[:, n:n + 1], acc[:, n],
                                               ALU.mult, ALU.add).then_inc(summed, 1)
                dve.wait_ge(summed, n + 1)
                nc.vector.bn_stats(stats[:, n], acc[:, n]).then_inc(stat, 1)
                dve.wait_ge(stat, n + 1)
                nc.vector.bn_aggr(moments[:, n], stats[:, n]).then_inc(moment, 1)
                if n >= 1:
                    finish(n - 1)
            finish(NT - 1)

        @block.scalar
        def _(act):
            act.wait_ge(eps_set, 1)
            for n in range(NT):
                act.wait_ge(moment, n + 1)
                nc.scalar.activation(rstd[:, n:n + 1], moments[:, n, 1:2], ACT.Ln, bias=eps[:, 0:1]).then_inc(root, 1)
                act.wait_ge(root, 2 * n + 1)
                nc.scalar.activation(rstd[:, n:n + 1], rstd[:, n:n + 1], ACT.Exp, scale=-0.5).then_inc(root, 1)

        @block.sync
        def _(sp):
            sp.dma_start(scale[:, :], ins["scale"].broadcast_to([P, D])).then_inc(scale_in, 16)
            for n in range(NT):
                sp.wait_ge(normed, n + 1)
                sp.dma_start(out[n * P:(n + 1) * P, :], acc[:, n]).then_inc(out_done, 16)
            sp.wait_ge(out_done, 16 * NT)

def stage_constants(nc, identity, zeros, sorted_x, zero_filled):
    with nc.semaphore("k_ones") as ones, nc.semaphore("k_zeroed") as zeroed, nc.Block() as block:
        @block.gpsimd
        def _(pool):
            nc.gpsimd.memset(identity[:, :], 1.0).then_inc(ones, 1)
            pool.wait_ge(ones, 1)
            nc.gpsimd.affine_select(out=identity[:, :], in_=identity[:, :], compare_op=ALU.is_equal, fill=0.0,
                                    base=0, pattern=[[1, P]], channel_multiplier=-1).then_inc(ones, 1)
            pool.wait_ge(ones, 2)

        @block.vector
        def _(dve):
            nc.vector.memset(zeros[:, :], 0.0).then_inc(zeroed, 1)

        @block.sync
        def _(sp):
            sp.wait_ge(zeroed, 1)
            sp.dma_start(sorted_x.rearrange("(n p) d -> p n d", p=P),
                         zeros[:, :].unsqueeze(1).broadcast_to([P, NSLOT, D])).then_inc(zero_filled, 16)



def build(nc, out, ins):
    with ExitStack() as held:
        def sb(name, shape, dtype=fp32):
            return held.enter_context(nc.sbuf_tensor(name, shape, dtype))

        pairs = [held.enter_context(nc.psum_tensor(f"bank{i}", [P, 2, 512], fp32)) for i in range(4)]
        bank = [pairs[i // 2][:, i % 2, :] for i in range(8)]
        acc = sb("acc", [P, NT, D])
        identity = sb("identity", [P, P])
        logits = sb("logits", [P, NT, NE])
        pos, top = sb("pos", [P, NT], u32), sb("top", [P, NT])
        tile_expert = sb("tile_expert", [1, NSLOT], i32)
        sorted_x = nc.dram_tensor("sorted_x", [NSLOT * P, D], fp32, kind="Internal").ap()
        sorted_y = nc.dram_tensor("sorted_y", [NSLOT * P, D], fp32, kind="Internal").ap()
        zero_filled = held.enter_context(nc.semaphore("zero_filled"))

        with ExitStack() as part:
            xyh = part.enter_context(nc.sbuf_tensor("xyh", [P, DC, T], fp32r))
            xyl = part.enter_context(nc.sbuf_tensor("xyl", [P, DC, T], fp32r))
            stage_qkv(nc, ins, xyh, xyl, acc, bank)
            zeros = part.enter_context(nc.sbuf_tensor("zeros", [P, D], fp32))
            stage_constants(nc, identity, zeros, sorted_x, zero_filled)
            stage_swiglu(nc, ins, xyh, xyl, acc, zero_filled, bank)
        with ExitStack() as part:
            def of_part(name, shape, dtype=fp32):
                return part.enter_context(nc.sbuf_tensor(name, shape, dtype))

            kT, vrows = of_part("kT", [P, DC, NBATCH * KT]), of_part("vrows", [P, NBATCH, D])
            head_mean, biases = of_part("head_mean", [P, P]), of_part("biases", [P, 6, DC])
            weights = [of_part(name, [P, DC, D], fp32r) for name in ("wqh", "wql", "woh", "wol")]
            stage_context(nc, ins, kT, vrows, head_mean, biases, *weights, bank)
            stage_cross(nc, ins, acc, logits, kT, vrows, head_mean, biases, identity, *weights, pairs)
        stage_route(nc, acc, logits, pos, top, tile_expert, sorted_x, bank)
        stage_experts(nc, ins, tile_expert, identity, sorted_x, sorted_y, bank)
        stage_last(nc, ins, out, acc, pos, top, sorted_y)


def layouts(given):
    g = {name: np.asarray(a) for name, a in given.items()}

    def keys_values(w):
        w = w.reshape(w.shape[0], H, 2, HD)
        return w[:, :, 0].reshape(-1, D), w[:, :, 1].reshape(-1, D)

    def column(b):
        return b.reshape(DC, P).T

    parts = 8
    inner = g["L0_attn_w_out"].shape[1]
    wk_main, wv_main = keys_values(np.concatenate([g["L0_xattn_Wk"], g["L0_xattn_Wv"]], 1))
    bk_main, bv_main = keys_values(np.concatenate([g["L0_xattn_bk"], g["L0_xattn_bv"]])[None])
    w_last, b_last = g["L0_xattn_Wkv_dca"], g["L0_xattn_bkv_dca"]
    biases = np.zeros((P, 6, DC), np.float32)
    biases[:, 0], biases[:, 1], biases[:, 2] = column(g["L0_xattn_bq"]), column(bk_main[0]), column(b_last[:D])
    for n, name in enumerate(("kn", "kn_dca", "qn")):
        biases[:, 3 + n, 0] = np.tile(g[f"L0_xattn_{name}_w"], HC)
        biases[:, 3 + n, 1] = np.tile(g[f"L0_xattn_{name}_b"], HC)
    ins = dict(
        x=g["x"].reshape(T, D), xT=g["x"].transpose(0, 2, 1),
        wqkvT=g["L0_attn_w_qkv"].reshape(3, D, D).transpose(0, 2, 1),
        wsT=g["L0_attn_w_swiglu"].reshape(2, parts, inner // parts, DC, P).transpose(1, 4, 3, 0, 2),
        woT=g["L0_attn_w_out"].reshape(D, parts, inner // parts // P, P).transpose(1, 3, 2, 0),
        wk_main=wk_main, wv_main=wv_main, wk_last=w_last[:, :D], wv_last=w_last[:, D:],
        ctxT=g["ctx_1024"].transpose(2, 0, 1), biases=biases, bv=np.stack([bv_main[0], b_last[D:]])[None],
        wq=g["L0_xattn_Wq"], wo=g["L0_xattn_Wo"], bo=g["L0_xattn_bo"][None],
        w_ffnT=g["L0_ffn_weight"].T, scale=g["L0_ffn_scale"][None],
        maskT=g["L0_ffn_expert_masks"].transpose(0, 2, 1), routerT=g["L0_ffn_router_w"].T)
    return {name: np.ascontiguousarray(a) for name, a in ins.items()}


def kernel(**inputs):
    import concourse.bacc as bacc
    from concourse.bass_utils import run_bass_kernel_spmd

    nc = bacc.Bacc("TRN2", target_bir_lowering=False, num_devices=1)
    arrays = layouts(inputs)
    ins = {name: nc.dram_tensor(f"in_{name}_dram", a.shape, mybir.dt.from_np(a.dtype), kind="ExternalInput").ap()
           for name, a in arrays.items()}
    out = nc.dram_tensor("out_0_dram", (T, D), fp32, kind="ExternalOutput").ap()
    build(nc, out, ins)
    r = run_bass_kernel_spmd(nc, [{f"in_{name}_dram": a for name, a in arrays.items()}], core_ids=[0])
    return r.results[0]["out_0_dram"].reshape(NBATCH, S, D)
```

```python
import numpy as np
import concourse.bass as bass
from concourse import mybir
from contextlib import ExitStack

fp32 = mybir.dt.float32
fp32r = mybir.dt.float32r
bf16 = mybir.dt.bfloat16
i32 = mybir.dt.int32
u32 = mybir.dt.uint32
ALU = mybir.AluOpType
ACT = mybir.ActivationFunctionType
AX = mybir.AxisListType

P = 128
NBATCH = 4
S = 512
T = NBATCH * S
D = 512
DC = D // P
EPS_RMS = 1.1920929e-07
EPS_CUM = 1e-6


def this(i, n, m):
    return n * (i + 1) + m


def last(i, n, m):
    return n * i + m


def swiglu_weights(w, n):
    return w[:, n].rearrange("p c (u f) -> p c u f", u=2), w[:, 2, 2 * n:2 * n + 2]


def stage_qkv(nc, ins, xyh, xyl, wh, wl, acc, bank):
    xT, wqkvT = ins["xT"], ins["wqkvT"]
    LOADS = [("x", 0), ("x", 1), ("x", 2), ("w", 1), ("x", 3), ("w", 0), ("w", 2)]
    RING = 6
    K, Q, V = 0, 1, 2
    W_OF = {K: 1, Q: 0, V: 2}
    N_PROJ, N_KQ, N_ADD, N_C, N_ROOT = 3 * DC, 2 * DC, 6, 6, 4
    DOWN = 20
    HALF = 2 * DC

    with ExitStack() as held:
        def sb(name, shape, dtype):
            return held.enter_context(nc.sbuf_tensor(name, shape, dtype))

        sems = []

        def sem(name):
            sems.append(nc.alloc_semaphore(name))
            return sems[-1]

        sq = acc[:, 2 * DC:4 * DC, :]
        raw_s, raw_o = acc[:, HALF:HALF + DC, :], acc[:, HALF + DC:HALF + DC + 2, :]
        qbuf = sb("a_q", [P, 2 * DC, S], fp32)
        kbuf = sb("a_k", [P, 2 * DC, S], fp32)
        vbuf = sb("a_v", [P, DC, S], fp32)
        sqsum = sb("a_sqsum", [P, 2, S], fp32)
        rx = sb("a_r", [P, NBATCH, S], fp32)
        ckq = sb("a_ckq", [P, 2, S], fp32)
        mean_w = sb("a_mean", [P, P], fp32)
        eps = sb("a_eps", [P, 2], fp32)
        raw = [buf[:, n * DC:(n + 1) * DC, :] for buf, n in
               ((acc, 0), (acc, 1), (kbuf, 0), (kbuf, 1), (qbuf, 0), (qbuf, 1), (acc, 3))]
        raw_in = [sem(f"a_raw{l}_in") for l in range(len(LOADS))]
        consts = sem("a_consts")
        hi_made = sem("a_hi_made")
        lo_made = sem("a_lo_made")
        xsq_made = sem("a_xsq_made")
        xsq_add = sem("a_xsq_add")
        x_ms = sem("a_x_ms")
        x_root = sem("a_x_root")
        proj = sem("a_proj")
        kq_read = sem("a_kq_read")
        sq_add = sem("a_sq_add")
        ms_made = sem("a_ms_made")
        c_scaled = sem("a_c_scaled")
        c_root = sem("a_c_root")
        normed = sem("a_normed")
        exped = sem("a_exped")
        v_scaled, v_weighed, v_summed = sem("a_v_scaled"), sem("a_v_weighed"), sem("a_v_summed")
        w_summed = sem("a_w_summed")
        divisor, log, inverse = sem("a_divisor"), sem("a_log"), sem("a_inverse")
        terms, y_made, y_hi, y_lo = sem("a_terms"), sem("a_y_made"), sem("a_y_hi"), sem("a_y_lo")
        next_in, next_hi, next_lo = sem("a_next_in"), sem("a_next_hi"), sem("a_next_lo")
        x_rows_in = sem("a_x_rows_in")
        block = held.enter_context(nc.Block())
        looped = [(proj, N_PROJ), (kq_read, N_KQ), (sq_add, N_ADD), (ms_made, 2),
                  (c_scaled, N_C), (c_root, N_ROOT), (normed, N_KQ), (exped, N_KQ), (v_scaled, DC),
                  (v_weighed, DC), (v_summed, DC), (w_summed, DC), (divisor, DC), (log, DC),
                  (inverse, DC), (terms, 2 * DC), (y_made, DC), (y_hi, DC), (y_lo, DC)]

        def end(n):
            return this(NBATCH - 1, n, n)


        def split_target(l):
            kind, n = LOADS[l]
            if kind == "w":
                return wh[:, n], wl[:, n]
            return xyh[:, :, n * S:(n + 1) * S], xyl[:, :, n * S:(n + 1) * S]

        def half(buf, par, c):
            return buf[:, par * DC + c, :]

        def tokens(buf, b, c):
            return buf[:, c, bass.ds(b * S, S)]

        @block.sync
        def _(sp):
            for l, (kind, n) in enumerate(LOADS):
                src = wqkvT[n] if kind == "w" else xT[n]
                sp.dma_start(raw[l], src.rearrange("(c p) t -> p c t", p=P)).then_inc(raw_in[l], 16)
            sp.wait_ge(lo_made, len(LOADS))
            sp.wait_ge(xsq_made, NBATCH)
            sp.dma_start(acc[:, 0:HALF, :], ins["x"][0:HALF * P, :].rearrange("(n p) d -> p n d", p=P)
                         ).then_inc(x_rows_in, 16)
            sp.wait_ge(sq_add, end(N_ADD))
            sp.dma_start(raw_s.rearrange("p c (u f) -> p c u f", u=2), ins["wsT"][0]).then_inc(next_in, 16)
            sp.dma_start(raw_o, ins["woT"][0]).then_inc(next_in, 16)

        @block.tensor
        def _(pe):
            def mean_square(out, src):
                return nc.tensor.matmul(out[:, :], mean_w[:, :], src, start=True, stop=True)

            pe.wait_ge(consts, 3)
            for n in range(NBATCH):
                pe.wait_ge(xsq_add, 2 * n + 2)
                if n >= 2:
                    pe.wait_ge(x_root, 2 * (n - 2) + 1)
                mean_square(bank[6 + n % 2], sqsum[:, n % 2]).then_inc(x_ms, 1)
            pe.wait_ge(x_root, 2 * NBATCH)
            with pe.Fori(0, NBATCH // 2) as pair:
                for par in range(2):
                    b = pair * 2 + par
                    for j in range(N_PROJ):
                        which, c = j // DC, j % DC
                        if j < 2:
                            pe.wait_ge(kq_read, last(b, N_KQ, 7 + j))
                        elif j < RING:
                            pe.wait_ge(v_scaled, last(b, DC, j - 1))
                        else:
                            pe.wait_ge(kq_read, this(b, N_KQ, j - RING + 1))
                        if j % DC == 0:
                            pe.wait_ge(lo_made, LOADS.index(("w", W_OF[which])) + 1)
                            pe.wait_ge(lo_made, LOADS.index(("x", NBATCH - 1)) + 1)
                        out = bank[j % RING][:, :]
                        w, cols = W_OF[which], slice(c * P, (c + 1) * P)
                        for kc in range(DC):
                            xh, xl = tokens(xyh, b, kc), tokens(xyl, b, kc)
                            nc.tensor.matmul(out, wh[:, w, kc, cols], xl, start=kc == 0, stop=False)
                            nc.tensor.matmul(out, wh[:, w, kc, cols], xh, start=False, stop=False)
                            mm = nc.tensor.matmul(out, wl[:, w, kc, cols], xh, start=False, stop=kc == DC - 1)
                        mm.then_inc(proj, 1)
                        if j == DC + 2 or j == 2 * DC + 2:
                            w = j // DC - 1
                            pe.wait_ge(sq_add, this(b, N_ADD, 3 * w + 3))
                            pe.wait_ge(c_scaled, last(b, N_C, 3 * w + 1))
                            mean_square(bank[6 + w], sqsum[:, w]).then_inc(ms_made, 1)

        @block.scalar
        def _(act):
            def root(dst, src, sem, value):
                nc.scalar.activation(dst, src, ACT.Ln, bias=eps[:, 0:1]).then_inc(sem, 1)
                act.wait_ge(sem, value)
                nc.scalar.activation(dst, dst, ACT.Exp, scale=-0.5).then_inc(sem, 1)

            nc.scalar.preload_act_table_set("natural_log_exp_and_others")
            act.wait_ge(consts, 3)
            xs = 0
            for l, (kind, n) in enumerate(LOADS):
                act.wait_ge(raw_in[l], 16)
                hi, _ = split_target(l)
                nc.scalar.activation(hi, raw[l], ACT.Copy).then_inc(hi_made, 1)
                if kind == "x":
                    if xs:
                        act.wait_ge(xsq_add, 2 * xs)
                    nc.scalar.activation(sq[:, 0:DC, :], raw[l], ACT.Square).then_inc(xsq_made, 1)
                    xs += 1
            for n in range(NBATCH):
                act.wait_ge(x_ms, n + 1)
                root(rx[:, n], bank[6 + n % 2][:, :], x_root, 2 * n + 1)
            act.wait_ge(xsq_add, 2 * NBATCH)
            act.wait_ge(lo_made, len(LOADS))

            def log_of(b, par, c):
                act.wait_ge(divisor, this(b, DC, c + 1))
                nc.scalar.activation(half(qbuf, par, c), half(kbuf, par, c), ACT.Ln, scale=2.0 ** -DOWN).then_inc(log, 1)

            def inverse_of(b, par, c):
                act.wait_ge(log, this(b, DC, c + 1))
                nc.scalar.activation(half(qbuf, par, c), half(qbuf, par, c), ACT.Exp, scale=-1.0,
                                     bias=eps[:, 1:2]).then_inc(inverse, 1)

            def gate_step(b, par, n):
                if n < DC:
                    log_of(b, par, n)
                if 1 <= n <= DC:
                    inverse_of(b, par, n - 1)

            def batch(b, par, before):
                for j in range(2 * DC):
                    buf, c = (kbuf, qbuf)[j // DC], j % DC
                    act.wait_ge(proj, this(b, N_PROJ, j + 1))
                    if j == 0:
                        act.wait_ge(sq_add, last(b, N_ADD, 6))
                        act.wait_ge(v_scaled, last(b, DC, 1))
                    nc.scalar.activation(half(buf, par, c), bank[j % RING][:, :], ACT.Copy)
                    nc.scalar.activation(sq[:, j], bank[j % RING][:, :], ACT.Square).then_inc(kq_read, 1)
                    if before is not None:
                        gate_step(*before, j)
                for w, buf in enumerate((kbuf, qbuf)):
                    act.wait_ge(c_scaled, this(b, N_C, 3 * w + 2))
                    root(ckq[:, w], ckq[:, w], c_root, this(b, N_ROOT, 2 * w + 1))
                    for c in range(DC):
                        act.wait_ge(normed, this(b, N_KQ, DC * w + c + 1))
                        nc.scalar.activation(half(buf, par, c), half(buf, par, c), ACT.Exp,
                                             scale=(1.0, -1.0)[w]).then_inc(exped, 1)

            with act.Fori(0, NBATCH // 2) as pair:
                batch(pair * 2, 0, None)
                batch(pair * 2 + 1, 1, (pair * 2, 0))
                for n in range(DC + 1):
                    gate_step(pair * 2 + 1, 1, n)
            act.wait_ge(proj, end(N_PROJ))
            act.wait_ge(next_in, 32)
            nc.scalar.activation(swiglu_weights(wh, 0)[0], raw_s.rearrange("p c (u f) -> p c u f", u=2),
                                 ACT.Copy).then_inc(next_hi, 1)
            nc.scalar.activation(swiglu_weights(wh, 0)[1], raw_o, ACT.Copy).then_inc(next_hi, 1)

        @block.gpsimd
        def _(pool):
            nc.gpsimd.memset(mean_w[:, :], 1.0 / D).then_inc(consts, 1)
            nc.gpsimd.memset(eps[:, 0:1], EPS_RMS).then_inc(consts, 1)
            nc.gpsimd.memset(eps[:, 1:2], -DOWN * float(np.log(2.0))).then_inc(consts, 1)
            for sem, n in looped:
                pool.sem_inc(sem, n)
            for n in range(NBATCH):
                pool.wait_ge(xsq_made, n + 1)
                if n >= 2:
                    pool.wait_ge(x_ms, n - 1)
                nc.gpsimd.tensor_tensor(sq[:, 0:2], sq[:, 0:2], sq[:, 2:4], ALU.add).then_inc(xsq_add, 1)
                pool.wait_ge(xsq_add, 2 * n + 1)
                nc.gpsimd.tensor_tensor(sqsum[:, n % 2], sq[:, 0], sq[:, 1], ALU.add).then_inc(xsq_add, 1)
            pool.wait_ge(x_ms, NBATCH)
            with pool.Fori(0, NBATCH // 2) as pair:
                for par in range(2):
                    b = pair * 2 + par
                    for w, buf in enumerate((kbuf, qbuf)):
                        for c in range(1, DC):
                            pool.wait_ge(kq_read, this(b, N_KQ, DC * w + c + 1))
                            if c == 1:
                                pool.wait_ge(ms_made, last(b, 2, w + 1))
                            else:
                                pool.wait_ge(sq_add, this(b, N_ADD, 3 * w + c - 1))
                            nc.gpsimd.tensor_tensor(sqsum[:, w], sq[:, DC * w] if c == 1 else sqsum[:, w],
                                                    sq[:, DC * w + c], ALU.add).then_inc(sq_add, 1)
                    for w, buf in enumerate((kbuf, qbuf)):
                        pool.wait_ge(c_scaled, this(b, N_C, 3 * w + 3))
                        for c in range(DC):
                            nc.gpsimd.tensor_tensor(half(buf, par, c), half(buf, par, c), ckq[:, w],
                                                    ALU.mult).then_inc(normed, 1)
            pool.wait_ge(next_hi, 2)
            for n, raw_w in enumerate((raw_s.rearrange("p c (u f) -> p c u f", u=2), raw_o)):
                nc.gpsimd.tensor_tensor(swiglu_weights(wl, 0)[n], raw_w, swiglu_weights(wh, 0)[n].bitcast(fp32),
                                        ALU.subtract).then_inc(next_lo, 1)
            pool.wait_ge(x_rows_in, 16)

        @block.vector
        def _(dve):
            for l in range(len(LOADS)):
                dve.wait_ge(hi_made, l + 1)
                hi, lo = split_target(l)
                nc.vector.tensor_tensor(lo, raw[l], hi.bitcast(fp32), ALU.subtract).then_inc(lo_made, 1)
            dve.wait_ge(x_root, 2 * NBATCH)
            with dve.Fori(0, NBATCH // 2) as pair:
                for par in range(2):
                    b = pair * 2 + par
                    r = rx[:, bass.ds(b, 1), :].rearrange("p o t -> p (o t)")

                    def mean_of_normed(w):
                        dve.wait_ge(ms_made, this(b, 2, w + 1))
                        dve.wait_ge(normed, last(b, N_KQ, DC * w + DC))
                        nc.vector.tensor_tensor(ckq[:, w], bank[6 + w][:, :], r, ALU.mult).then_inc(c_scaled, 1)
                        dve.wait_ge(c_scaled, this(b, N_C, 3 * w + 1))
                        nc.vector.tensor_tensor(ckq[:, w], ckq[:, w], r, ALU.mult).then_inc(c_scaled, 1)

                    def factor(w):
                        dve.wait_ge(c_root, this(b, N_ROOT, 2 * w + 2))
                        nc.vector.tensor_tensor(ckq[:, w], ckq[:, w], r, ALU.mult).then_inc(c_scaled, 1)

                    def sums(c):
                        expk, v = half(kbuf, par, c), vbuf[:, c]
                        dve.wait_ge(proj, this(b, N_PROJ, 2 * DC + c + 1))
                        dve.wait_ge(y_lo, last(b, DC, c + 1))
                        nc.vector.tensor_tensor(v, bank[(2 * DC + c) % RING][:, :], r, ALU.mult).then_inc(v_scaled, 1)
                        dve.wait_ge(exped, this(b, N_KQ, c + 1))
                        dve.wait_ge(v_scaled, this(b, DC, c + 1))
                        nc.vector.tensor_tensor(v, v, expk, ALU.mult).then_inc(v_weighed, 1)
                        dve.wait_ge(v_weighed, this(b, DC, c + 1))
                        nc.vector.tensor_tensor_scan(expk, expk, expk, EPS_CUM, ALU.add, ALU.bypass).then_inc(w_summed, 1)
                        nc.vector.tensor_tensor_scan(v, v, v, 0.0, ALU.add, ALU.bypass).then_inc(v_summed, 1)

                    def divide_by(c):
                        expk = half(kbuf, par, c)
                        dve.wait_ge(exped, this(b, N_KQ, DC + c + 1))
                        dve.wait_ge(w_summed, this(b, DC, c + 1))
                        nc.vector.scalar_tensor_tensor(expk, half(qbuf, par, c), 1.0, expk, ALU.add, ALU.mult
                                                       ).then_inc(divisor, 1)

                    def gate(c):
                        v, d, i = vbuf[:, c], half(kbuf, par, c), half(qbuf, par, c)
                        dve.wait_ge(inverse, this(b, DC, c + 1))
                        dve.wait_ge(v_summed, this(b, DC, c + 1))
                        nc.vector.scalar_tensor_tensor(d, d, -1.0, i, ALU.mult, ALU.mult).then_inc(terms, 1)
                        nc.vector.tensor_tensor(v, v, i, ALU.mult).then_inc(terms, 1)
                        dve.wait_ge(proj, this(b, N_PROJ, N_PROJ))
                        dve.wait_ge(terms, this(b, 2 * DC, 2 * c + 2))
                        nc.vector.scalar_tensor_tensor(v, d, 2.0, v, ALU.add, ALU.mult).then_inc(y_made, 1)
                        dve.wait_ge(y_made, this(b, DC, c + 1))
                        nc.vector.tensor_copy(tokens(xyh, b, c), v).then_inc(y_hi, 1)
                        dve.wait_ge(y_hi, this(b, DC, c + 1))
                        nc.vector.tensor_tensor(tokens(xyl, b, c), v, tokens(xyh, b, c).bitcast(fp32),
                                                ALU.subtract).then_inc(y_lo, 1)

                    mean_of_normed(0)
                    factor(0)
                    sums(0)
                    mean_of_normed(1)
                    sums(1)
                    factor(1)
                    sums(2)
                    divide_by(0)
                    sums(3)
                    for c in range(1, DC):
                        divide_by(c)
                        if c >= 2:
                            gate(c - 2)
                    gate(DC - 2)
                    gate(DC - 1)
    return sems


def stage_swiglu(nc, ins, yh, yl, wh, wl, acc, identity, zeros, sorted_x, used_sems, bank):
    x, wsT, woT = ins["x"], ins["wsT"], ins["woT"]
    NE = 8
    FE = 2048 // NE
    FC = FE // P
    STEPS = 2 * NBATCH
    N_UV, N_OUT = FC * STEPS, 4 * STEPS

    with ExitStack() as held:
        def sb(name, shape, dtype):
            return held.enter_context(nc.sbuf_tensor(name, shape, dtype))

        def sem(name):
            return held.enter_context(nc.semaphore(name))

        raw_s = sb("f_raw_s", [P, DC, 2, FE], fp32)
        raw_o = sb("f_raw_o", [P, FC, D], fp32)
        sh, oh = zip(*(swiglu_weights(wh, i) for i in range(2)))
        sl, ol = zip(*(swiglu_weights(wl, i) for i in range(2)))
        silu = sb("f_silu", [P, FC, S], fp32)
        hf = [sb(f"f_h{i}", [P, FC, S], fp32) for i in range(2)]
        hh = [sb(f"f_hh{i}", [P, FC, S], fp32r) for i in range(2)]
        hl = [sb(f"f_hl{i}", [P, FC, S], fp32r) for i in range(2)]
        x_in, s_in, o_in = sem("f_x_in"), sem("f_s_in"), sem("f_o_in")
        x_doubled, zeroed, zero_filled = sem("f_x_doubled"), sem("f_zeroed"), sem("f_zero_filled")
        w_hi, w_lo = sem("f_w_hi"), sem("f_w_lo")
        uv_done, silu_done, h_done = sem("f_uv_done"), sem("f_silu_done"), sem("f_h_done")
        h_hi, h_lo = sem("f_h_hi"), sem("f_h_lo")
        out_done, added = sem("f_out_done"), sem("f_added")
        credit = [(uv_done, N_UV), (silu_done, N_UV), (h_done, N_UV), (h_hi, N_UV), (h_lo, N_UV),
                  (out_done, N_OUT), (added, N_OUT)]
        first = [(s_in, 16), (o_in, 16), (w_hi, 2), (w_lo, 2)]
        HALF = T // P // 2
        nc.clear_and_free_semaphores(used_sems)
        block = held.enter_context(nc.Block())

        def of(i, n, per, s, m):
            return this(i, n, per * s + m) if s >= 0 else last(i, n, per * (s + STEPS) + m)

        def passes(eng, body):
            with eng.Fori(0, NE // 2 - 1) as i:
                body(i, False)
            body(NE // 2 - 1, True)

        @block.sync
        def _(sp):
            def load(e, free):
                sp.wait_ge(w_lo, free)
                sp.dma_start(raw_s[:, :, :, :], wsT[e] if type(e) is int else
                             wsT[bass.ds(e, 1)].rearrange("o p c u f -> p (o c) u f")).then_inc(s_in, 16)
                sp.dma_start(raw_o[:, :, :], woT[e] if type(e) is int else
                             woT[bass.ds(e, 1)].rearrange("o p c f -> p (o c) f")).then_inc(o_in, 16)

            sp.dma_start(acc[:, HALF:, :], x[HALF * P:, :].rearrange("(n p) d -> p n d", p=P)).then_inc(x_in, 16)

            def body(i, final):
                for half in range(1 if final else 2):
                    load(2 * i + half + 1, 2 * (2 * i + half + 1))
            passes(sp, body)
            sp.wait_ge(zeroed, 1)
            sp.dma_start(sorted_x.rearrange("(n p) d -> p n d", p=P),
                         zeros[:, :].unsqueeze(1).broadcast_to([P, sorted_x.shape[0] // P, D])).then_inc(zero_filled, 16)
            sp.wait_ge(zero_filled, 16)

        @block.gpsimd
        def _(pool):
            for s, n in credit + first:
                pool.sem_inc(s, n)
            nc.gpsimd.memset(zeros[:, :], 0.0).then_inc(zeroed, 1)
            nc.gpsimd.memset(identity[:, :], 1.0).then_inc(zeroed, 1)
            pool.wait_ge(zeroed, 2)
            nc.gpsimd.affine_select(out=identity[:, :], in_=identity[:, :], compare_op=ALU.is_equal, fill=0.0,
                                    base=0, pattern=[[1, P]], channel_multiplier=-1).then_inc(zeroed, 1)
            for n in range(NBATCH):
                if n == NBATCH // 2:
                    pool.wait_ge(x_in, 16)
                rows = acc[:, 4 * n:4 * n + 4, :]
                nc.gpsimd.tensor_scalar(rows, rows, 2.0, None, ALU.mult).then_inc(x_doubled, 1)

        @block.tensor
        def _(pe):
            def up(i, s):
                w, b = s // NBATCH, s % NBATCH
                for c in range(FC):
                    pe.wait_ge(h_done, of(i, N_UV, FC, s - 1, c + 1))
                    for g in range(2):
                        out = bank[2 * c + g][:, :]
                        cols = slice(c * P, (c + 1) * P)
                        for kc in range(DC):
                            y_hi, y_lo = yh[:, kc, b * S:(b + 1) * S], yl[:, kc, b * S:(b + 1) * S]
                            nc.tensor.matmul(out, sh[w][:, kc, g, cols], y_lo, start=kc == 0, stop=False)
                            nc.tensor.matmul(out, sh[w][:, kc, g, cols], y_hi, start=False, stop=False)
                            mm = nc.tensor.matmul(out, sl[w][:, kc, g, cols], y_hi, start=False, stop=kc == DC - 1)
                    mm.then_inc(uv_done, 1)

            def down(i, s):
                w = s // NBATCH
                pe.wait_ge(h_lo, of(i, N_UV, FC, s, FC))
                for n in range(4):
                    pe.wait_ge(added, of(i, N_OUT, 4, s - 1, n + 1))
                    out = bank[4 + n][:, :]
                    rows = slice(n * P, (n + 1) * P)
                    for c in range(FC):
                        h_h, h_l = hh[s % 2][:, c, rows], hl[s % 2][:, c, rows]
                        nc.tensor.matmul(out, h_h, ol[w][:, c, :], start=c == 0, stop=False)
                        nc.tensor.matmul(out, h_h, oh[w][:, c, :], start=False, stop=False)
                        mm = nc.tensor.matmul(out, h_l, oh[w][:, c, :], start=False, stop=c == FC - 1)
                    mm.then_inc(out_done, 1)

            def body(i, final):
                for s in range(STEPS):
                    if s % NBATCH == 0:
                        pe.wait_ge(w_lo, 4 * i + 2 * (s // NBATCH) + 2)
                    up(i, s)
                    if s >= 1:
                        down(i, s - 1)
                down(i, STEPS - 1)
            passes(pe, body)

        def fetched(i, s, final):
            return s % NBATCH == 1 and not (final and s // NBATCH == 1)

        @block.scalar
        def _(act):
            def split_hi(e, w):
                act.wait_ge(s_in, 16 * e + 16)
                nc.scalar.activation(sh[w], raw_s[:, :, :, :], ACT.Copy).then_inc(w_hi, 1)
                act.wait_ge(o_in, 16 * e + 16)
                nc.scalar.activation(oh[w], raw_o[:, :, :], ACT.Copy).then_inc(w_hi, 1)

            def body(i, final):
                for s in range(STEPS):
                    for c in range(FC):
                        act.wait_ge(uv_done, of(i, N_UV, FC, s, c + 1))
                        act.wait_ge(h_done, of(i, N_UV, FC, s - 1, c + 1))
                        nc.scalar.activation(silu[:, c], bank[2 * c + 1][:, :], ACT.Silu).then_inc(silu_done, 1)
                    act.wait_ge(out_done, of(i, N_OUT, 4, s - 2, 4))
                    for c in range(FC):
                        act.wait_ge(h_done, of(i, N_UV, FC, s, c + 1))
                        nc.scalar.activation(hh[s % 2][:, c], hf[s % 2][:, c], ACT.Copy).then_inc(h_hi, 1)
                    if fetched(i, s, final):
                        w = s // NBATCH
                        act.wait_ge(out_done, of(i, N_OUT, 4, 4 * w - 1, 4))
                        split_hi(2 * i + w + 1, 1 - w)
            passes(act, body)

        @block.vector
        def _(dve):
            def split_lo(e, w):
                dve.wait_ge(w_hi, 2 * e + 1)
                nc.vector.tensor_tensor(sl[w], raw_s[:, :, :, :], sh[w].bitcast(fp32),
                                        ALU.subtract).then_inc(w_lo, 1)
                dve.wait_ge(w_hi, 2 * e + 2)
                nc.vector.tensor_tensor(ol[w], raw_o[:, :, :], oh[w].bitcast(fp32),
                                        ALU.subtract).then_inc(w_lo, 1)

            def add(i, s):
                dve.wait_ge(x_doubled, min(s + 1, NBATCH))
                for n in range(4):
                    a = acc[:, (s % NBATCH) * 4 + n, :]
                    dve.wait_ge(out_done, of(i, N_OUT, 4, s, n + 1))
                    nc.vector.tensor_tensor(a, bank[4 + n][:, :], a, ALU.add).then_inc(added, 1)

            def body(i, final):
                for s in range(STEPS):
                    for c in range(FC):
                        dve.wait_ge(silu_done, of(i, N_UV, FC, s, c + 1))
                        nc.vector.tensor_tensor(hf[s % 2][:, c], bank[2 * c][:, :], silu[:, c], ALU.mult).then_inc(h_done, 1)
                    for c in range(FC):
                        dve.wait_ge(h_hi, of(i, N_UV, FC, s, c + 1))
                        nc.vector.tensor_tensor(hl[s % 2][:, c], hf[s % 2][:, c], hh[s % 2][:, c].bitcast(fp32),
                                                ALU.subtract).then_inc(h_lo, 1)
                    if fetched(i, s, final):
                        split_lo(2 * i + s // NBATCH + 1, 1 - s // NBATCH)
                    if s >= 1:
                        add(i, s - 1)
                add(i, STEPS - 1)
            passes(dve, body)


H, HD = 16, 32
HC = P // HD
KM, KD = 48, 16
KT = KM + KD
CK = 256 // P
SCALE = HD ** -0.5
EPS_HEAD = 1e-6
EPS_LN = 1e-5


def stage_context(nc, ins, kT, vrows, head_mean, biases, wqh, wql, woh, wol, bank):
    with ExitStack() as held:
        def sb(name, shape, dtype):
            return held.enter_context(nc.sbuf_tensor(name, shape, dtype))

        def sem(name):
            return held.enter_context(nc.semaphore(name))

        wq = sb("c_wq", [P, DC, D], fp32)
        wo = sb("c_wo", [P, DC, D], fp32)
        wk = sb("c_wk", [P, 2, CK, D], fp32)
        wv = sb("c_wv", [P, 2, CK, D], fp32)
        ctx = sb("c_ctx", [P, CK, NBATCH, KT], fp32)
        ctx2 = sb("c_ctx2", [P, 2, CK, NBATCH, 2, KT], fp32)
        bv = sb("c_bv", [1, 2, D], fp32)
        kinds = sb("c_kinds", [1, 2, 2, KT], fp32)
        gsum = sb("c_gsum", [P, 4, 8 * H], fp32)
        kc = sb("c_kc", [P, DC, NBATCH * KT], fp32)
        ksq = sb("c_ksq", [P, DC, NBATCH * KT], fp32)
        rstd = sb("c_rstd", [P, DC, NBATCH * KT], fp32)
        bias_c = sb("c_bias_c", [P, 3, DC], fp32)
        eps = sb("c_eps", [P, 1], fp32)
        w_in, b_in, q_in, o_in = sem("c_w_in"), sem("c_b_in"), sem("c_q_in"), sem("c_o_in")
        consts, zeroed, placed = sem("c_consts"), sem("c_zeroed"), sem("c_placed")
        summed, centred = sem("c_summed"), sem("c_centred")
        bias_mean, bias_done = sem("c_bias_mean"), sem("c_bias_done")
        k_proj, k_biased, k_sq, k_var = sem("c_k_proj"), sem("c_k_biased"), sem("c_k_sq"), sem("c_k_var")
        k_root, k_steps = sem("c_k_root"), sem("c_k_steps")
        v_proj, v_copied = sem("c_v_proj"), sem("c_v_copied")
        q_hi, q_lo = sem("c_q_hi"), sem("c_q_lo")
        block = held.enter_context(nc.Block())
        SPANS = [(0, KM), (KM, KT)]

        @block.sync
        def _(sp):
            for n, name in enumerate(("wk_main", "wk_last")):
                sp.dma_start(wk[:, n], ins[name].rearrange("(c p) n -> p c n", p=P)).then_inc(w_in, 16)
            sp.dma_start(ctx[:, :, :, :], ins["ctxT"].rearrange("(c p) b k -> p c b k", p=P)).then_inc(w_in, 16)
            for n, name in enumerate(("wv_main", "wv_last")):
                sp.dma_start(wv[:, n], ins[name].rearrange("(c p) n -> p c n", p=P)).then_inc(w_in, 16)
            sp.dma_start(wq[:, :, :], ins["wq"].rearrange("(c p) n -> p c n", p=P)).then_inc(q_in, 16)
            sp.dma_start(wo[:, :, :], ins["wo"].rearrange("(c p) n -> p c n", p=P)).then_inc(o_in, 16)

        @block.gpsimd
        def _(pool):
            nc.gpsimd.memset(head_mean[:, :], 0.0).then_inc(zeroed, 1)
            nc.gpsimd.memset(kinds[:, :, :, :], 0.0).then_inc(zeroed, 1)
            nc.gpsimd.memset(ctx2[:, :, :, :, :, :], 0.0).then_inc(zeroed, 1)
            nc.gpsimd.memset(eps[:, :], EPS_HEAD).then_inc(consts, 1)
            pool.wait_ge(zeroed, 3)
            for h in range(HC):
                rows = slice(h * HD, (h + 1) * HD)
                pool.wait_ge(consts, 1 + h)
                nc.gpsimd.memset(head_mean[rows, rows], 1.0 / HD).then_inc(consts, 1)
            for n, (a, z) in enumerate(SPANS):
                pool.wait_ge(consts, 1 + HC + n)
                nc.gpsimd.memset(kinds[:, n, :, a:z], 1.0).then_inc(consts, 1)
            pool.wait_ge(w_in, 80)
            pool.wait_ge(consts, 1 + HC + 2)
            for n, (a, z) in enumerate(SPANS):
                for half in range(2):
                    nc.gpsimd.tensor_copy(ctx2[:, n, :, :, half, a:z], ctx[:, :, :, a:z]).then_inc(placed, 1)

        @block.scalar
        def _(act):
            act.dma_start(biases[:, :, :], ins["biases"]).then_inc(b_in, 16)
            act.dma_start(bv[:, :, :], ins["bv"]).then_inc(b_in, 16)
            nc.scalar.preload_act_table_set("natural_log_exp_and_others")
            for c in range(DC):
                act.wait_ge(k_biased, 2 * c + 2)
                nc.scalar.activation(ksq[:, c], kc[:, c], ACT.Square).then_inc(k_sq, 1)
            for c in range(DC):
                act.wait_ge(k_var, c + 1)
                nc.scalar.activation(rstd[:, c], bank[4 + c % 2][:, 0:NBATCH * KT], ACT.Ln,
                                     bias=eps[:, 0:1]).then_inc(k_root, 1)
            act.wait_ge(k_root, DC)
            nc.scalar.activation(rstd[:, :, :], rstd[:, :, :], ACT.Exp, scale=-0.5).then_inc(k_root, 1)
            for b in range(NBATCH):
                act.wait_ge(v_proj, b + 1)
                nc.scalar.activation(vrows[:, b], bank[6 + b % 2][:, :], ACT.Copy).then_inc(v_copied, 1)
            act.wait_ge(centred, 3)
            nc.scalar.activation(wqh[:, :, :], wq[:, :, :], ACT.Copy).then_inc(q_hi, 1)
            act.wait_ge(o_in, 16)
            nc.scalar.activation(woh[:, :, :], wo[:, :, :], ACT.Copy).then_inc(q_hi, 1)

        @block.vector
        def _(dve):
            def centre(n, w, chunks):
                v = w.rearrange("p c (h d) -> p (c h) d", d=HD)
                g = gsum[:, n, 0:chunks * H]
                nc.vector.tensor_reduce(g, v, AX.X, ALU.add).then_inc(summed, 1)
                dve.wait_ge(summed, 2 * n + 1)
                nc.vector.tensor_scalar(g, g, 1.0 / HD, None, ALU.mult).then_inc(summed, 1)
                dve.wait_ge(summed, 2 * n + 2)
                nc.vector.tensor_tensor(v, v, g.unsqueeze(2).broadcast_to([P, chunks * H, HD]),
                                        ALU.subtract).then_inc(centred, 1)

            dve.wait_ge(w_in, 80)
            centre(0, wk[:, 0], CK)
            centre(1, wk[:, 1], CK)
            dve.wait_ge(bias_mean, 1)
            nc.vector.tensor_tensor(bias_c[:, :, :], biases[:, 0:3, :], bank[3][:, 0:3 * DC].rearrange(
                "p (n c) -> p n c", n=3), ALU.subtract).then_inc(bias_done, 1)
            dve.wait_ge(bias_done, 1)
            for c in range(DC):
                src = bank[c % 2][:, 0:NBATCH * KT].rearrange("p (b k) -> p b k", k=KT)
                dst = kc[:, c].rearrange("p (b k) -> p b k", k=KT)
                dve.wait_ge(k_proj, c + 1)
                for n, (a, z) in enumerate(SPANS):
                    nc.vector.tensor_scalar(dst[:, :, a:z], src[:, :, a:z], bias_c[:, 1 + n, c:c + 1], None,
                                            ALU.add).then_inc(k_biased, 1)
            nc.vector.tensor_copy(biases[:, 0, :], bias_c[:, 0, :]).then_inc(bias_done, 1)
            dve.wait_ge(k_root, DC + 1)
            dve.wait_ge(k_biased, 2 * DC)
            nc.vector.tensor_tensor(kc[:, :, :], kc[:, :, :], rstd[:, :, :], ALU.mult).then_inc(k_steps, 1)
            dve.wait_ge(k_steps, 1)
            src = kc[:, :, :].rearrange("p c (b k) -> p (c b) k", k=KT)
            dst = kT[:, :, :].rearrange("p c (b k) -> p (c b) k", k=KT)
            for n, (a, z) in enumerate(SPANS):
                nc.vector.tensor_scalar(dst[:, :, a:z], src[:, :, a:z], biases[:, 3 + n, 0:1],
                                        biases[:, 3 + n, 1:2], ALU.mult, ALU.add).then_inc(k_steps, 1)
            dve.wait_ge(k_steps, 3)
            nc.vector.tensor_scalar(kT[:, :, :], kT[:, :, :], SCALE, None, ALU.mult).then_inc(k_steps, 1)
            dve.wait_ge(q_in, 16)
            centre(2, wq[:, :, :], DC)
            for n, (hi, lo, w) in enumerate(((wqh, wql, wq), (woh, wol, wo))):
                dve.wait_ge(q_hi, n + 1)
                nc.vector.tensor_tensor(lo[:, :, :], w[:, :, :], hi[:, :, :].bitcast(fp32),
                                        ALU.subtract).then_inc(q_lo, 1)

        @block.tensor
        def _(pe):
            pe.wait_ge(consts, 1 + HC + 2)
            pe.wait_ge(b_in, 32)
            nc.tensor.matmul(bank[3][:, 0:3 * DC], head_mean[:, :], biases[:, 0:3, :].rearrange("p n c -> p (n c)"),
                             start=True, stop=True).then_inc(bias_mean, 1)
            pe.wait_ge(w_in, 80)
            for c in range(DC):
                out = bank[c % 2][:, 0:NBATCH * KT].rearrange("p (b k) -> p b k", k=KT)
                for n, (a, z) in enumerate(SPANS):
                    pe.wait_ge(centred, n + 1)
                    if c >= 2:
                        pe.wait_ge(k_biased, 2 * (c - 1))
                    for i in range(CK):
                        mm = nc.tensor.matmul(out[:, :, a:z], wk[:, n, i, c * P:(c + 1) * P], ctx[:, i, :, a:z],
                                              start=i == 0, stop=i == CK - 1)
                mm.then_inc(k_proj, 1)
            for c in range(DC):
                pe.wait_ge(k_sq, c + 1)
                if c >= 2:
                    pe.wait_ge(k_root, c - 1)
                nc.tensor.matmul(bank[4 + c % 2][:, 0:NBATCH * KT], head_mean[:, :], ksq[:, c],
                                 start=True, stop=True).then_inc(k_var, 1)
            pe.wait_ge(placed, 4)
            for b in range(NBATCH):
                if b >= 2:
                    pe.wait_ge(v_copied, b - 1)
                out = bank[6 + b % 2][:, :]
                for n in range(2):
                    nc.tensor.matmul(out, kinds[0:1, n].rearrange("o h k -> o (h k)"), bv[0:1, n],
                                     start=n == 0, stop=False)
                    for i in range(CK):
                        mm = nc.tensor.matmul(out, ctx2[:, n, i, b].rearrange("p h k -> p (h k)"), wv[:, n, i],
                                              start=False, stop=n == 1 and i == CK - 1)
                mm.then_inc(v_proj, 1)


def stage_cross(nc, ins, acc, logits, kT, vrows, head_mean, biases, identity, wqh, wql, woh, wol, bank):
    PAIRS = H // 2
    NT = S // P
    NE = 32
    SPANS = [(0, KM), (KM, KT)]

    def one(i):
        return bank[i // 2][:, i % 2, :]

    with ExitStack() as held:
        def sb(name, shape, dtype=fp32):
            return held.enter_context(nc.sbuf_tensor(name, shape, dtype))

        def sem(name):
            return held.enter_context(nc.semaphore("x_" + name))

        xb = sb("x_x", [P, NT, D])
        xth, xtl = sb("x_xth", [P, DC, S], fp32r), sb("x_xtl", [P, DC, S], fp32r)
        cth, ctl = xth, xtl
        qc = sb("x_qc", [P, DC, S])
        qsq = sb("x_qsq", [P, 2, S])
        rs = sb("x_rs", [P, 2, S])
        qh, ql = sb("x_qh", [P, DC, S], fp32r), sb("x_ql", [P, DC, S], fp32r)
        kh, kl = sb("x_kh", [P, DC, HC, KT], fp32r), sb("x_kl", [P, DC, HC, KT], fp32r)
        vh, vl = sb("x_vh", [P, PAIRS, P], fp32r), sb("x_vl", [P, PAIRS, P], fp32r)
        pf = sb("x_p", [P, 2, H, KT])
        pth, ptl = sb("x_pth", [P, PAIRS, S], fp32r), sb("x_ptl", [P, PAIRS, S], fp32r)
        mx, den = sb("x_mx", [P, 2, H, 2]), sb("x_den", [P, 2, H, 2])
        stats, moments = sb("x_stats", [P, NT, 6]), sb("x_moments", [P, NT, 2])
        rstd = sb("x_rstd", [P, NT])
        bo = sb("x_bo", [P, D])
        router = sb("x_router", [P, DC, NE])
        eps = sb("x_eps", [P, 2])
        io_in, consts, zeroed = sem("in"), sem("consts"), sem("zeroed")
        names = dict(stat=2 * NT, stat_seen=2, moment=2 * NT, root=4, x1=NT, t1=DC, x1_hi=DC, x1_lo=DC, k_hi=HC, k_lo=HC,
                     v_hi=4, v_lo=4, q=DC, q_b=DC, q_sq=DC, var=DC, q_root=2 * DC, q_n=DC, q_aff=DC, q_hi=DC,
                     q_lo=DC, sc=NT, mx=2 * NT, sub=2 * NT, ex=NT, sm=2 * NT, rc=NT, nm=2 * NT, pt=NT,
                     p_hi=NT, p_lo=NT, pv=DC, c_hi=DC, c_lo=DC, bo=NT, wo=NT, res=NT, x2=NT, kept=1,
                     t2=DC, xt=DC, lg=1, lg_out=1)
        s = {k: sem(k) for k in names}
        block = held.enter_context(nc.Block())

        def at(b, name, m):
            return this(b, names[name], m)

        def before(b, name):
            return last(b, names[name], names[name])

        HALVES = [(half, j) for half in range(2) for j in range(2)]

        def values_at(t, half, j):
            g = 2 * j + half
            return t[half * KT:(half + 1) * KT, j::2, g * HD:(g + 1) * HD]

        def values_of(b, half, j):
            v = vrows[half * KT:(half + 1) * KT, bass.ds(b, 1), :]
            return v.rearrange("p o (c g d) -> p (o c) g d", g=HC, d=HD)[:, :, 2 * j + half, :]

        def keys_of(b, h):
            return kT[h * HD:(h + 1) * HD, :, bass.ds(b * KT, KT)]

        @block.sync
        def _(sp):
            sp.dma_start(bo[:, :], ins["bo"].broadcast_to([P, D])).then_inc(io_in, 16)
            sp.dma_start(router[:, :, :], ins["routerT"].rearrange("(c p) e -> p c e", p=P)).then_inc(io_in, 16)

        @block.gpsimd
        def _(pool):
            nc.gpsimd.memset(eps[:, 0:1], EPS_LN).then_inc(consts, 1)
            nc.gpsimd.memset(eps[:, 1:2], EPS_HEAD).then_inc(consts, 1)
            for t in (kh, kl):
                nc.gpsimd.memset(t[:, :, :, :].bitcast(fp32), 0.0).then_inc(zeroed, 1)
            for t in (vh, vl):
                nc.gpsimd.memset(t[:, :, :].bitcast(fp32), 0.0).then_inc(zeroed, 1)
            for name, n in names.items():
                pool.sem_inc(s[name], n)
            pool.wait_ge(io_in, 32)
            with pool.Fori(0, NBATCH) as b:
                for n in range(NT):
                    pool.wait_ge(s["t1"], at(b, "t1", DC))
                    nc.gpsimd.tensor_tensor(xb[:, n], xb[:, n], bo[:, :], ALU.add).then_inc(s["bo"], 1)
                for c in range(DC):
                    pool.wait_ge(s["q_root"], at(b, "q_root", 2 * c + 2))
                    nc.gpsimd.tensor_tensor(qc[:, c], qc[:, c], rs[:, c % 2], ALU.mult).then_inc(s["q_n"], 1)

        @block.scalar
        def _(act):
            nc.scalar.preload_act_table_set("natural_log_exp_and_others")
            act.wait_ge(zeroed, 4)
            act.wait_ge(consts, 2)
            with act.Fori(0, NBATCH) as b:
                def roots(m):
                    act.wait_ge(s["moment"], at(b, "moment", m * NT))
                    nc.scalar.activation(rstd[:, :], moments[:, :, 1], ACT.Ln, bias=eps[:, 0:1]).then_inc(s["root"], 1)
                    act.wait_ge(s["root"], at(b, "root", 2 * m - 1))
                    nc.scalar.activation(rstd[:, :], rstd[:, :], ACT.Exp, scale=-0.5).then_inc(s["root"], 1)

                def q_root(c):
                    act.wait_ge(s["var"], at(b, "var", c + 1))
                    if c >= 2:
                        act.wait_ge(s["q_n"], at(b, "q_n", c - 1))
                    nc.scalar.activation(rs[:, c % 2], one(6 + c % 2), ACT.Ln, bias=eps[:, 1:2]).then_inc(s["q_root"], 1)
                    act.wait_ge(s["q_root"], at(b, "q_root", 2 * c + 1))
                    nc.scalar.activation(rs[:, c % 2], rs[:, c % 2], ACT.Exp, scale=-0.5).then_inc(s["q_root"], 1)

                roots(1)
                act.wait_ge(s["sc"], before(b, "sc"))
                act.wait_ge(s["pv"], before(b, "pv"))
                act.wait_ge(consts, 2)
                for h in range(HC):
                    nc.scalar.activation(kh[h * HD:(h + 1) * HD, :, h, :], keys_of(b, h), ACT.Copy).then_inc(s["k_hi"], 1)
                for half, j in HALVES:
                    nc.scalar.activation(values_at(vh, half, j), values_of(b, half, j), ACT.Copy).then_inc(s["v_hi"], 1)
                for c in range(DC):
                    act.wait_ge(s["t1"], at(b, "t1", c + 1))
                    nc.scalar.activation(xth[:, c], one(c), ACT.Copy).then_inc(s["x1_hi"], 1)
                act.wait_ge(s["lg"], before(b, "lg"))
                for c in range(DC):
                    act.wait_ge(s["q"], at(b, "q", c + 1))
                    nc.scalar.activation(qc[:, c], one(4 + c % 2), ACT.Identity, bias=biases[:, 0, c:c + 1]).then_inc(s["q_b"], 1)
                    nc.scalar.activation(qsq[:, c % 2], one(4 + c % 2), ACT.Square, bias=biases[:, 0, c:c + 1]).then_inc(s["q_sq"], 1)
                    if c >= 1:
                        q_root(c - 1)
                q_root(DC - 1)
                for c in range(DC):
                    act.wait_ge(s["q_aff"], at(b, "q_aff", c + 1))
                    nc.scalar.activation(qh[:, c], qc[:, c], ACT.Copy).then_inc(s["q_hi"], 1)

                def p_hi(n):
                    act.wait_ge(s["pt"], at(b, "pt", n + 1))
                    nc.scalar.activation(pth[:, :, n * P:(n + 1) * P], bank[2 + n % 2][:, :, :].rearrange(
                        "p a (j t) -> p (a j) t", t=P), ACT.Copy).then_inc(s["p_hi"], 1)
                for n in range(NT):
                    act.wait_ge(s["sub"], at(b, "sub", 2 * n + 2))
                    nc.scalar.activation(pf[:, n % 2], pf[:, n % 2], ACT.Exp).then_inc(s["ex"], 1)
                    if n >= 1:
                        p_hi(n - 1)
                p_hi(NT - 1)
                for c in range(DC):
                    act.wait_ge(s["pv"], at(b, "pv", c + 1))
                    nc.scalar.activation(cth[:, c], one(c), ACT.Copy).then_inc(s["c_hi"], 1)
                roots(2)
                act.wait_ge(s["x2"], at(b, "x2", NT))
                act.wait_ge(consts, 2)
                nc.scalar.activation(acc[:, bass.ds(b * NT, NT), :], xb[:, :, :], ACT.Copy).then_inc(s["kept"], 1)
                for c in range(DC):
                    act.wait_ge(s["t2"], at(b, "t2", c + 1))
                    nc.scalar.activation(qc[:, c], one(c), ACT.Copy).then_inc(s["xt"], 1)

        @block.vector
        def _(dve):
            dve.wait_ge(zeroed, 4)
            with dve.Fori(0, NBATCH) as b:
                def norm(src, dst, m):
                    for n in range(NT):
                        nc.vector.bn_stats(stats[:, n], src(n)).then_inc(s["stat"], 1)
                    dve.wait_ge(s["stat"], at(b, "stat", m * NT))
                    dve.sem_inc(s["stat_seen"], 1)
                    for n in range(NT):
                        dve.wait_ge(zeroed, 4)
                        nc.vector.bn_aggr(moments[:, n], stats[:, n]).then_inc(s["moment"], 1)
                    dve.wait_ge(s["root"], at(b, "root", 2 * m))
                    for n in range(NT):
                        nc.vector.tensor_scalar(dst(n), src(n), moments[:, n, 0:1], rstd[:, n:n + 1],
                                                ALU.subtract, ALU.mult).then_inc(s[("x1", "x2")[m - 1]], 1)

                def rows(n):
                    return acc[:, bass.ds(b * NT + n, 1), :].rearrange("p o d -> p (o d)")

                dve.wait_ge(s["kept"], before(b, "kept"))
                dve.wait_ge(s["t2"], before(b, "t2"))
                dve.wait_ge(zeroed, 4)
                norm(rows, lambda n: xb[:, n], 1)
                for h in range(HC):
                    dve.wait_ge(s["k_hi"], at(b, "k_hi", h + 1))
                    nc.vector.tensor_tensor(kl[h * HD:(h + 1) * HD, :, h, :], keys_of(b, h),
                                            kh[h * HD:(h + 1) * HD, :, h, :].bitcast(fp32), ALU.subtract).then_inc(s["k_lo"], 1)
                for n, (half, j) in enumerate(HALVES):
                    dve.wait_ge(s["v_hi"], at(b, "v_hi", n + 1))
                    nc.vector.tensor_tensor(values_at(vl, half, j), values_of(b, half, j),
                                            values_at(vh, half, j).bitcast(fp32), ALU.subtract).then_inc(s["v_lo"], 1)
                for c in range(DC):
                    dve.wait_ge(s["x1_hi"], at(b, "x1_hi", c + 1))
                    nc.vector.tensor_tensor(xtl[:, c], one(c), xth[:, c].bitcast(fp32), ALU.subtract).then_inc(s["x1_lo"], 1)
                for c in range(DC):
                    dve.wait_ge(s["q_n"], at(b, "q_n", c + 1))
                    nc.vector.tensor_scalar(qc[:, c], qc[:, c], biases[:, 5, 0:1], biases[:, 5, 1:2],
                                            ALU.mult, ALU.add).then_inc(s["q_aff"], 1)
                for c in range(DC):
                    dve.wait_ge(s["q_hi"], at(b, "q_hi", c + 1))
                    nc.vector.tensor_tensor(ql[:, c], qc[:, c], qh[:, c].bitcast(fp32), ALU.subtract).then_inc(s["q_lo"], 1)

                def scores(n):
                    return bank[n % 2][:, :, :].rearrange("p a (h k) -> p (a h) k", k=KT)

                def minus_max(n):
                    dve.wait_ge(s["sc"], at(b, "sc", n + 1))
                    for i, (a, z) in enumerate(SPANS):
                        nc.vector.tensor_reduce(mx[:, n % 2, :, i], scores(n)[:, :, a:z], AX.X, ALU.max).then_inc(s["mx"], 1)
                    for i, (a, z) in enumerate(SPANS):
                        dve.wait_ge(s["mx"], at(b, "mx", 2 * n + i + 1))
                        nc.vector.tensor_tensor(pf[:, n % 2, :, a:z], scores(n)[:, :, a:z],
                                                mx[:, n % 2, :, i:i + 1].broadcast_to([P, H, z - a]),
                                                ALU.subtract).then_inc(s["sub"], 1)

                def normalise(n):
                    dve.wait_ge(s["ex"], at(b, "ex", n + 1))
                    for i, (a, z) in enumerate(SPANS):
                        nc.vector.tensor_reduce(den[:, n % 2, :, i], pf[:, n % 2, :, a:z], AX.X, ALU.add).then_inc(s["sm"], 1)
                    dve.wait_ge(s["sm"], at(b, "sm", 2 * n + 2))
                    nc.vector.reciprocal(den[:, n % 2], den[:, n % 2]).then_inc(s["rc"], 1)
                    dve.wait_ge(s["rc"], at(b, "rc", n + 1))
                    for i, (a, z) in enumerate(SPANS):
                        nc.vector.tensor_tensor(pf[:, n % 2, :, a:z], pf[:, n % 2, :, a:z],
                                                den[:, n % 2, :, i:i + 1].broadcast_to([P, H, z - a]),
                                                ALU.mult).then_inc(s["nm"], 1)

                def p_lo(n):
                    dve.wait_ge(s["p_hi"], at(b, "p_hi", n + 1))
                    nc.vector.tensor_tensor(ptl[:, :, n * P:(n + 1) * P], bank[2 + n % 2][:, :, :].rearrange(
                        "p a (j t) -> p (a j) t", t=P), pth[:, :, n * P:(n + 1) * P].bitcast(fp32),
                        ALU.subtract).then_inc(s["p_lo"], 1)

                for n in range(NT + 1):
                    if n < NT:
                        if n >= 2:
                            dve.wait_ge(s["pt"], at(b, "pt", n - 1))
                        minus_max(n)
                    if n >= 1:
                        normalise(n - 1)
                    if n >= 2:
                        p_lo(n - 2)
                p_lo(NT - 1)
                for c in range(DC):
                    dve.wait_ge(s["c_hi"], at(b, "c_hi", c + 1))
                    nc.vector.tensor_tensor(ctl[:, c], one(c), cth[:, c].bitcast(fp32), ALU.subtract).then_inc(s["c_lo"], 1)
                for n in range(NT):
                    dve.wait_ge(s["bo"], at(b, "bo", NT))
                    dve.wait_ge(s["wo"], at(b, "wo", n + 1))
                    nc.vector.tensor_tensor(xb[:, n], one(4 + n), xb[:, n], ALU.add).then_inc(s["res"], 1)
                dve.wait_ge(s["res"], at(b, "res", NT))
                dve.wait_ge(zeroed, 4)
                norm(lambda n: xb[:, n], lambda n: xb[:, n], 2)
                dve.wait_ge(s["lg"], at(b, "lg", 1))
                nc.vector.tensor_copy(logits[:, bass.ds(b * NT, NT), :],
                                      one(4)[:, 0:NT * NE].rearrange("p (n e) -> p n e", e=NE)).then_inc(s["lg_out"], 1)

        @block.tensor
        def _(pe):
            def product(out, lh, ll, rh, rl, first, stop):
                nc.tensor.matmul(out, lh, rl, start=first, stop=False)
                nc.tensor.matmul(out, lh, rh, start=False, stop=False)
                return nc.tensor.matmul(out, ll, rh, start=False, stop=stop)

            pe.wait_ge(zeroed, 4)
            pe.wait_ge(consts, 2)
            with pe.Fori(0, NBATCH) as b:
                pe.wait_ge(s["x1"], at(b, "x1", NT))
                for c in range(DC):
                    for n in range(NT):
                        mm = nc.tensor.transpose(one(c)[:, n * P:(n + 1) * P], xb[:, n, c * P:(c + 1) * P], identity[:, :])
                    mm.then_inc(s["t1"], 1)

                def variance(c):
                    pe.wait_ge(s["q_sq"], at(b, "q_sq", c + 1))
                    if c >= 2:
                        pe.wait_ge(s["q_root"], at(b, "q_root", 2 * c - 3))
                    nc.tensor.matmul(one(6 + c % 2), head_mean[:, :], qsq[:, c % 2], start=True, stop=True).then_inc(s["var"], 1)

                pe.wait_ge(s["x1_lo"], at(b, "x1_lo", DC))
                for c in range(DC):
                    if c >= 2:
                        pe.wait_ge(s["q_sq"], at(b, "q_sq", c - 1))
                    for kc in range(DC):
                        cols = slice(c * P, (c + 1) * P)
                        mm = product(one(4 + c % 2), wqh[:, kc, cols], wql[:, kc, cols], xth[:, kc], xtl[:, kc],
                                     kc == 0, kc == DC - 1)
                    mm.then_inc(s["q"], 1)
                    if c >= 1:
                        variance(c - 1)
                variance(DC - 1)

                def turn(n):
                    pe.wait_ge(s["nm"], at(b, "nm", 2 * n + 2))
                    if n >= 2:
                        pe.wait_ge(s["p_lo"], at(b, "p_lo", n - 1))
                    for j in range(PAIRS):
                        mm = nc.tensor.transpose(bank[2 + n % 2][:, j // 4, (j % 4) * P:(j % 4 + 1) * P],
                                                 pf[:, n % 2, 2 * j:2 * j + 2, :].rearrange("p h k -> p (h k)"), identity[:, :])
                    mm.then_inc(s["pt"], 1)

                pe.wait_ge(s["k_lo"], at(b, "k_lo", HC))
                pe.wait_ge(s["q_lo"], at(b, "q_lo", DC))
                for n in range(NT):
                    if n >= 2:
                        pe.wait_ge(s["sub"], at(b, "sub", 2 * n - 2))
                    for c in range(DC):
                        toks = slice(n * P, (n + 1) * P)
                        out = bank[n % 2][:, c // 2, (c % 2) * HC * KT:(c % 2 + 1) * HC * KT]
                        keys = [k[:, c].rearrange("p h k -> p (h k)") for k in (kh, kl)]
                        mm = product(out, qh[:, c, toks], ql[:, c, toks], *keys, True, True)
                    mm.then_inc(s["sc"], 1)
                    if n >= 1:
                        turn(n - 1)
                turn(NT - 1)
                pe.wait_ge(s["v_lo"], at(b, "v_lo", 4))
                pe.wait_ge(s["p_lo"], at(b, "p_lo", NT))
                for c in range(DC):
                    for j in (2 * c, 2 * c + 1):
                        mm = product(one(c), vh[:, j], vl[:, j], pth[:, j], ptl[:, j], j == 2 * c, j == 2 * c + 1)
                    mm.then_inc(s["pv"], 1)
                pe.wait_ge(s["c_lo"], at(b, "c_lo", DC))
                for n in range(NT):
                    for c in range(DC):
                        toks = slice(n * P, (n + 1) * P)
                        mm = product(one(4 + n), cth[:, c, toks], ctl[:, c, toks], woh[:, c], wol[:, c],
                                     c == 0, c == DC - 1)
                    mm.then_inc(s["wo"], 1)
                pe.wait_ge(s["x2"], at(b, "x2", NT))
                for c in range(DC):
                    for n in range(NT):
                        mm = nc.tensor.transpose(one(c)[:, n * P:(n + 1) * P], xb[:, n, c * P:(c + 1) * P], identity[:, :])
                    mm.then_inc(s["t2"], 1)
                pe.wait_ge(s["xt"], at(b, "xt", DC))
                for n in range(NT):
                    for c in range(DC):
                        mm = nc.tensor.matmul(one(4)[:, n * NE:(n + 1) * NE], qc[:, c, n * P:(n + 1) * P], router[:, c],
                                              start=c == 0, stop=c == DC - 1)
                mm.then_inc(s["lg"], 1)


NE = 32
NT = T // P
NSLOT = NT + NE - 1


def stage_route(nc, acc, logits, pos, top, tile_expert, sorted_x, bank):
    with ExitStack() as held:
        def sb(name, shape, dtype=fp32):
            return held.enter_context(nc.sbuf_tensor("r_" + name, shape, dtype))

        def sem(name):
            return held.enter_context(nc.semaphore("r_" + name))

        mx, den, best = sb("mx", [P, NT]), sb("den", [P, NT]), sb("best", [P, NT])
        ex = sb("ex", [P, NT, NE])
        eq = sb("eq", [P, NT, NE])
        onehot = sb("onehot", [P, NT, NE])
        onehot_b = sb("onehot_b", [P, NT, NE], bf16)
        below = sb("below", [P, P], bf16)
        ones = sb("ones", [P, P], bf16)
        rev = sb("rev", [P, NE])
        marks = sb("marks", [P, NT])
        steps = sb("steps", [P, NSLOT])
        total, run_a, run_b = sb("total", [P, NT, NE]), sb("run_a", [P, NT, NE]), sb("run_b", [P, NT, NE])
        over = sb("over", [P, NE, NT])
        tiles, end, base = sb("tiles", [P, NE]), sb("end", [P, NE]), sb("base", [P, NE])
        done = sb("done", [P, NSLOT, NE])
        expert_f = sb("expert_f", [P, NSLOT])
        pos_f = sb("pos_f", [P, NT])
        consts, steps_done, exps, counted, placed = (sem("consts"), sem("steps"), sem("exps"), sem("counted"),
                                                     sem("placed"))
        ready, scattered = sem("ready"), sem("scattered")
        block = held.enter_context(nc.Block())
        N_CONST = 7

        @block.gpsimd
        def _(pool):
            nc.gpsimd.memset(ones[:, :], 1.0).then_inc(consts, 1)
            nc.gpsimd.memset(below[:, :], 1.0).then_inc(consts, 1)
            nc.gpsimd.iota(rev[:, :], pattern=[[-1, NE]], base=NE, channel_multiplier=0,
                           allow_small_or_imprecise_dtypes=True).then_inc(consts, 1)
            nc.gpsimd.iota(marks[:, :], pattern=[[P, NT]], base=0, channel_multiplier=0,
                           allow_small_or_imprecise_dtypes=True).then_inc(consts, 1)
            nc.gpsimd.iota(steps[:, :], pattern=[[1, NSLOT]], base=0, channel_multiplier=0,
                           allow_small_or_imprecise_dtypes=True).then_inc(consts, 1)
            pool.wait_ge(consts, 5)
            nc.gpsimd.affine_select(out=below[:, :], in_=below[:, :], compare_op=ALU.is_gt, fill=0.0, base=0,
                                    pattern=[[1, P]], channel_multiplier=-1).then_inc(consts, 2)
            pool.wait_ge(ready, 1)
            for n in range(NT):
                nc.gpsimd.indirect_dma_start(
                    out=sorted_x, out_offset=bass.IndirectOffsetOnAxis(ap=pos[:, n:n + 1], axis=0),
                    in_=acc[:, n, :], in_offset=None).then_inc(scattered, 16)
            pool.wait_ge(scattered, 16 * NT)

        @block.scalar
        def _(act):
            act.wait_ge(exps, 1)
            nc.scalar.activation(ex[:, :, :], ex[:, :, :], ACT.Exp).then_inc(exps, 1)

        @block.tensor
        def _(pe):
            pe.wait_ge(consts, N_CONST)
            pe.wait_ge(placed, 1)
            flat = onehot_b[:, :, :].rearrange("p n e -> p (n e)")
            nc.tensor.matmul(bank[0][:, :], below[:, :], flat, start=True, stop=True).then_inc(counted, 1)
            nc.tensor.matmul(bank[1][:, :], ones[:, :], flat, start=True, stop=True).then_inc(counted, 1)

        @block.vector
        def _(dve):
            count = [0]

            def step(ins):
                count[0] += 1
                ins.then_inc(steps_done, 1)
                dve.wait_ge(steps_done, count[0])

            def over_experts(t):
                return t[:, :].unsqueeze(2).broadcast_to([P, NT, NE])

            def over_tiles(t):
                return t[:, :].unsqueeze(1).broadcast_to([P, NT, NE])

            v = nc.vector
            step(v.tensor_reduce(mx[:, :], logits[:, :, :], AX.X, ALU.max))
            v.tensor_tensor(ex[:, :, :], logits[:, :, :], over_experts(mx), ALU.subtract).then_inc(exps, 1)
            dve.wait_ge(consts, N_CONST)
            step(v.tensor_tensor(eq[:, :, :], logits[:, :, :], over_experts(mx), ALU.is_equal))
            step(v.tensor_tensor(eq[:, :, :], eq[:, :, :], over_tiles(rev), ALU.mult))
            step(v.tensor_reduce(best[:, :], eq[:, :, :], AX.X, ALU.max))
            step(v.tensor_tensor(onehot[:, :, :], eq[:, :, :], over_experts(best), ALU.is_equal))
            v.tensor_copy(onehot_b[:, :, :], onehot[:, :, :]).then_inc(placed, 1)
            dve.wait_ge(exps, 2)
            step(v.tensor_reduce(den[:, :], ex[:, :, :], AX.X, ALU.add))
            step(v.reciprocal(top[:, :], den[:, :]))
            dve.wait_ge(counted, 2)
            step(v.tensor_copy(total[:, :, :], bank[1][:, :].rearrange("p (n e) -> p n e", e=NE)))
            src, dst = total, run_a
            k = 1
            while k < NT:
                v.tensor_copy(dst[:, 0:k], src[:, 0:k]).then_inc(steps_done, 1)
                count[0] += 1
                step(v.tensor_tensor(dst[:, k:NT], src[:, k:NT], src[:, 0:NT - k], ALU.add))
                src, dst = dst, (run_b if dst is run_a else run_a)
                k *= 2
            each = src[:, NT - 1, :].unsqueeze(2).broadcast_to([P, NE, NT])
            step(v.tensor_tensor(over[:, :, :], each, marks[:, :].unsqueeze(1).broadcast_to([P, NE, NT]), ALU.is_gt))
            step(v.tensor_reduce(tiles[:, :], over[:, :, :], AX.X, ALU.add))
            step(v.tensor_tensor_scan(end[:, :], tiles[:, :], tiles[:, :], 0.0, ALU.add, ALU.bypass))
            step(v.tensor_tensor(base[:, :], end[:, :], tiles[:, :], ALU.subtract))
            step(v.tensor_scalar(base[:, :], base[:, :], float(P), None, ALU.mult))
            step(v.tensor_tensor(src[:, :, :], src[:, :, :], total[:, :, :], ALU.subtract))
            step(v.tensor_tensor(src[:, :, :], src[:, :, :], over_tiles(base), ALU.add))
            step(v.tensor_tensor(src[:, :, :], bank[0][:, :].rearrange("p (n e) -> p n e", e=NE), src[:, :, :], ALU.add))
            step(v.tensor_tensor(src[:, :, :], src[:, :, :], onehot[:, :, :], ALU.mult))
            step(v.tensor_reduce(pos_f[:, :], src[:, :, :], AX.X, ALU.add))
            step(v.tensor_copy(pos[:, :], pos_f[:, :]))
            step(v.tensor_tensor(done[:, :, :], end[:, :].unsqueeze(1).broadcast_to([P, NSLOT, NE]),
                                 steps[:, :].unsqueeze(2).broadcast_to([P, NSLOT, NE]), ALU.is_le))
            step(v.tensor_reduce(expert_f[:, :], done[:, :, :], AX.X, ALU.add))
            step(v.tensor_scalar(expert_f[:, :], expert_f[:, :], float(NE - 1), None, ALU.min))
            v.tensor_copy(tile_expert[:, :], expert_f[0:1, :]).then_inc(ready, 1)


def stage_experts(nc, ins, tile_expert, identity, sorted_x, sorted_y, bank):
    maskT, w_ffnT = ins["maskT"], ins["w_ffnT"]
    RING = 4

    with ExitStack() as held:
        def sb(name, shape, dtype=fp32):
            return held.enter_context(nc.sbuf_tensor("e_" + name, shape, dtype))

        def sem(name):
            return held.enter_context(nc.semaphore("e_" + name))

        ternary, low = sb("ternary", [P, DC, D]), sb("low", [P, DC, D])
        m = [sb(f"m{i}", [P, DC, D]) for i in range(RING)]
        xs = [sb(f"xs{i}", [P, D]) for i in range(RING)]
        xt = [sb(f"xt{i}", [P, D]) for i in range(RING)]
        ys = [sb(f"ys{i}", [P, D]) for i in range(RING)]
        t_in, t_steps = sem("t_in"), sem("t_steps")
        m_in, x_in, y_out = ([sem(f"{k}{i}") for i in range(RING)] for k in ("m_in", "x_in", "y_out"))
        counted = ("masked", "turned", "x_copied", "y", "y_copied")
        s = {k: sem(k) for k in counted}
        block = held.enter_context(nc.Block())

        def passes(eng, body):
            with eng.Fori(0, NSLOT // RING) as i:
                for r in range(RING):
                    body(i * RING + r, r)
            for t in range(NSLOT // RING * RING, NSLOT):
                body(t, t % RING)

        def through(t):
            return t + RING + 1

        def freed(t):
            return t + 1

        def arrived(t, r):
            return 4 * (t - r) + 16

        def rows(dram, t):
            return dram[bass.ds(t * P, P), :] if type(t) is not int else dram[t * P:(t + 1) * P, :]

        @block.sync
        def _(sp):
            sp.dma_start(m[RING - 1][:, :, :], w_ffnT.rearrange("(c p) n -> p c n", p=P)).then_inc(t_in, 16)

            def body(t, r):
                e = sp.value_load(tile_expert[0:1, bass.ds(t, 1)], min_val=0, max_val=NE - 1)
                sp.wait_ge(s["turned"], freed(t))
                sp.dma_start(xs[r][:, :], rows(sorted_x, t)).then_inc(x_in[r], 16)
                sp.wait_ge(s["y"], freed(t))
                if r == RING - 1:
                    sp.wait_ge(t_steps, 2)
                sp.dma_start(m[r][:, :, :], maskT[bass.ds(e, 1)].rearrange("o (c p) n -> p (o c) n", p=P)
                             ).then_inc(m_in[r], 16)
            passes(sp, body)

        @block.gpsimd
        def _(pool):
            for k in counted:
                pool.sem_inc(s[k], RING)
            for o in y_out:
                pool.sem_inc(o, 16)

        @block.vector
        def _(dve):
            dve.wait_ge(t_in, 16)
            nc.vector.tensor_scalar(low[:, :, :], m[RING - 1][:, :, :], -0.25, None, ALU.is_lt).then_inc(t_steps, 1)
            nc.vector.tensor_scalar(ternary[:, :, :], m[RING - 1][:, :, :], 0.25, None, ALU.is_gt).then_inc(t_steps, 1)
            dve.wait_ge(t_steps, 2)
            nc.vector.tensor_tensor(ternary[:, :, :], ternary[:, :, :], low[:, :, :], ALU.subtract).then_inc(t_steps, 1)
            dve.wait_ge(t_steps, 3)

            def body(t, r):
                dve.wait_ge(m_in[r], arrived(t, r))
                nc.vector.tensor_tensor(m[r][:, :, :], m[r][:, :, :], ternary[:, :, :], ALU.mult).then_inc(s["masked"], 1)
            passes(dve, body)

        @block.scalar
        def _(act):
            def turned_out(t, r):
                act.wait_ge(s["turned"], through(t))
                act.wait_ge(s["y"], freed(t))
                nc.scalar.activation(xt[r][:, :], bank[r][:, :], ACT.Copy).then_inc(s["x_copied"], 1)

            def y_out_of(t, r):
                act.wait_ge(s["y"], through(t))
                act.wait_ge(y_out[r], arrived(t, r))
                nc.scalar.activation(ys[r][:, :], bank[RING + r][:, :], ACT.Copy).then_inc(s["y_copied"], 1)
                act.wait_ge(s["y_copied"], through(t))
                act.dma_start(rows(sorted_y, t), ys[r][:, :]).then_inc(y_out[r], 16)

            turned_out(0, 0)

            def body(t, r):
                if type(t) is not int or t < NSLOT - 1:
                    turned_out(t + 1, (r + 1) % RING)
                y_out_of(t, r)
            passes(act, body)
            for r in range(RING):
                act.wait_ge(y_out[r], 16 * ((NSLOT - 1 - r) // RING + 2))

        @block.tensor
        def _(pe):
            def turn(t, r):
                pe.wait_ge(x_in[r], arrived(t, r))
                pe.wait_ge(s["x_copied"], freed(t))
                for c in range(DC):
                    cols = slice(c * P, (c + 1) * P)
                    mm = nc.tensor.transpose(bank[r][:, cols], xs[r][:, cols], identity[:, :])
                mm.then_inc(s["turned"], 1)

            turn(0, 0)

            def body(t, r):
                if type(t) is not int or t < NSLOT - 1:
                    turn(t + 1, (r + 1) % RING)
                pe.wait_ge(s["x_copied"], through(t))
                pe.wait_ge(s["masked"], through(t))
                pe.wait_ge(s["y_copied"], freed(t))
                for c in range(DC):
                    mm = nc.tensor.matmul(bank[RING + r][:, :], xt[r][:, c * P:(c + 1) * P], m[r][:, c],
                                          start=c == 0, stop=c == DC - 1)
                mm.then_inc(s["y"], 1)
            passes(pe, body)


def stage_last(nc, ins, out, acc, pos, top, sorted_y):
    RING = 4

    with ExitStack() as held:
        def sb(name, shape, dtype=fp32):
            return held.enter_context(nc.sbuf_tensor("l_" + name, shape, dtype))

        def sem(name):
            return held.enter_context(nc.semaphore("l_" + name))

        y = [sb(f"y{i}", [P, D]) for i in range(RING)]
        scale = sb("scale", [P, D])
        stats, moments, rstd, eps = (sb("stats", [P, NT, 6]), sb("moments", [P, NT, 2]), sb("rstd", [P, NT]),
                                     sb("eps", [P, 1]))
        scale_in, eps_set = sem("scale_in"), sem("eps_set")
        y_in = [sem(f"y_in{i}") for i in range(RING)]
        scaled, summed, stat, moment, root, normed, out_done = (
            sem(k) for k in ("scaled", "summed", "stat", "moment", "root", "normed", "out_done"))
        block = held.enter_context(nc.Block())

        @block.gpsimd
        def _(pool):
            nc.gpsimd.memset(eps[:, :], EPS_LN).then_inc(eps_set, 1)

            def gather(n):
                if n >= RING:
                    pool.wait_ge(summed, n - RING + 1)
                nc.gpsimd.indirect_dma_start(
                    out=y[n % RING][:, :], out_offset=None, in_=sorted_y,
                    in_offset=bass.IndirectOffsetOnAxis(ap=pos[:, n:n + 1], axis=0)).then_inc(y_in[n % RING], 16)

            for n in range(RING - 1):
                gather(n)
            pool.wait_ge(scale_in, 16)
            for n in range(NT):
                if n + RING - 1 < NT:
                    gather(n + RING - 1)
                pool.wait_ge(y_in[n % RING], 16 * (n // RING + 1))
                nc.gpsimd.tensor_tensor(y[n % RING][:, :], y[n % RING][:, :], scale[:, :], ALU.mult).then_inc(scaled, 1)

        @block.vector
        def _(dve):
            def finish(n):
                dve.wait_ge(root, 2 * n + 2)
                nc.vector.tensor_scalar(acc[:, n], acc[:, n], moments[:, n, 0:1], rstd[:, n:n + 1],
                                        ALU.subtract, ALU.mult).then_inc(normed, 1)
            for n in range(NT):
                dve.wait_ge(scaled, n + 1)
                nc.vector.scalar_tensor_tensor(acc[:, n], y[n % RING][:, :], top[:, n:n + 1], acc[:, n],
                                               ALU.mult, ALU.add).then_inc(summed, 1)
                dve.wait_ge(summed, n + 1)
                nc.vector.bn_stats(stats[:, n], acc[:, n]).then_inc(stat, 1)
                dve.wait_ge(stat, n + 1)
                nc.vector.bn_aggr(moments[:, n], stats[:, n]).then_inc(moment, 1)
                if n >= 1:
                    finish(n - 1)
            finish(NT - 1)

        @block.scalar
        def _(act):
            act.wait_ge(eps_set, 1)
            for n in range(NT):
                act.wait_ge(moment, n + 1)
                nc.scalar.activation(rstd[:, n:n + 1], moments[:, n, 1:2], ACT.Ln, bias=eps[:, 0:1]).then_inc(root, 1)
                act.wait_ge(root, 2 * n + 1)
                nc.scalar.activation(rstd[:, n:n + 1], rstd[:, n:n + 1], ACT.Exp, scale=-0.5).then_inc(root, 1)

        @block.sync
        def _(sp):
            sp.dma_start(scale[:, :], ins["scale"].broadcast_to([P, D])).then_inc(scale_in, 16)
            for n in range(NT):
                sp.wait_ge(normed, n + 1)
                sp.dma_start(out[n * P:(n + 1) * P, :], acc[:, n]).then_inc(out_done, 16)
            sp.wait_ge(out_done, 16 * NT)


def build(nc, out, ins):
    with ExitStack() as held:
        def sb(name, shape, dtype=fp32):
            return held.enter_context(nc.sbuf_tensor(name, shape, dtype))

        pairs = [held.enter_context(nc.psum_tensor(f"bank{i}", [P, 2, 512], fp32)) for i in range(4)]
        bank = [pairs[i // 2][:, i % 2, :] for i in range(8)]
        acc = sb("acc", [P, NT, D])
        identity = sb("identity", [P, P])
        logits = sb("logits", [P, NT, NE])
        pos, top = sb("pos", [P, NT], u32), sb("top", [P, NT])
        tile_expert = sb("tile_expert", [1, NSLOT], i32)
        sorted_x = nc.dram_tensor("sorted_x", [NSLOT * P, D], fp32, kind="Internal").ap()
        sorted_y = nc.dram_tensor("sorted_y", [NSLOT * P, D], fp32, kind="Internal").ap()

        with ExitStack() as part:
            xyh = part.enter_context(nc.sbuf_tensor("xyh", [P, DC, T], fp32r))
            xyl = part.enter_context(nc.sbuf_tensor("xyl", [P, DC, T], fp32r))
            wh = part.enter_context(nc.sbuf_tensor("wh", [P, 3, DC, D], fp32r))
            wl = part.enter_context(nc.sbuf_tensor("wl", [P, 3, DC, D], fp32r))
            used_sems = stage_qkv(nc, ins, xyh, xyl, wh, wl, acc, bank)
            zeros = part.enter_context(nc.sbuf_tensor("zeros", [P, D], fp32))
            stage_swiglu(nc, ins, xyh, xyl, wh, wl, acc, identity, zeros, sorted_x, used_sems, bank)
        with ExitStack() as part:
            def of_part(name, shape, dtype=fp32):
                return part.enter_context(nc.sbuf_tensor(name, shape, dtype))

            kT, vrows = of_part("kT", [P, DC, NBATCH * KT]), of_part("vrows", [P, NBATCH, D])
            head_mean, biases = of_part("head_mean", [P, P]), of_part("biases", [P, 6, DC])
            weights = [of_part(name, [P, DC, D], fp32r) for name in ("wqh", "wql", "woh", "wol")]
            stage_context(nc, ins, kT, vrows, head_mean, biases, *weights, bank)
            stage_cross(nc, ins, acc, logits, kT, vrows, head_mean, biases, identity, *weights, pairs)
        stage_route(nc, acc, logits, pos, top, tile_expert, sorted_x, bank)
        stage_experts(nc, ins, tile_expert, identity, sorted_x, sorted_y, bank)
        stage_last(nc, ins, out, acc, pos, top, sorted_y)


def layouts(given):
    g = {name: np.asarray(a) for name, a in given.items()}

    def keys_values(w):
        w = w.reshape(w.shape[0], H, 2, HD)
        return w[:, :, 0].reshape(-1, D), w[:, :, 1].reshape(-1, D)

    def column(b):
        return b.reshape(DC, P).T

    parts = 8
    inner = g["L0_attn_w_out"].shape[1]
    wk_main, wv_main = keys_values(np.concatenate([g["L0_xattn_Wk"], g["L0_xattn_Wv"]], 1))
    bk_main, bv_main = keys_values(np.concatenate([g["L0_xattn_bk"], g["L0_xattn_bv"]])[None])
    w_last, b_last = g["L0_xattn_Wkv_dca"], g["L0_xattn_bkv_dca"]
    biases = np.zeros((P, 6, DC), np.float32)
    biases[:, 0], biases[:, 1], biases[:, 2] = column(g["L0_xattn_bq"]), column(bk_main[0]), column(b_last[:D])
    for n, name in enumerate(("kn", "kn_dca", "qn")):
        biases[:, 3 + n, 0] = np.tile(g[f"L0_xattn_{name}_w"], HC)
        biases[:, 3 + n, 1] = np.tile(g[f"L0_xattn_{name}_b"], HC)
    ins = dict(
        x=g["x"].reshape(T, D), xT=g["x"].transpose(0, 2, 1),
        wqkvT=g["L0_attn_w_qkv"].reshape(3, D, D).transpose(0, 2, 1),
        wsT=g["L0_attn_w_swiglu"].reshape(2, parts, inner // parts, DC, P).transpose(1, 4, 3, 0, 2),
        woT=g["L0_attn_w_out"].reshape(D, parts, inner // parts // P, P).transpose(1, 3, 2, 0),
        wk_main=wk_main, wv_main=wv_main, wk_last=w_last[:, :D], wv_last=w_last[:, D:],
        ctxT=g["ctx_1024"].transpose(2, 0, 1), biases=biases, bv=np.stack([bv_main[0], b_last[D:]])[None],
        wq=g["L0_xattn_Wq"], wo=g["L0_xattn_Wo"], bo=g["L0_xattn_bo"][None],
        w_ffnT=g["L0_ffn_weight"].T, scale=g["L0_ffn_scale"][None],
        maskT=g["L0_ffn_expert_masks"].transpose(0, 2, 1), routerT=g["L0_ffn_router_w"].T)
    return {name: np.ascontiguousarray(a) for name, a in ins.items()}


def kernel(**inputs):
    import concourse.bacc as bacc
    from concourse.bass_utils import run_bass_kernel_spmd

    nc = bacc.Bacc("TRN2", target_bir_lowering=False, num_devices=1)
    arrays = layouts(inputs)
    ins = {name: nc.dram_tensor(f"in_{name}_dram", a.shape, mybir.dt.from_np(a.dtype), kind="ExternalInput").ap()
           for name, a in arrays.items()}
    out = nc.dram_tensor("out_0_dram", (T, D), fp32, kind="ExternalOutput").ap()
    build(nc, out, ins)
    r = run_bass_kernel_spmd(nc, [{f"in_{name}_dram": a for name, a in arrays.items()}], core_ids=[0])
    return r.results[0]["out_0_dram"].reshape(NBATCH, S, D)
```

```python
import numpy as np
import concourse.bass as bass
from concourse import mybir
from contextlib import ExitStack

fp32 = mybir.dt.float32
fp32r = mybir.dt.float32r
bf16 = mybir.dt.bfloat16
i32 = mybir.dt.int32
u32 = mybir.dt.uint32
ALU = mybir.AluOpType
ACT = mybir.ActivationFunctionType
AX = mybir.AxisListType

P = 128
NBATCH = 4
S = 512
T = NBATCH * S
D = 512
DC = D // P
EPS_RMS = 1.1920929e-07
EPS_CUM = 1e-6


def this(i, n, m):
    return n * (i + 1) + m


def last(i, n, m):
    return n * i + m


def swiglu_weights(w, n):
    return w[:, n].rearrange("p c (u f) -> p c u f", u=2), w[:, 2, 2 * n:2 * n + 2]


def stage_qkv(nc, ins, xyh, xyl, wh, wl, acc, bank):
    xT, wqkvT = ins["xT"], ins["wqkvT"]
    LOADS = [("x", 0), ("x", 1), ("x", 2), ("x", 3), ("w", 1), ("w", 0), ("w", 2)]
    RING = 6
    K, Q, V = 0, 1, 2
    W_OF = {K: 1, Q: 0, V: 2}
    N_PROJ, N_KQ, N_ADD, N_C, N_ROOT = 3 * DC, 2 * DC, 6, 6, 4
    DOWN = 20
    HALF = 2 * DC

    with ExitStack() as held:
        def sb(name, shape, dtype):
            return held.enter_context(nc.sbuf_tensor(name, shape, dtype))

        sems = []

        def sem(name):
            sems.append(nc.alloc_semaphore(name))
            return sems[-1]

        sq = acc[:, 2 * DC:4 * DC, :]
        raw_s, raw_o = acc[:, HALF:HALF + DC, :], acc[:, HALF + DC:HALF + DC + 2, :]
        qbuf = sb("a_q", [P, 2 * DC, S], fp32)
        kbuf = sb("a_k", [P, 2 * DC, S], fp32)
        vbuf = sb("a_v", [P, DC, S], fp32)
        sqsum = sb("a_sqsum", [P, 2, S], fp32)
        rx = sb("a_r", [P, NBATCH, S], fp32)
        ckq = sb("a_ckq", [P, 2, S], fp32)
        mean_w = sb("a_mean", [P, P], fp32)
        eps = sb("a_eps", [P, 2], fp32)
        raw = [buf[:, n * DC:(n + 1) * DC, :] for buf, n in
               ((acc, 0), (acc, 1), (kbuf, 0), (kbuf, 1), (qbuf, 0), (qbuf, 1), (acc, 3))]
        raw_in = [sem(f"a_raw{l}_in") for l in range(len(LOADS))]
        consts = sem("a_consts")
        x_hi, w_hi = sem("a_x_hi"), sem("a_w_hi")
        lo_made = sem("a_lo_made")
        xsq_made = sem("a_xsq_made")
        xsq_add = sem("a_xsq_add")
        x_ms = sem("a_x_ms")
        x_root = sem("a_x_root")
        proj = sem("a_proj")
        kq_read = sem("a_kq_read")
        sq_add = sem("a_sq_add")
        ms_made = sem("a_ms_made")
        c_scaled = sem("a_c_scaled")
        c_root = sem("a_c_root")
        normed = sem("a_normed")
        exped = sem("a_exped")
        v_scaled, v_weighed, v_summed = sem("a_v_scaled"), sem("a_v_weighed"), sem("a_v_summed")
        w_summed = sem("a_w_summed")
        divisor, log, inverse = sem("a_divisor"), sem("a_log"), sem("a_inverse")
        terms, y_made, y_hi, y_lo = sem("a_terms"), sem("a_y_made"), sem("a_y_hi"), sem("a_y_lo")
        next_in, next_hi, next_lo = sem("a_next_in"), sem("a_next_hi"), sem("a_next_lo")
        x_rows_in = sem("a_x_rows_in")
        block = held.enter_context(nc.Block())
        looped = [(proj, N_PROJ), (kq_read, N_KQ), (sq_add, N_ADD), (ms_made, 2),
                  (c_scaled, N_C), (c_root, N_ROOT), (normed, N_KQ), (exped, N_KQ), (v_scaled, DC),
                  (v_weighed, DC), (v_summed, DC), (w_summed, DC), (divisor, DC), (log, DC),
                  (inverse, DC), (terms, 2 * DC), (y_made, DC), (y_hi, DC), (y_lo, DC)]

        def end(n):
            return this(NBATCH - 1, n, n)


        def split_target(l):
            kind, n = LOADS[l]
            if kind == "w":
                return wh[:, n], wl[:, n]
            return xyh[:, :, n * S:(n + 1) * S], xyl[:, :, n * S:(n + 1) * S]

        def half(buf, par, c):
            return buf[:, par * DC + c, :]

        def tokens(buf, b, c):
            return buf[:, c, bass.ds(b * S, S)]

        @block.sync
        def _(sp):
            for l, (kind, n) in enumerate(LOADS):
                src = wqkvT[n] if kind == "w" else xT[n]
                sp.dma_start(raw[l], src.rearrange("(c p) t -> p c t", p=P)).then_inc(raw_in[l], 16)
            sp.wait_ge(lo_made, len(LOADS))
            sp.wait_ge(xsq_made, NBATCH)
            sp.dma_start(acc[:, 0:HALF, :], ins["x"][0:HALF * P, :].rearrange("(n p) d -> p n d", p=P)
                         ).then_inc(x_rows_in, 16)
            sp.wait_ge(sq_add, end(N_ADD))
            sp.dma_start(raw_s.rearrange("p c (u f) -> p c u f", u=2), ins["wsT"][0]).then_inc(next_in, 16)
            sp.dma_start(raw_o, ins["woT"][0]).then_inc(next_in, 16)

        @block.tensor
        def _(pe):
            def mean_square(out, src):
                return nc.tensor.matmul(out[:, :], mean_w[:, :], src, start=True, stop=True)

            pe.wait_ge(consts, 3)
            for n in range(NBATCH):
                pe.wait_ge(xsq_add, 2 * n + 2)
                mean_square(bank[4 + n], sqsum[:, n % 2]).then_inc(x_ms, 1)
            with pe.Fori(0, NBATCH // 2) as pair:
                for par in range(2):
                    b = pair * 2 + par
                    for j in range(N_PROJ):
                        which, c = j // DC, j % DC
                        if j < 2:
                            pe.wait_ge(kq_read, last(b, N_KQ, 7 + j))
                        elif j < RING:
                            pe.wait_ge(v_scaled, last(b, DC, j - 1))
                        else:
                            pe.wait_ge(kq_read, this(b, N_KQ, j - RING + 1))
                        if j % DC == 0:
                            pe.wait_ge(lo_made, LOADS.index(("w", W_OF[which])) + 1)
                        if j == 4:
                            pe.wait_ge(x_root, 2 * NBATCH)
                        out = bank[j % RING][:, :]
                        w, cols = W_OF[which], slice(c * P, (c + 1) * P)
                        for kc in range(DC):
                            xh, xl = tokens(xyh, b, kc), tokens(xyl, b, kc)
                            nc.tensor.matmul(out, wh[:, w, kc, cols], xl, start=kc == 0, stop=False)
                            nc.tensor.matmul(out, wh[:, w, kc, cols], xh, start=False, stop=False)
                            mm = nc.tensor.matmul(out, wl[:, w, kc, cols], xh, start=False, stop=kc == DC - 1)
                        mm.then_inc(proj, 1)
                        if j == DC + 2 or j == 2 * DC + 2:
                            w = j // DC - 1
                            pe.wait_ge(sq_add, this(b, N_ADD, 3 * w + 3))
                            pe.wait_ge(c_scaled, last(b, N_C, 3 * w + 1))
                            mean_square(bank[6 + w], sqsum[:, w]).then_inc(ms_made, 1)

        @block.scalar
        def _(act):
            def root(dst, src, sem, value):
                nc.scalar.activation(dst, src, ACT.Ln, bias=eps[:, 0:1]).then_inc(sem, 1)
                act.wait_ge(sem, value)
                nc.scalar.activation(dst, dst, ACT.Exp, scale=-0.5).then_inc(sem, 1)

            nc.scalar.preload_act_table_set("natural_log_exp_and_others")
            act.wait_ge(consts, 3)
            for n in range(NBATCH):
                l = LOADS.index(("x", n))
                act.wait_ge(raw_in[l], 16)
                nc.scalar.activation(split_target(l)[0], raw[l], ACT.Copy).then_inc(x_hi, 1)
                if n:
                    act.wait_ge(xsq_add, 2 * n)
                nc.scalar.activation(sq[:, 0:DC, :], raw[l], ACT.Square).then_inc(xsq_made, 1)
            for n in range(NBATCH):
                act.wait_ge(x_ms, n + 1)
                root(rx[:, n], bank[4 + n][:, :], x_root, 2 * n + 1)
            act.wait_ge(xsq_add, 2 * NBATCH)
            act.wait_ge(lo_made, len(LOADS))

            def log_of(b, par, c):
                act.wait_ge(divisor, this(b, DC, c + 1))
                nc.scalar.activation(half(qbuf, par, c), half(kbuf, par, c), ACT.Ln, scale=2.0 ** -DOWN).then_inc(log, 1)

            def inverse_of(b, par, c):
                act.wait_ge(log, this(b, DC, c + 1))
                nc.scalar.activation(half(qbuf, par, c), half(qbuf, par, c), ACT.Exp, scale=-1.0,
                                     bias=eps[:, 1:2]).then_inc(inverse, 1)

            def gate_step(b, par, n):
                if n < DC:
                    log_of(b, par, n)
                if 1 <= n <= DC:
                    inverse_of(b, par, n - 1)

            def batch(b, par, before):
                for j in range(2 * DC):
                    buf, c = (kbuf, qbuf)[j // DC], j % DC
                    act.wait_ge(proj, this(b, N_PROJ, j + 1))
                    if j == 0:
                        act.wait_ge(sq_add, last(b, N_ADD, 6))
                        act.wait_ge(v_scaled, last(b, DC, 1))
                    nc.scalar.activation(half(buf, par, c), bank[j % RING][:, :], ACT.Copy)
                    nc.scalar.activation(sq[:, j], bank[j % RING][:, :], ACT.Square).then_inc(kq_read, 1)
                    if before is not None:
                        gate_step(*before, j)
                for w, buf in enumerate((kbuf, qbuf)):
                    act.wait_ge(c_scaled, this(b, N_C, 3 * w + 2))
                    root(ckq[:, w], ckq[:, w], c_root, this(b, N_ROOT, 2 * w + 1))
                    for c in range(DC):
                        act.wait_ge(normed, this(b, N_KQ, DC * w + c + 1))
                        nc.scalar.activation(half(buf, par, c), half(buf, par, c), ACT.Exp,
                                             scale=(1.0, -1.0)[w]).then_inc(exped, 1)

            with act.Fori(0, NBATCH // 2) as pair:
                batch(pair * 2, 0, None)
                batch(pair * 2 + 1, 1, (pair * 2, 0))
                for n in range(DC + 1):
                    gate_step(pair * 2 + 1, 1, n)

        @block.gpsimd
        def _(pool):
            nc.gpsimd.memset(mean_w[:, :], 1.0 / D).then_inc(consts, 1)
            nc.gpsimd.memset(eps[:, 0:1], EPS_RMS).then_inc(consts, 1)
            nc.gpsimd.memset(eps[:, 1:2], -DOWN * float(np.log(2.0))).then_inc(consts, 1)
            for sem, n in looped:
                pool.sem_inc(sem, n)
            for n in range(NBATCH):
                pool.wait_ge(xsq_made, n + 1)
                if n >= 2:
                    pool.wait_ge(x_ms, n - 1)
                nc.gpsimd.tensor_tensor(sq[:, 0:2], sq[:, 0:2], sq[:, 2:4], ALU.add).then_inc(xsq_add, 1)
                pool.wait_ge(xsq_add, 2 * n + 1)
                nc.gpsimd.tensor_tensor(sqsum[:, n % 2], sq[:, 0], sq[:, 1], ALU.add).then_inc(xsq_add, 1)
            pool.wait_ge(x_ms, NBATCH)
            with pool.Fori(0, NBATCH // 2) as pair:
                for par in range(2):
                    b = pair * 2 + par
                    for w, buf in enumerate((kbuf, qbuf)):
                        for c in range(1, DC):
                            pool.wait_ge(kq_read, this(b, N_KQ, DC * w + c + 1))
                            if c == 1:
                                pool.wait_ge(ms_made, last(b, 2, w + 1))
                            else:
                                pool.wait_ge(sq_add, this(b, N_ADD, 3 * w + c - 1))
                            nc.gpsimd.tensor_tensor(sqsum[:, w], sq[:, DC * w] if c == 1 else sqsum[:, w],
                                                    sq[:, DC * w + c], ALU.add).then_inc(sq_add, 1)
                    for w, buf in enumerate((kbuf, qbuf)):
                        pool.wait_ge(c_scaled, this(b, N_C, 3 * w + 3))
                        for c in range(DC):
                            nc.gpsimd.tensor_tensor(half(buf, par, c), half(buf, par, c), ckq[:, w],
                                                    ALU.mult).then_inc(normed, 1)
            pool.wait_ge(proj, end(N_PROJ))
            pool.wait_ge(next_in, 32)
            for n, raw_w in enumerate((raw_s.rearrange("p c (u f) -> p c u f", u=2), raw_o)):
                nc.gpsimd.tensor_copy(swiglu_weights(wh, 0)[n], raw_w).then_inc(next_hi, 1)
            pool.wait_ge(next_hi, 1)
            nc.gpsimd.tensor_tensor(swiglu_weights(wl, 0)[0], raw_s.rearrange("p c (u f) -> p c u f", u=2),
                                    swiglu_weights(wh, 0)[0].bitcast(fp32), ALU.subtract).then_inc(next_lo, 1)
            pool.wait_ge(x_rows_in, 16)

        @block.vector
        def _(dve):
            for l, (kind, n) in enumerate(LOADS):
                hi, lo = split_target(l)
                if kind == "x":
                    dve.wait_ge(x_hi, n + 1)
                else:
                    dve.wait_ge(raw_in[l], 16)
                    nc.vector.tensor_copy(hi, raw[l]).then_inc(w_hi, 1)
                    dve.wait_ge(w_hi, l + 1 - NBATCH)
                nc.vector.tensor_tensor(lo, raw[l], hi.bitcast(fp32), ALU.subtract).then_inc(lo_made, 1)
            dve.wait_ge(x_root, 2 * NBATCH)
            with dve.Fori(0, NBATCH // 2) as pair:
                for par in range(2):
                    b = pair * 2 + par
                    r = rx[:, bass.ds(b, 1), :].rearrange("p o t -> p (o t)")

                    def mean_of_normed(w):
                        dve.wait_ge(ms_made, this(b, 2, w + 1))
                        dve.wait_ge(normed, last(b, N_KQ, DC * w + DC))
                        nc.vector.tensor_tensor(ckq[:, w], bank[6 + w][:, :], r, ALU.mult).then_inc(c_scaled, 1)
                        dve.wait_ge(c_scaled, this(b, N_C, 3 * w + 1))
                        nc.vector.tensor_tensor(ckq[:, w], ckq[:, w], r, ALU.mult).then_inc(c_scaled, 1)

                    def factor(w):
                        dve.wait_ge(c_root, this(b, N_ROOT, 2 * w + 2))
                        nc.vector.tensor_tensor(ckq[:, w], ckq[:, w], r, ALU.mult).then_inc(c_scaled, 1)

                    def sums(c):
                        expk, v = half(kbuf, par, c), vbuf[:, c]
                        dve.wait_ge(proj, this(b, N_PROJ, 2 * DC + c + 1))
                        dve.wait_ge(y_lo, last(b, DC, c + 1))
                        nc.vector.tensor_tensor(v, bank[(2 * DC + c) % RING][:, :], r, ALU.mult).then_inc(v_scaled, 1)
                        dve.wait_ge(exped, this(b, N_KQ, c + 1))
                        dve.wait_ge(v_scaled, this(b, DC, c + 1))
                        nc.vector.tensor_tensor(v, v, expk, ALU.mult).then_inc(v_weighed, 1)
                        dve.wait_ge(v_weighed, this(b, DC, c + 1))
                        nc.vector.tensor_tensor_scan(expk, expk, expk, EPS_CUM, ALU.add, ALU.bypass).then_inc(w_summed, 1)
                        nc.vector.tensor_tensor_scan(v, v, v, 0.0, ALU.add, ALU.bypass).then_inc(v_summed, 1)

                    def divide_by(c):
                        expk = half(kbuf, par, c)
                        dve.wait_ge(exped, this(b, N_KQ, DC + c + 1))
                        dve.wait_ge(w_summed, this(b, DC, c + 1))
                        nc.vector.scalar_tensor_tensor(expk, half(qbuf, par, c), 1.0, expk, ALU.add, ALU.mult
                                                       ).then_inc(divisor, 1)

                    def gate_terms(c):
                        v, d, i = vbuf[:, c], half(kbuf, par, c), half(qbuf, par, c)
                        dve.wait_ge(inverse, this(b, DC, c + 1))
                        dve.wait_ge(v_summed, this(b, DC, c + 1))
                        nc.vector.scalar_tensor_tensor(d, d, -1.0, i, ALU.mult, ALU.mult).then_inc(terms, 1)
                        nc.vector.tensor_tensor(v, v, i, ALU.mult).then_inc(terms, 1)

                    def gated(c):
                        v, d = vbuf[:, c], half(kbuf, par, c)
                        dve.wait_ge(proj, this(b, N_PROJ, N_PROJ))
                        dve.wait_ge(terms, this(b, 2 * DC, 2 * c + 2))
                        nc.vector.scalar_tensor_tensor(v, d, 2.0, v, ALU.add, ALU.mult).then_inc(y_made, 1)

                    def high(c):
                        dve.wait_ge(y_made, this(b, DC, c + 1))
                        nc.vector.tensor_copy(tokens(xyh, b, c), vbuf[:, c]).then_inc(y_hi, 1)

                    def low(c):
                        dve.wait_ge(y_hi, this(b, DC, c + 1))
                        nc.vector.tensor_tensor(tokens(xyl, b, c), vbuf[:, c], tokens(xyh, b, c).bitcast(fp32),
                                                ALU.subtract).then_inc(y_lo, 1)

                    mean_of_normed(0)
                    factor(0)
                    sums(0)
                    mean_of_normed(1)
                    sums(1)
                    factor(1)
                    sums(2)
                    divide_by(0)
                    sums(3)
                    for c in range(1, DC):
                        divide_by(c)
                    for c in range(DC + 1):
                        if c < DC:
                            gate_terms(c)
                        if 1 <= c <= DC:
                            high(c - 1)
                        if c < DC:
                            gated(c)
                        if 1 <= c <= DC:
                            low(c - 1)
            dve.wait_ge(next_hi, 2)
            nc.vector.tensor_tensor(swiglu_weights(wl, 0)[1], raw_o, swiglu_weights(wh, 0)[1].bitcast(fp32),
                                    ALU.subtract).then_inc(next_lo, 1)
    return sems


def stage_swiglu(nc, ins, yh, yl, wh, wl, acc, identity, zeros, sorted_x, wqh, wql, used_sems, bank):
    x, wsT, woT = ins["x"], ins["wsT"], ins["woT"]
    NE = 8
    FE = 2048 // NE
    FC = FE // P
    STEPS = 2 * NBATCH
    N_UV, N_OUT = FC * STEPS, 4 * STEPS

    with ExitStack() as held:
        def sb(name, shape, dtype):
            return held.enter_context(nc.sbuf_tensor(name, shape, dtype))

        def sem(name):
            return held.enter_context(nc.semaphore(name))

        raw_s = sb("f_raw_s", [P, DC, 2, FE], fp32)
        raw_o = sb("f_raw_o", [P, FC, D], fp32)
        sh, oh = zip(*(swiglu_weights(wh, i) for i in range(2)))
        sl, ol = zip(*(swiglu_weights(wl, i) for i in range(2)))
        silu = sb("f_silu", [P, FC, S], fp32)
        hf = [sb(f"f_h{i}", [P, FC, S], fp32) for i in range(2)]
        hh = [sb(f"f_hh{i}", [P, FC, S], fp32r) for i in range(2)]
        hl = [sb(f"f_hl{i}", [P, FC, S], fp32r) for i in range(2)]
        x_in, s_in, o_in = sem("f_x_in"), sem("f_s_in"), sem("f_o_in")
        x_doubled, zeroed, zero_filled = sem("f_x_doubled"), sem("f_zeroed"), sem("f_zero_filled")
        w_hi, w_lo = sem("f_w_hi"), sem("f_w_lo")
        uv_done, silu_done, h_done = sem("f_uv_done"), sem("f_silu_done"), sem("f_h_done")
        h_hi, h_lo = sem("f_h_hi"), sem("f_h_lo")
        out_done, added = sem("f_out_done"), sem("f_added")
        credit = [(uv_done, N_UV), (silu_done, N_UV), (h_done, N_UV), (h_hi, N_UV), (h_lo, N_UV),
                  (out_done, N_OUT), (added, N_OUT)]
        gsum = sb("f_gsum", [P, DC * H], fp32)
        wq = raw_s[:, :, :, :].rearrange("p c u f -> p c (u f)")
        q_in, q_steps, q_hi, q_lo = sem("f_q_in"), sem("f_q_steps"), sem("f_q_hi"), sem("f_q_lo")
        first = [(s_in, 16), (o_in, 16), (w_hi, 2), (w_lo, 2)]
        HALF = T // P // 2
        nc.clear_and_free_semaphores(used_sems)
        block = held.enter_context(nc.Block())

        def of(i, n, per, s, m):
            return this(i, n, per * s + m) if s >= 0 else last(i, n, per * (s + STEPS) + m)

        def passes(eng, body):
            with eng.Fori(0, NE // 2 - 1) as i:
                body(i, False)
            body(NE // 2 - 1, True)

        @block.sync
        def _(sp):
            def load(e, free):
                sp.wait_ge(w_lo, free)
                sp.dma_start(raw_s[:, :, :, :], wsT[e] if type(e) is int else
                             wsT[bass.ds(e, 1)].rearrange("o p c u f -> p (o c) u f")).then_inc(s_in, 16)
                sp.dma_start(raw_o[:, :, :], woT[e] if type(e) is int else
                             woT[bass.ds(e, 1)].rearrange("o p c f -> p (o c) f")).then_inc(o_in, 16)

            sp.dma_start(acc[:, HALF:, :], x[HALF * P:, :].rearrange("(n p) d -> p n d", p=P)).then_inc(x_in, 16)

            def body(i, final):
                for half in range(1 if final else 2):
                    load(2 * i + half + 1, 2 * (2 * i + half + 1))
            passes(sp, body)
            sp.wait_ge(w_lo, 2 * NE)
            sp.dma_start(wq, ins["wq"].rearrange("(c p) n -> p c n", p=P)).then_inc(q_in, 16)
            sp.wait_ge(zeroed, 1)
            sp.dma_start(sorted_x.rearrange("(n p) d -> p n d", p=P),
                         zeros[:, :].unsqueeze(1).broadcast_to([P, sorted_x.shape[0] // P, D])).then_inc(zero_filled, 16)
            sp.wait_ge(zero_filled, 16)

        @block.gpsimd
        def _(pool):
            for s, n in credit + first:
                pool.sem_inc(s, n)
            nc.gpsimd.memset(zeros[:, :], 0.0).then_inc(zeroed, 1)
            nc.gpsimd.memset(identity[:, :], 1.0).then_inc(zeroed, 1)
            pool.wait_ge(zeroed, 2)
            nc.gpsimd.affine_select(out=identity[:, :], in_=identity[:, :], compare_op=ALU.is_equal, fill=0.0,
                                    base=0, pattern=[[1, P]], channel_multiplier=-1).then_inc(zeroed, 1)
            for n in range(NBATCH):
                if n == NBATCH // 2:
                    pool.wait_ge(x_in, 16)
                rows = acc[:, 4 * n:4 * n + 4, :]
                nc.gpsimd.tensor_scalar(rows, rows, 2.0, None, ALU.mult).then_inc(x_doubled, 1)

        @block.tensor
        def _(pe):
            def up(i, s):
                w, b = s // NBATCH, s % NBATCH
                for c in range(FC):
                    pe.wait_ge(h_done, of(i, N_UV, FC, s - 1, c + 1))
                    for g in range(2):
                        out = bank[2 * c + g][:, :]
                        cols = slice(c * P, (c + 1) * P)
                        for kc in range(DC):
                            y_hi, y_lo = yh[:, kc, b * S:(b + 1) * S], yl[:, kc, b * S:(b + 1) * S]
                            nc.tensor.matmul(out, sh[w][:, kc, g, cols], y_lo, start=kc == 0, stop=False)
                            nc.tensor.matmul(out, sh[w][:, kc, g, cols], y_hi, start=False, stop=False)
                            mm = nc.tensor.matmul(out, sl[w][:, kc, g, cols], y_hi, start=False, stop=kc == DC - 1)
                    mm.then_inc(uv_done, 1)

            def down(i, s):
                w = s // NBATCH
                pe.wait_ge(h_lo, of(i, N_UV, FC, s, FC))
                for n in range(4):
                    pe.wait_ge(added, of(i, N_OUT, 4, s - 1, n + 1))
                    out = bank[4 + n][:, :]
                    rows = slice(n * P, (n + 1) * P)
                    for c in range(FC):
                        h_h, h_l = hh[s % 2][:, c, rows], hl[s % 2][:, c, rows]
                        nc.tensor.matmul(out, h_h, ol[w][:, c, :], start=c == 0, stop=False)
                        nc.tensor.matmul(out, h_h, oh[w][:, c, :], start=False, stop=False)
                        mm = nc.tensor.matmul(out, h_l, oh[w][:, c, :], start=False, stop=c == FC - 1)
                    mm.then_inc(out_done, 1)

            def body(i, final):
                for s in range(STEPS):
                    if s % NBATCH == 0:
                        pe.wait_ge(w_lo, 4 * i + 2 * (s // NBATCH) + 2)
                    up(i, s)
                    if s >= 1:
                        down(i, s - 1)
                down(i, STEPS - 1)
            passes(pe, body)

        def fetched(i, s, final):
            return s % NBATCH == 1 and not (final and s // NBATCH == 1)

        @block.scalar
        def _(act):
            def split_hi(e, w):
                act.wait_ge(s_in, 16 * e + 16)
                nc.scalar.activation(sh[w], raw_s[:, :, :, :], ACT.Copy).then_inc(w_hi, 1)
                act.wait_ge(o_in, 16 * e + 16)
                nc.scalar.activation(oh[w], raw_o[:, :, :], ACT.Copy).then_inc(w_hi, 1)

            def body(i, final):
                for s in range(STEPS):
                    for c in range(FC):
                        act.wait_ge(uv_done, of(i, N_UV, FC, s, c + 1))
                        act.wait_ge(h_done, of(i, N_UV, FC, s - 1, c + 1))
                        nc.scalar.activation(silu[:, c], bank[2 * c + 1][:, :], ACT.Silu).then_inc(silu_done, 1)
                    act.wait_ge(out_done, of(i, N_OUT, 4, s - 2, 4))
                    for c in range(FC):
                        act.wait_ge(h_done, of(i, N_UV, FC, s, c + 1))
                        nc.scalar.activation(hh[s % 2][:, c], hf[s % 2][:, c], ACT.Copy).then_inc(h_hi, 1)
                    if fetched(i, s, final):
                        w = s // NBATCH
                        act.wait_ge(out_done, of(i, N_OUT, 4, 4 * w - 1, 4))
                        split_hi(2 * i + w + 1, 1 - w)
                    if final and s == NBATCH + 1:
                        act.wait_ge(q_steps, 3)
                        nc.scalar.activation(wqh[:, :, :], wq, ACT.Copy).then_inc(q_hi, 1)
            passes(act, body)

        @block.vector
        def _(dve):
            def split_lo(e, w):
                dve.wait_ge(w_hi, 2 * e + 1)
                nc.vector.tensor_tensor(sl[w], raw_s[:, :, :, :], sh[w].bitcast(fp32),
                                        ALU.subtract).then_inc(w_lo, 1)
                dve.wait_ge(w_hi, 2 * e + 2)
                nc.vector.tensor_tensor(ol[w], raw_o[:, :, :], oh[w].bitcast(fp32),
                                        ALU.subtract).then_inc(w_lo, 1)

            def add(i, s):
                dve.wait_ge(x_doubled, min(s + 1, NBATCH))
                for n in range(4):
                    a = acc[:, (s % NBATCH) * 4 + n, :]
                    dve.wait_ge(out_done, of(i, N_OUT, 4, s, n + 1))
                    nc.vector.tensor_tensor(a, bank[4 + n][:, :], a, ALU.add).then_inc(added, 1)

            def centre_wq():
                columns = wq.rearrange("p c (h d) -> p (c h) d", d=HD)
                dve.wait_ge(q_in, 16)
                nc.vector.tensor_reduce(gsum[:, :], columns, AX.X, ALU.add).then_inc(q_steps, 1)
                dve.wait_ge(q_steps, 1)
                nc.vector.tensor_scalar(gsum[:, :], gsum[:, :], 1.0 / HD, None, ALU.mult).then_inc(q_steps, 1)
                dve.wait_ge(q_steps, 2)
                nc.vector.tensor_tensor(columns, columns, gsum[:, :].unsqueeze(2).broadcast_to([P, DC * H, HD]),
                                        ALU.subtract).then_inc(q_steps, 1)

            def body(i, final):
                for s in range(STEPS):
                    for c in range(FC):
                        dve.wait_ge(silu_done, of(i, N_UV, FC, s, c + 1))
                        nc.vector.tensor_tensor(hf[s % 2][:, c], bank[2 * c][:, :], silu[:, c], ALU.mult).then_inc(h_done, 1)
                    for c in range(FC):
                        dve.wait_ge(h_hi, of(i, N_UV, FC, s, c + 1))
                        nc.vector.tensor_tensor(hl[s % 2][:, c], hf[s % 2][:, c], hh[s % 2][:, c].bitcast(fp32),
                                                ALU.subtract).then_inc(h_lo, 1)
                    if fetched(i, s, final):
                        split_lo(2 * i + s // NBATCH + 1, 1 - s // NBATCH)
                    if s >= 1:
                        add(i, s - 1)
                    if final and s == NBATCH - 1:
                        centre_wq()
                    if final and s == NBATCH + 2:
                        dve.wait_ge(q_hi, 1)
                        nc.vector.tensor_tensor(wql[:, :, :], wq, wqh[:, :, :].bitcast(fp32), ALU.subtract).then_inc(q_lo, 1)
                add(i, STEPS - 1)
            passes(dve, body)


H, HD = 16, 32
HC = P // HD
KM, KD = 48, 16
KT = KM + KD
CK = 256 // P
SCALE = HD ** -0.5
EPS_HEAD = 1e-6
EPS_LN = 1e-5


def stage_cross(nc, ins, acc, logits, identity, wqh, wql, early, t_in, m_in, bank):
    PAIRS = H // 2
    NT = S // P
    NE = 32
    SPANS = [(0, KM), (KM, KT)]

    def one(i):
        return bank[i // 2][:, i % 2, :]

    with ExitStack() as held:
        def sb(name, shape, dtype=fp32):
            return held.enter_context(nc.sbuf_tensor(name, shape, dtype))

        def sem(name):
            return held.enter_context(nc.semaphore("x_" + name))

        kT = sb("x_kT", [P, DC, NBATCH * KT])
        vrows = sb("x_vrows", [P, NBATCH, D])
        head_mean, biases = sb("x_head_mean", [P, P]), sb("x_biases", [P, 6, DC])
        woh, wol = (sb("x_" + k, [P, DC, D], fp32r) for k in ("woh", "wol"))
        xb = sb("x_x", [P, NT, D])
        x2t = sb("x_x2t", [P, DC, S])
        xth, xtl = sb("x_xth", [P, DC, S], fp32r), sb("x_xtl", [P, DC, S], fp32r)
        cth, ctl = xth, xtl
        qc = sb("x_qc", [P, DC, S])
        qsq = sb("x_qsq", [P, 2, S])
        rs = sb("x_rs", [P, 2, S])
        qh, ql = (held.enter_context(nc.sbuf_tensor("x_" + k, [P, DC, S], fp32r, side="right"))
                  for k in ("qh", "ql"))
        kh, kl = sb("x_kh", [P, DC, HC, KT], fp32r), sb("x_kl", [P, DC, HC, KT], fp32r)
        vh, vl = sb("x_vh", [P, PAIRS, P], fp32r), sb("x_vl", [P, PAIRS, P], fp32r)
        pf = sb("x_p", [P, 2, H, KT])
        with nc.sbuf_tensor("x_weights", [P, 3 * DC, D], fp32) as weights:
            wk, wo, wv = (weights[:, n * DC:(n + 1) * DC, :] for n in range(3))
            wk, wv = (w.rearrange("p (n c) d -> p n c d", n=2) for w in (wk, wv))
        pth, ptl = sb("x_pth", [P, PAIRS, S], fp32r), sb("x_ptl", [P, PAIRS, S], fp32r)
        mx, den = sb("x_mx", [P, 2, H, 2]), sb("x_den", [P, 2, H, 2])
        stats, moments = sb("x_stats", [P, 2, NT, 6]), sb("x_moments", [P, 2, NT, 2])
        rstd = sb("x_rstd", [P, 2, NT])
        bo = sb("x_bo", [P, D])
        router = sb("x_router", [P, DC, NE])
        eps = sb("x_eps", [P, 2])
        kc, ksq = x2t[:, 0:2, :], x2t[:, 2:4, :]
        kc, ksq = (k.rearrange("p c (t k) -> p (c t) k", k=NBATCH * KT) for k in (kc, ksq))
        k_rstd = ksq
        ctx2 = pf[:, :, :, :].rearrange("p n (c b j) k -> p n c b (j k)", c=CK, b=NBATCH)
        ctx = sb("x_ctx", [P, CK, NBATCH, KT])
        vbias = sb("x_vbias", [P, D])
        gsum = sb("x_gsum", [P, 2, CK * H])
        bias_c = sb("x_bias_c", [P, 3, DC])
        w_in, o_in, v_in, b_in, vb_in = (sem(k) for k in ("w_in", "o_in", "v_in", "b_in", "vb_in"))
        ctx_in = sem("ctx_in")
        head_set, ctx_zeroed, placed, summed, centred = (sem(k) for k in ("head_set", "ctx_zeroed", "placed",
                                                                           "summed", "centred"))
        bias_mean, bias_done, k_proj, k_biased, k_sq, k_var, k_root, k_steps = (sem(k) for k in (
            "bias_mean", "bias_done", "k_proj", "k_biased", "k_sq", "k_var", "k_root", "k_steps"))
        v_proj, v_made, w_hi, w_lo = (sem(k) for k in ("v_proj", "v_made", "w_hi", "w_lo"))
        io_in, consts, zeroed = sem("in"), sem("consts"), sem("zeroed")
        names = dict(stat1=NT, stat1_seen=1, moment1=NT, root1=2, stat2=NT, stat2_seen=1, moment2=NT, root2=2, x1=NT, t1=DC, x1_hi=DC, x1_lo=DC, k_hi=HC, k_lo=HC,
                     v_hi=4, v_lo=4, q=DC, q_b=DC, q_sq=DC, var=DC, q_root=2 * DC, q_n=DC, q_aff=DC, q_hi=DC,
                     q_lo=DC, sc=NT, mx=2 * NT, sub=2 * NT, ex=NT, sm=2 * NT, rc=NT, nm=2 * NT, pt=NT,
                     p_hi=NT, p_lo=NT, pv=DC, c_hi=DC, c_lo=DC, bo=NT, wo=NT, res=NT, res_seen=1, x2=NT, kept=NT,
                     t2=DC, xt=DC, lg=1, lg_out=1)
        s = {k: sem(k) for k in names}
        block = held.enter_context(nc.Block())

        def at(b, name, m):
            return this(b, names[name], m)

        def before(b, name):
            return last(b, names[name], names[name])

        HALVES = [(half, j) for half in range(2) for j in range(2)]

        def values_at(t, half, j):
            g = 2 * j + half
            return t[half * KT:(half + 1) * KT, j::2, g * HD:(g + 1) * HD]

        def values_of(b, half, j):
            v = vrows[half * KT:(half + 1) * KT, bass.ds(b, 1), :]
            return v.rearrange("p o (c g d) -> p (o c) g d", g=HC, d=HD)[:, :, 2 * j + half, :]

        def keys_of(b, h):
            return kT[h * HD:(h + 1) * HD, :, bass.ds(b * KT, KT)]

        def rows_of(b, n):
            return acc[:, bass.ds(b * NT + n, 1), :].rearrange("p o d -> p (o d)")

        @block.sync
        def _(sp):
            sp.dma_start(ctx[:, :, :, :], ins["ctxT"].rearrange("(c p) b k -> p c b k", p=P)).then_inc(ctx_in, 16)
            for n, name in enumerate(("wk_main", "wk_last")):
                sp.dma_start(wk[:, n], ins[name].rearrange("(c p) n -> p c n", p=P)).then_inc(w_in, 16)
            for n, name in enumerate(("wv_main", "wv_last")):
                sp.dma_start(wv[:, n], ins[name].rearrange("(c p) n -> p c n", p=P)).then_inc(v_in, 16)
            sp.dma_start(wo, ins["wo"].rearrange("(c p) n -> p c n", p=P)).then_inc(o_in, 16)
            sp.dma_start(bo[:, :], ins["bo"].broadcast_to([P, D])).then_inc(io_in, 16)
            sp.dma_start(router[:, :, :], ins["routerT"].rearrange("(c p) e -> p c e", p=P)).then_inc(io_in, 16)
            sp.wait_ge(s["q"], at(NBATCH - 1, "q", DC))
            sp.dma_start(early[:, 3], ins["w_ffnT"].rearrange("(c p) n -> p c n", p=P)).then_inc(t_in, 16)
            for e in range(len(m_in)):
                if e == 1:
                    sp.wait_ge(s["sc"], at(NBATCH - 1, "sc", NT))
                sp.dma_start(early[:, 2 - e], ins["maskT"][e].rearrange("(c p) n -> p c n", p=P)).then_inc(m_in[e], 16)

        @block.gpsimd
        def _(pool):
            nc.gpsimd.memset(ctx2, 0.0).then_inc(ctx_zeroed, 1)
            nc.gpsimd.memset(head_mean[:, :], 0.0).then_inc(head_set, 1)
            nc.gpsimd.memset(eps[:, 0:1], EPS_LN).then_inc(consts, 1)
            nc.gpsimd.memset(eps[:, 1:2], EPS_HEAD).then_inc(consts, 1)
            for name, n in names.items():
                pool.sem_inc(s[name], n)
            for h in range(HC):
                rows = slice(h * HD, (h + 1) * HD)
                pool.wait_ge(head_set, 1 + h)
                nc.gpsimd.memset(head_mean[rows, rows], 1.0 / HD).then_inc(head_set, 1)
            pool.wait_ge(ctx_zeroed, 1)
            pool.wait_ge(head_set, 1 + HC)
            pool.wait_ge(ctx_in, 16)
            for n, (a, z) in enumerate(SPANS):
                for copy in range(2):
                    nc.gpsimd.tensor_copy(ctx2[:, n, :, :, copy * KT + a:copy * KT + z], ctx[:, :, :, a:z]).then_inc(placed, 1)
            for t in (kh, kl):
                nc.gpsimd.memset(t[:, :, :, :].bitcast(fp32), 0.0).then_inc(zeroed, 1)
            for t in (vh, vl):
                nc.gpsimd.memset(t[:, :, :].bitcast(fp32), 0.0).then_inc(zeroed, 1)
            pool.wait_ge(io_in, 32)

            def step(f, g):
                if f is not None:
                    for n in range(NT):
                        pool.wait_ge(s["x1"], at(f, "x1", n + 1))
                        nc.gpsimd.tensor_tensor(rows_of(f, n), xb[:, n], bo[:, :], ALU.add).then_inc(s["bo"], 1)
                for c in range(DC + 1):
                    if c == DC // 2 and g is not None:
                        for n in range(NT):
                            pool.wait_ge(s["x2"], at(g, "x2", n + 1))
                            nc.gpsimd.tensor_copy(rows_of(g, n), xb[:, n]).then_inc(s["kept"], 1)
                    if c < DC and f is not None:
                        pool.wait_ge(s["q_root"], at(f, "q_root", 2 * c + 2))
                        nc.gpsimd.tensor_tensor(qc[:, c], qc[:, c], rs[:, c % 2], ALU.mult).then_inc(s["q_n"], 1)

            step(0, None)
            step(1, None)
            with pool.Fori(0, NBATCH - 2) as i:
                step(i + 2, i)
            step(None, NBATCH - 2)
            step(None, NBATCH - 1)

        def steps(eng, front0, step, tail):
            front0(0)
            step(0, True, False)
            with eng.Fori(0, NBATCH - 2) as i:
                step(i + 1, True, True)
            step(NBATCH - 1, False, True)
            tail(NBATCH - 1)

        @block.scalar
        def _(act):
            nc.scalar.preload_act_table_set("natural_log_exp_and_others")
            act.wait_ge(consts, 2)

            def roots(b, m):
                root, moment = f"root{m}", f"moment{m}"
                act.wait_ge(s[moment], at(b, moment, NT))
                nc.scalar.activation(rstd[:, m - 1, :], moments[:, m - 1, :, 1], ACT.Ln, bias=eps[:, 0:1]).then_inc(s[root], 1)
                act.wait_ge(s[root], at(b, root, 1))
                nc.scalar.activation(rstd[:, m - 1, :], rstd[:, m - 1, :], ACT.Exp, scale=-0.5).then_inc(s[root], 1)

            def x1_hi(f):
                for c in range(DC):
                    act.wait_ge(s["t1"], at(f, "t1", c + 1))
                    nc.scalar.activation(xth[:, c], one(4 + c), ACT.Copy).then_inc(s["x1_hi"], 1)

            def q_of(f, c):
                if c == 0:
                    act.wait_ge(s["q_lo"], before(f, "q_lo"))
                act.wait_ge(s["q"], at(f, "q", c + 1))
                nc.scalar.activation(qc[:, c], one(4 + c % 2), ACT.Identity, bias=biases[:, 0, c:c + 1]).then_inc(s["q_b"], 1)
                nc.scalar.activation(qsq[:, c % 2], one(4 + c % 2), ACT.Square, bias=biases[:, 0, c:c + 1]).then_inc(s["q_sq"], 1)

            def q_root(f, c):
                act.wait_ge(s["var"], at(f, "var", c + 1))
                if c >= 2:
                    act.wait_ge(s["q_n"], at(f, "q_n", c - 1))
                nc.scalar.activation(rs[:, c % 2], one(6 + c % 2), ACT.Ln, bias=eps[:, 1:2]).then_inc(s["q_root"], 1)
                act.wait_ge(s["q_root"], at(f, "q_root", 2 * c + 1))
                nc.scalar.activation(rs[:, c % 2], rs[:, c % 2], ACT.Exp, scale=-0.5).then_inc(s["q_root"], 1)

            def q_affine(f, c):
                act.wait_ge(s["q_n"], at(f, "q_n", c + 1))
                nc.scalar.activation(qc[:, c], qc[:, c], ACT.Identity, scale=biases[:, 5, 0:1],
                                     bias=biases[:, 5, 1:2]).then_inc(s["q_aff"], 1)

            def q_hi(f, c):
                act.wait_ge(s["q_aff"], at(f, "q_aff", c + 1))
                nc.scalar.activation(qh[:, c], qc[:, c], ACT.Copy).then_inc(s["q_hi"], 1)

            def k_hi(f):
                act.wait_ge(s["sc"], before(f, "sc"))
                act.wait_ge(zeroed, 4)
                for h in range(HC):
                    nc.scalar.activation(kh[h * HD:(h + 1) * HD, :, h, :], keys_of(f, h), ACT.Copy).then_inc(s["k_hi"], 1)

            def v_hi(f):
                act.wait_ge(s["pv"], before(f, "pv"))
                act.wait_ge(consts, 2)
                for half, j in HALVES:
                    nc.scalar.activation(values_at(vh, half, j), values_of(f, half, j), ACT.Copy).then_inc(s["v_hi"], 1)

            def exps(b, n):
                act.wait_ge(s["sub"], at(b, "sub", 2 * n + 2))
                nc.scalar.activation(pf[:, n % 2], pf[:, n % 2], ACT.Exp).then_inc(s["ex"], 1)

            def p_hi(b, n):
                act.wait_ge(s["pt"], at(b, "pt", n + 1))
                nc.scalar.activation(pth[:, :, n * P:(n + 1) * P], bank[1][:, :, :].rearrange(
                    "p a (j t) -> p (a j) t", t=P), ACT.Copy).then_inc(s["p_hi"], 1)

            def xt(g, half):
                if half == 0:
                    act.wait_ge(s["lg"], before(g, "lg"))
                for c in (2 * half, 2 * half + 1):
                    act.wait_ge(s["t2"], at(g, "t2", c + 1))
                    nc.scalar.activation(x2t[:, c], one(6 + c % 2), ACT.Copy).then_inc(s["xt"], 1)

            def c_hi(g):
                for c in range(DC):
                    act.wait_ge(s["pv"], at(g, "pv", c + 1))
                    nc.scalar.activation(cth[:, c], one(c), ACT.Copy).then_inc(s["c_hi"], 1)

            def front0(f):
                act.dma_start(biases[:, :, :], ins["biases"]).then_inc(b_in, 16)
                for copy in range(2):
                    for n, (a, z) in enumerate(SPANS):
                        act.dma_start(vbias[copy * KT + a:copy * KT + z, :],
                                      ins["bv"][:, n].broadcast_to([z - a, D])).then_inc(vb_in, 16)
                roots(f, 1)
                x1_hi(f)
                act.wait_ge(o_in, 16)
                nc.scalar.activation(woh[:, :, :], wo, ACT.Copy).then_inc(w_hi, 1)
                act.wait_ge(bias_done, 2)
                q_of(f, 0)
                q_of(f, 1)
                q_root(f, 0)
                for c in range(DC):
                    act.wait_ge(k_biased, 2 * c + 2)
                    nc.scalar.activation(ksq[:, c], kc[:, c], ACT.Square).then_inc(k_sq, 1)
                q_of(f, 2)
                q_root(f, 1)
                for c in range(DC):
                    act.wait_ge(k_var, c + 1)
                    nc.scalar.activation(k_rstd[:, c], one(2 + c % 2)[:, 0:NBATCH * KT], ACT.Ln,
                                         bias=eps[:, 1:2]).then_inc(k_root, 1)
                act.wait_ge(k_root, DC)
                nc.scalar.activation(k_rstd, k_rstd, ACT.Exp, scale=-0.5).then_inc(k_root, 1)
                q_affine(f, 0)
                q_affine(f, 1)
                q_of(f, 3)
                q_root(f, 2)
                q_hi(f, 0)
                q_hi(f, 1)
                q_root(f, 3)
                act.wait_ge(k_steps, 4)
                k_hi(f)
                for c in (2, 3):
                    q_affine(f, c)
                    q_hi(f, c)

            def step(b, front, tail):
                f, g = b + 1, b - 1
                if tail:
                    c_hi(g)
                exps(b, 0)
                if front:
                    roots(f, 1)
                v_hi(b)
                p_hi(b, 0)
                if front:
                    x1_hi(f)
                exps(b, 1)
                if front:
                    q_of(f, 0)
                    q_of(f, 1)
                exps(b, 2)
                p_hi(b, 1)
                if front:
                    q_root(f, 0)
                if tail:
                    roots(g, 2)
                if front:
                    q_of(f, 2)
                    q_root(f, 1)
                p_hi(b, 2)
                exps(b, 3)
                if tail:
                    xt(g, 0)
                if front:
                    q_of(f, 3)
                if tail:
                    xt(g, 1)
                if front:
                    q_affine(f, 0)
                    q_affine(f, 1)
                    k_hi(f)
                p_hi(b, 3)
                if front:
                    q_hi(f, 0)
                    q_root(f, 2)
                    q_hi(f, 1)
                    q_root(f, 3)
                    for c in (2, 3):
                        q_affine(f, c)
                        q_hi(f, c)

            def last_tail(g):
                c_hi(g)
                roots(g, 2)
                xt(g, 0)
                xt(g, 1)
            steps(act, front0, step, last_tail)

        @block.vector
        def _(dve):
            dve.wait_ge(consts, 2)

            def moments_of(b, m):
                for n in range(NT):
                    nc.vector.bn_stats(stats[:, m - 1, n], rows_of(b, n)).then_inc(s[f"stat{m}"], 1)
                dve.wait_ge(s[f"stat{m}"], at(b, f"stat{m}", NT))
                dve.sem_inc(s[f"stat{m}_seen"], 1)
                for n in range(NT):
                    dve.wait_ge(consts, 2)
                    nc.vector.bn_aggr(moments[:, m - 1, n], stats[:, m - 1, n]).then_inc(s[f"moment{m}"], 1)

            def normed(b, m):
                dve.wait_ge(s[f"root{m}"], at(b, f"root{m}", 2))
                for n in range(NT):
                    nc.vector.tensor_scalar(xb[:, n], rows_of(b, n), moments[:, m - 1, n, 0:1],
                                            rstd[:, m - 1, n:n + 1], ALU.subtract, ALU.mult).then_inc(s[f"x{m}"], 1)

            def first_moments(f):
                dve.wait_ge(s["x1"], before(f, "x1"))
                dve.wait_ge(consts, 2)
                moments_of(f, 1)

            def second_moments(g):
                dve.wait_ge(s["x2"], before(g, "x2"))
                dve.wait_ge(s["res"], at(g, "res", NT))
                dve.sem_inc(s["res_seen"], 1)
                dve.wait_ge(consts, 2)
                moments_of(g, 2)

            def first_normed(f, tail):
                if tail:
                    dve.wait_ge(s["t2"], before(f - 2, "t2"))
                    dve.wait_ge(s["kept"], before(f - 2, "kept"))
                dve.wait_ge(s["t1"], before(f, "t1"))
                dve.wait_ge(s["bo"], before(f, "bo"))
                normed(f, 1)

            def second_normed(g, front):
                dve.wait_ge(s["t2"], before(g, "t2"))
                dve.wait_ge(s["kept"], before(g, "kept"))
                if front:
                    dve.wait_ge(s["t1"], at(g + 2, "t1", DC))
                    dve.wait_ge(s["bo"], at(g + 2, "bo", NT))
                normed(g, 2)

            def k_lo(f):
                for h in range(HC):
                    dve.wait_ge(s["k_hi"], at(f, "k_hi", h + 1))
                    nc.vector.tensor_tensor(kl[h * HD:(h + 1) * HD, :, h, :], keys_of(f, h),
                                            kh[h * HD:(h + 1) * HD, :, h, :].bitcast(fp32), ALU.subtract).then_inc(s["k_lo"], 1)

            def v_lo(f):
                for n, (half, j) in enumerate(HALVES):
                    dve.wait_ge(s["v_hi"], at(f, "v_hi", n + 1))
                    nc.vector.tensor_tensor(values_at(vl, half, j), values_of(f, half, j),
                                            values_at(vh, half, j).bitcast(fp32), ALU.subtract).then_inc(s["v_lo"], 1)

            def x1_lo(f):
                for c in range(DC):
                    dve.wait_ge(s["x1_hi"], at(f, "x1_hi", c + 1))
                    nc.vector.tensor_tensor(xtl[:, c], one(4 + c), xth[:, c].bitcast(fp32), ALU.subtract).then_inc(s["x1_lo"], 1)

            def q_lo(f, c):
                dve.wait_ge(s["q_hi"], at(f, "q_hi", c + 1))
                nc.vector.tensor_tensor(ql[:, c], qc[:, c], qh[:, c].bitcast(fp32), ALU.subtract).then_inc(s["q_lo"], 1)

            scores = bank[0][:, :, :].rearrange("p a (h k) -> p (a h) k", k=KT)

            def minus_max(b, n):
                if n >= 2:
                    dve.wait_ge(s["pt"], at(b, "pt", n - 1))
                dve.wait_ge(s["sc"], at(b, "sc", n + 1))
                for i, (a, z) in enumerate(SPANS):
                    nc.vector.tensor_reduce(mx[:, n % 2, :, i], scores[:, :, a:z], AX.X, ALU.max).then_inc(s["mx"], 1)
                for i, (a, z) in enumerate(SPANS):
                    dve.wait_ge(s["mx"], at(b, "mx", 2 * n + i + 1))
                    nc.vector.tensor_tensor(pf[:, n % 2, :, a:z], scores[:, :, a:z],
                                            mx[:, n % 2, :, i:i + 1].broadcast_to([P, H, z - a]),
                                            ALU.subtract).then_inc(s["sub"], 1)

            def normalise(b, n):
                dve.wait_ge(s["ex"], at(b, "ex", n + 1))
                for i, (a, z) in enumerate(SPANS):
                    nc.vector.tensor_reduce(den[:, n % 2, :, i], pf[:, n % 2, :, a:z], AX.X, ALU.add).then_inc(s["sm"], 1)
                dve.wait_ge(s["sm"], at(b, "sm", 2 * n + 2))
                nc.vector.reciprocal(den[:, n % 2], den[:, n % 2]).then_inc(s["rc"], 1)
                dve.wait_ge(s["rc"], at(b, "rc", n + 1))
                for i, (a, z) in enumerate(SPANS):
                    nc.vector.tensor_tensor(pf[:, n % 2, :, a:z], pf[:, n % 2, :, a:z],
                                            den[:, n % 2, :, i:i + 1].broadcast_to([P, H, z - a]),
                                            ALU.mult).then_inc(s["nm"], 1)

            def p_lo(b, n):
                dve.wait_ge(s["p_hi"], at(b, "p_hi", n + 1))
                nc.vector.tensor_tensor(ptl[:, :, n * P:(n + 1) * P], bank[1][:, :, :].rearrange(
                    "p a (j t) -> p (a j) t", t=P), pth[:, :, n * P:(n + 1) * P].bitcast(fp32),
                    ALU.subtract).then_inc(s["p_lo"], 1)

            def logits_of(g):
                dve.wait_ge(s["lg"], at(g, "lg", 1))
                nc.vector.tensor_copy(logits[:, bass.ds(g * NT, NT), :],
                                      one(4)[:, 0:NT * NE].rearrange("p (n e) -> p n e", e=NE)).then_inc(s["lg_out"], 1)

            def c_lo(g):
                for c in range(DC):
                    dve.wait_ge(s["c_hi"], at(g, "c_hi", c + 1))
                    nc.vector.tensor_tensor(ctl[:, c], one(c), cth[:, c].bitcast(fp32), ALU.subtract).then_inc(s["c_lo"], 1)

            def residual(g):
                dve.wait_ge(s["bo"], at(g, "bo", NT))
                for n in range(NT):
                    dve.wait_ge(s["wo"], at(g, "wo", n + 1))
                    nc.vector.tensor_tensor(rows_of(g, n), one(4 + n), rows_of(g, n), ALU.add).then_inc(s["res"], 1)

            def residual_and_moments(g):
                dve.wait_ge(s["x2"], before(g, "x2"))
                dve.wait_ge(s["bo"], at(g, "bo", NT))
                for n in range(NT):
                    dve.wait_ge(s["wo"], at(g, "wo", n + 1))
                    nc.vector.tensor_tensor(rows_of(g, n), one(4 + n), rows_of(g, n), ALU.add).then_inc(s["res"], 1)
                    dve.wait_ge(s["res"], at(g, "res", n + 1))
                    nc.vector.bn_stats(stats[:, 1, n], rows_of(g, n)).then_inc(s["stat2"], 1)
                    dve.wait_ge(s["stat2"], at(g, "stat2", n + 1))
                    nc.vector.bn_aggr(moments[:, 1, n], stats[:, 1, n]).then_inc(s["moment2"], 1)

            def head_sums(n, w):
                g = gsum[:, n, 0:w.shape[1] * H]
                nc.vector.tensor_reduce(g, w.rearrange("p c (h d) -> p (c h) d", d=HD), AX.X, ALU.add).then_inc(summed, 1)
                dve.wait_ge(summed, 2 * n + 1)
                nc.vector.tensor_scalar(g, g, 1.0 / HD, None, ALU.mult).then_inc(summed, 1)

            def centre(n, w):
                v = w.rearrange("p c (h d) -> p (c h) d", d=HD)
                dve.wait_ge(summed, 2 * n + 2)
                nc.vector.tensor_tensor(v, v, gsum[:, n, 0:w.shape[1] * H].unsqueeze(2).broadcast_to(
                    [P, w.shape[1] * H, HD]), ALU.subtract).then_inc(centred, 1)

            def keys():
                for c in range(DC):
                    src = one(c % 2)[:, 0:NBATCH * KT].rearrange("p (b k) -> p b k", k=KT)
                    dst = kc[:, c].rearrange("p (b k) -> p b k", k=KT)
                    dve.wait_ge(k_proj, c + 1)
                    for n, (a, z) in enumerate(SPANS):
                        nc.vector.tensor_scalar(dst[:, :, a:z], src[:, :, a:z], bias_c[:, 1 + n, c:c + 1], None,
                                                ALU.add).then_inc(k_biased, 1)

            def keys_normed():
                dve.wait_ge(k_root, DC + 1)
                dve.wait_ge(k_biased, 2 * DC)
                nc.vector.tensor_tensor(kc, kc, k_rstd, ALU.mult).then_inc(k_steps, 1)
                dve.wait_ge(k_steps, 1)
                src = kc.rearrange("p c (b k) -> p (c b) k", k=KT)
                dst = kT[:, :, :].rearrange("p c (b k) -> p (c b) k", k=KT)
                for n, (a, z) in enumerate(SPANS):
                    nc.vector.tensor_scalar(dst[:, :, a:z], src[:, :, a:z], biases[:, 3 + n, 0:1],
                                            biases[:, 3 + n, 1:2], ALU.mult, ALU.add).then_inc(k_steps, 1)
                dve.wait_ge(k_steps, 3)
                nc.vector.tensor_scalar(kT[:, :, :], kT[:, :, :], SCALE, None, ALU.mult).then_inc(k_steps, 1)

            def values_made(b):
                dve.wait_ge(v_proj, b + 1)
                nc.vector.tensor_tensor(vrows[:, b], one(b % 2), vbias[:, :], ALU.add).then_inc(v_made, 1)

            def front0(f):
                first_moments(f)
                normed(f, 1)
                dve.wait_ge(w_in, 32)
                for n in range(2):
                    head_sums(n, wk[:, n])
                for n in range(2):
                    centre(n, wk[:, n])
                x1_lo(f)
                dve.wait_ge(bias_mean, 1)
                nc.vector.tensor_tensor(bias_c[:, :, :], biases[:, 0:3, :], one(3)[:, 0:3 * DC].rearrange(
                    "p (n c) -> p n c", n=3), ALU.subtract).then_inc(bias_done, 1)
                dve.wait_ge(bias_done, 1)
                nc.vector.tensor_copy(biases[:, 0, :], bias_c[:, 0, :]).then_inc(bias_done, 1)
                dve.wait_ge(vb_in, 64)
                values_made(0)
                values_made(1)
                dve.wait_ge(w_hi, 1)
                nc.vector.tensor_tensor(wol[:, :, :], wo, woh[:, :, :].bitcast(fp32), ALU.subtract).then_inc(w_lo, 1)
                keys()
                keys_normed()
                q_lo(f, 0)
                q_lo(f, 1)
                values_made(2)
                k_lo(f)
                q_lo(f, 2)
                q_lo(f, 3)
                values_made(3)

            def step(b, front, tail):
                f, g = b + 1, b - 1
                if tail:
                    c_lo(g)
                minus_max(b, 0)
                if front:
                    first_moments(f)
                normalise(b, 0)
                if front:
                    first_normed(f, tail)
                if tail:
                    residual(g)
                v_lo(b)
                minus_max(b, 1)
                if front:
                    x1_lo(f)
                p_lo(b, 0)
                normalise(b, 1)
                minus_max(b, 2)
                if tail:
                    second_moments(g)
                p_lo(b, 1)
                normalise(b, 2)
                if tail:
                    second_normed(g, front)
                minus_max(b, 3)
                p_lo(b, 2)
                normalise(b, 3)
                if front:
                    k_lo(f)
                p_lo(b, 3)
                if front:
                    for c in range(DC):
                        q_lo(f, c)
                if tail:
                    logits_of(g)

            def last_tail(g):
                c_lo(g)
                residual_and_moments(g)
                second_normed(g, False)
                logits_of(g)
            steps(dve, front0, step, last_tail)

        @block.tensor
        def _(pe):
            def product(out, lh, ll, rh, rl, first, stop):
                nc.tensor.matmul(out, lh, rl, start=first, stop=False)
                nc.tensor.matmul(out, lh, rh, start=False, stop=False)
                return nc.tensor.matmul(out, ll, rh, start=False, stop=stop)

            pe.wait_ge(consts, 2)

            def transposed(c, out, name):
                for n in range(NT):
                    mm = nc.tensor.transpose(out[:, n * P:(n + 1) * P], xb[:, n, c * P:(c + 1) * P], identity[:, :])
                mm.then_inc(s[name], 1)

            def t1(f, tail):
                pe.wait_ge(s["x1"], at(f, "x1", NT))
                if tail:
                    pe.wait_ge(s["res"], at(f - 2, "res", NT))
                for c in range(DC):
                    transposed(c, one(4 + c), "t1")

            def t2(g, half):
                if half == 0:
                    pe.wait_ge(s["x2"], at(g, "x2", NT))
                else:
                    pe.wait_ge(s["xt"], at(g, "xt", 2))
                for c in (2 * half, 2 * half + 1):
                    transposed(c, one(6 + c % 2), "t2")

            def project(f, c):
                if c >= 2:
                    pe.wait_ge(s["q_sq"], at(f, "q_sq", c - 1))
                for kc in range(DC):
                    cols = slice(c * P, (c + 1) * P)
                    mm = product(one(4 + c % 2), wqh[:, kc, cols], wql[:, kc, cols], xth[:, kc], xtl[:, kc],
                                 kc == 0, kc == DC - 1)
                mm.then_inc(s["q"], 1)

            def variance(f, c):
                pe.wait_ge(s["q_sq"], at(f, "q_sq", c + 1))
                if c >= 2:
                    pe.wait_ge(s["q_root"], at(f, "q_root", 2 * c - 3))
                nc.tensor.matmul(one(6 + c % 2), head_mean[:, :], qsq[:, c % 2], start=True, stop=True).then_inc(s["var"], 1)

            def scores(b, n):
                if n == 0:
                    pe.wait_ge(s["k_lo"], at(b, "k_lo", HC))
                    pe.wait_ge(s["q_lo"], at(b, "q_lo", DC))
                else:
                    pe.wait_ge(s["sub"], at(b, "sub", 2 * n))
                for c in range(DC):
                    toks = slice(n * P, (n + 1) * P)
                    out = bank[0][:, c // 2, (c % 2) * HC * KT:(c % 2 + 1) * HC * KT]
                    keys = [k[:, c].rearrange("p h k -> p (h k)") for k in (kh, kl)]
                    mm = product(out, qh[:, c, toks], ql[:, c, toks], *keys, True, True)
                mm.then_inc(s["sc"], 1)

            def turn(b, n):
                pe.wait_ge(s["nm"], at(b, "nm", 2 * n + 2))
                if n >= 1:
                    pe.wait_ge(s["p_lo"], at(b, "p_lo", n))
                for j in range(PAIRS):
                    mm = nc.tensor.transpose(bank[1][:, j // 4, (j % 4) * P:(j % 4 + 1) * P],
                                             pf[:, n % 2, 2 * j:2 * j + 2, :].rearrange("p h k -> p (h k)"), identity[:, :])
                mm.then_inc(s["pt"], 1)

            def logits_of(g):
                pe.wait_ge(io_in, 32)
                pe.wait_ge(s["xt"], at(g, "xt", DC))
                for n in range(NT):
                    for c in range(DC):
                        mm = nc.tensor.matmul(one(4)[:, n * NE:(n + 1) * NE], x2t[:, c, n * P:(n + 1) * P], router[:, c],
                                              start=c == 0, stop=c == DC - 1)
                mm.then_inc(s["lg"], 1)

            def values(g):
                pe.wait_ge(s["v_lo"], at(g, "v_lo", 4))
                pe.wait_ge(s["p_lo"], at(g, "p_lo", NT))
                for c in range(DC):
                    for j in (2 * c, 2 * c + 1):
                        mm = product(one(c), vh[:, j], vl[:, j], pth[:, j], ptl[:, j], j == 2 * c, j == 2 * c + 1)
                    mm.then_inc(s["pv"], 1)
                pe.wait_ge(s["c_lo"], at(g, "c_lo", DC))

            def out_of(g):
                pe.wait_ge(s["lg_out"], before(g, "lg_out"))
                for n in range(NT):
                    for c in range(DC):
                        toks = slice(n * P, (n + 1) * P)
                        mm = product(one(4 + n), cth[:, c, toks], ctl[:, c, toks], woh[:, c], wol[:, c],
                                     c == 0, c == DC - 1)
                    mm.then_inc(s["wo"], 1)

            def keys():
                for c in range(DC):
                    out = one(c % 2)[:, 0:NBATCH * KT].rearrange("p (b k) -> p b k", k=KT)
                    for n, (a, z) in enumerate(SPANS):
                        pe.wait_ge(centred, n + 1)
                        if c >= 2:
                            pe.wait_ge(k_biased, 2 * (c - 1))
                        for i in range(CK):
                            mm = nc.tensor.matmul(out[:, :, a:z], wk[:, n, i, c * P:(c + 1) * P], ctx[:, i, :, a:z],
                                                  start=i == 0, stop=i == CK - 1)
                    mm.then_inc(k_proj, 1)

            def key_variances():
                for c in range(DC):
                    pe.wait_ge(k_sq, c + 1)
                    if c >= 2:
                        pe.wait_ge(k_root, c - 1)
                    nc.tensor.matmul(one(2 + c % 2)[:, 0:NBATCH * KT], head_mean[:, :], ksq[:, c],
                                     start=True, stop=True).then_inc(k_var, 1)

            def values_of_batch(b):
                if b >= 2:
                    pe.wait_ge(v_made, b - 1)
                for n in range(2):
                    for i in range(CK):
                        mm = nc.tensor.matmul(one(b % 2), ctx2[:, n, i, b], wv[:, n, i],
                                              start=n == 0 and i == 0, stop=n == 1 and i == CK - 1)
                mm.then_inc(v_proj, 1)

            def front0(f):
                pe.wait_ge(head_set, 1 + HC)
                pe.wait_ge(b_in, 16)
                nc.tensor.matmul(one(3)[:, 0:3 * DC], head_mean[:, :], biases[:, 0:3, :].rearrange("p n c -> p (n c)"),
                                 start=True, stop=True).then_inc(bias_mean, 1)
                t1(f, False)
                pe.wait_ge(placed, 4)
                pe.wait_ge(v_in, 32)
                values_of_batch(0)
                values_of_batch(1)
                pe.wait_ge(s["x1_lo"], at(f, "x1_lo", DC))
                project(f, 0)
                project(f, 1)
                variance(f, 0)
                pe.wait_ge(v_made, 2)
                keys()
                project(f, 2)
                variance(f, 1)
                pe.wait_ge(bias_done, 1)
                key_variances()
                pe.wait_ge(k_biased, 2 * DC)
                values_of_batch(2)
                project(f, 3)
                variance(f, 2)
                variance(f, 3)
                values_of_batch(3)
                pe.wait_ge(v_made, NBATCH)
                pe.wait_ge(k_biased, 2 * DC)
                pe.wait_ge(k_root, DC + 1)
                pe.wait_ge(w_lo, 1)

            def step(b, front, tail):
                f, g = b + 1, b - 1
                pe.wait_ge(s["q_root"], at(b, "q_root", 2 * DC - 1))
                if tail:
                    values(g)
                scores(b, 0)
                if tail:
                    out_of(g)
                scores(b, 1)
                turn(b, 0)
                if front:
                    t1(f, tail)
                scores(b, 2)
                if front:
                    pe.wait_ge(s["x1_lo"], at(f, "x1_lo", DC))
                    project(f, 0)
                    project(f, 1)
                turn(b, 1)
                scores(b, 3)
                if front:
                    variance(f, 0)
                    project(f, 2)
                    variance(f, 1)
                turn(b, 2)
                if front:
                    project(f, 3)
                    pe.wait_ge(s["q_root"], at(f, "q_root", 3))
                if tail:
                    t2(g, 0)
                    t2(g, 1)
                turn(b, 3)
                if tail:
                    pe.wait_ge(s["xt"], at(g, "xt", DC))
                if front:
                    variance(f, 2)
                    variance(f, 3)
                if tail:
                    logits_of(g)

            def last_tail(g):
                values(g)
                out_of(g)
                t2(g, 0)
                t2(g, 1)
                logits_of(g)
            steps(pe, front0, step, last_tail)


NE = 32
NT = T // P
NOVER = NT - 1
NSLOT = NE + NOVER


def stage_experts(nc, ins, acc, logits, identity, pos, top, tile_expert, sorted_x, sorted_y, early, t_in, early_in,
                  bank):
    with ExitStack() as held:
        routed = held.enter_context(nc.semaphore("routed"))
        scattered = held.enter_context(nc.semaphore("scattered"))
        block = held.enter_context(nc.Block())
        route(nc, held, block, acc, logits, pos, top, tile_expert, sorted_x, routed, scattered, bank)
        multiply(nc, held, block, ins, tile_expert, identity, sorted_x, sorted_y, routed, scattered, early, t_in,
                 early_in, bank)


def route(nc, held, block, acc, logits, pos, top, tile_expert, sorted_x, routed, scattered, bank):
    def sb(name, shape, dtype=fp32):
        return held.enter_context(nc.sbuf_tensor("r_" + name, shape, dtype))

    def sem(name):
        return held.enter_context(nc.semaphore("r_" + name))

    mx, den, best = sb("mx", [P, NT]), sb("den", [P, NT]), sb("best", [P, NT])
    ex = sb("ex", [P, NT, NE])
    eq = sb("eq", [P, NT, NE])
    onehot = sb("onehot", [P, NT, NE])
    onehot_b = sb("onehot_b", [P, NT, NE], bf16)
    below = sb("below", [P, P], bf16)
    ones = sb("ones", [P, P], bf16)
    rev = sb("rev", [P, NE])
    marks = sb("marks", [P, NT])
    steps = sb("steps", [P, NOVER])
    ranks, bases = sb("ranks", [P, NT, NE]), sb("bases", [P, NT, NE])
    over = sb("over", [P, NE, NT])
    tiles, end, base = sb("tiles", [P, NE]), sb("end", [P, NE]), sb("base", [P, NE])
    done = sb("done", [P, NOVER, NE])
    expert_f = sb("expert_f", [P, NOVER])
    rank, own, beyond, first = (sb(k, [P, NT]) for k in ("rank", "own", "beyond", "first"))
    consts, steps_done, exps, counted, placed = (sem("consts"), sem("steps"), sem("exps"), sem("counted"),
                                                 sem("placed"))
    N_CONST = 7

    @block.gpsimd
    def _(pool):
        nc.gpsimd.memset(ones[:, :], 1.0).then_inc(consts, 1)
        nc.gpsimd.memset(below[:, :], 1.0).then_inc(consts, 1)
        nc.gpsimd.iota(rev[:, :], pattern=[[-1, NE]], base=NE, channel_multiplier=0,
                       allow_small_or_imprecise_dtypes=True).then_inc(consts, 1)
        nc.gpsimd.iota(marks[:, :], pattern=[[P, NT]], base=0, channel_multiplier=0,
                       allow_small_or_imprecise_dtypes=True).then_inc(consts, 1)
        nc.gpsimd.iota(steps[:, :], pattern=[[1, NOVER]], base=0, channel_multiplier=0,
                       allow_small_or_imprecise_dtypes=True).then_inc(consts, 1)
        pool.wait_ge(consts, 5)
        nc.gpsimd.affine_select(out=below[:, :], in_=below[:, :], compare_op=ALU.is_gt, fill=0.0, base=0,
                                pattern=[[1, P]], channel_multiplier=-1).then_inc(consts, 2)
        pool.wait_ge(routed, 1)
        for n in range(NT):
            nc.gpsimd.indirect_dma_start(
                out=sorted_x, out_offset=bass.IndirectOffsetOnAxis(ap=pos[:, n:n + 1], axis=0),
                in_=acc[:, n, :], in_offset=None).then_inc(scattered, 16)
        pool.wait_ge(scattered, 16 * NT)

    @block.scalar
    def _(act):
        act.wait_ge(exps, 1)
        nc.scalar.activation(ex[:, :, :], ex[:, :, :], ACT.Exp).then_inc(exps, 1)

    @block.tensor
    def _(pe):
        pe.wait_ge(consts, N_CONST)
        pe.wait_ge(placed, 1)
        flat = onehot_b[:, :, :].rearrange("p n e -> p (n e)")
        for n in range(NT):
            mm = nc.tensor.matmul(bank[1][:, 0:NE], ones[:, :], onehot_b[:, n], start=n == 0, stop=n == NT - 1)
        mm.then_inc(counted, 1)
        nc.tensor.matmul(bank[0][:, :], below[:, :], flat, start=True, stop=False)
        for n in range(1, NT):
            mm = nc.tensor.matmul(bank[0][:, n * NE:], ones[:, :], flat[:, 0:(NT - n) * NE], start=False,
                                  stop=n == NT - 1)
        mm.then_inc(counted, 1)

    @block.vector
    def _(dve):
        count = [0]

        def step(ins):
            count[0] += 1
            ins.then_inc(steps_done, 1)
            dve.wait_ge(steps_done, count[0])

        def over_experts(t):
            return t[:, :].unsqueeze(2).broadcast_to([P, NT, NE])

        def over_tiles(t):
            return t[:, :].unsqueeze(1).broadcast_to([P, NT, NE])

        v = nc.vector
        step(v.tensor_reduce(mx[:, :], logits[:, :, :], AX.X, ALU.max))
        v.tensor_tensor(ex[:, :, :], logits[:, :, :], over_experts(mx), ALU.subtract).then_inc(exps, 1)
        dve.wait_ge(consts, N_CONST)
        step(v.tensor_tensor(eq[:, :, :], logits[:, :, :], over_experts(mx), ALU.is_equal))
        step(v.tensor_tensor(eq[:, :, :], eq[:, :, :], over_tiles(rev), ALU.mult))
        step(v.tensor_reduce(best[:, :], eq[:, :, :], AX.X, ALU.max))
        step(v.tensor_tensor(onehot[:, :, :], eq[:, :, :], over_experts(best), ALU.is_equal))
        v.tensor_copy(onehot_b[:, :, :], onehot[:, :, :]).then_inc(placed, 1)
        dve.wait_ge(exps, 2)
        step(v.tensor_reduce(den[:, :], ex[:, :, :], AX.X, ALU.add))
        step(v.reciprocal(top[:, :], den[:, :]))
        dve.wait_ge(counted, 1)
        each = bank[1][:, 0:NE].unsqueeze(2).broadcast_to([P, NE, NT - 1])
        step(v.tensor_tensor(over[:, :, 1:NT], each, marks[:, 1:NT].unsqueeze(1).broadcast_to([P, NE, NT - 1]), ALU.is_gt))
        step(v.tensor_reduce(tiles[:, :], over[:, :, 1:NT], AX.X, ALU.add))
        step(v.tensor_tensor_scan(end[:, :], tiles[:, :], tiles[:, :], 0.0, ALU.add, ALU.bypass))
        step(v.tensor_tensor(base[:, :], end[:, :], tiles[:, :], ALU.subtract))
        step(v.tensor_scalar(base[:, :], base[:, :], float(P), float((NE - 1) * P), ALU.mult, ALU.add))
        dve.wait_ge(counted, 2)
        v.tensor_tensor(ranks[:, :, :], bank[0][:, :].rearrange("p (n e) -> p n e", e=NE), onehot[:, :, :],
                        ALU.mult).then_inc(steps_done, 1)
        count[0] += 1
        step(v.tensor_tensor(bases[:, :, :], onehot[:, :, :], over_tiles(base), ALU.mult))
        v.tensor_reduce(rank[:, :], ranks[:, :, :], AX.X, ALU.add).then_inc(steps_done, 1)
        v.tensor_reduce(beyond[:, :], bases[:, :, :], AX.X, ALU.add).then_inc(steps_done, 1)
        count[0] += 2
        step(v.tensor_scalar(own[:, :], best[:, :], -float(P), float(NE * P), ALU.mult, ALU.add))
        v.tensor_scalar(first[:, :], rank[:, :], float(P), None, ALU.is_ge).then_inc(steps_done, 1)
        count[0] += 1
        step(v.tensor_tensor(beyond[:, :], beyond[:, :], own[:, :], ALU.subtract))
        step(v.tensor_tensor(beyond[:, :], beyond[:, :], first[:, :], ALU.mult))
        step(v.tensor_tensor(own[:, :], own[:, :], rank[:, :], ALU.add))
        step(v.tensor_tensor(own[:, :], own[:, :], beyond[:, :], ALU.add))
        v.tensor_copy(pos[:, :], own[:, :]).then_inc(routed, 1)
        step(v.tensor_tensor(done[:, :, :], end[:, :].unsqueeze(1).broadcast_to([P, NOVER, NE]),
                             steps[:, :].unsqueeze(2).broadcast_to([P, NOVER, NE]), ALU.is_le))
        step(v.tensor_reduce(expert_f[:, :], done[:, :, :], AX.X, ALU.add))
        step(v.tensor_scalar(expert_f[:, :], expert_f[:, :], float(NE - 1), None, ALU.min))
        v.tensor_copy(tile_expert[:, :], expert_f[0:1, :]).then_inc(routed, 1)


def multiply(nc, held, block, ins, tile_expert, identity, sorted_x, sorted_y, routed, scattered, early, t_in,
             early_in, bank):
    maskT = ins["maskT"]
    RING = 4
    MASKS = 2 * RING
    EARLY = MASKS - 1

    def sb(name, shape, dtype=fp32):
        return held.enter_context(nc.sbuf_tensor("e_" + name, shape, dtype))

    def sem(name):
        return held.enter_context(nc.semaphore("e_" + name))

    ternary, low = sb("ternary", [P, DC, D]), sb("low", [P, DC, D])
    scale = sb("scale", [P, D])
    m = [early[:, 2], early[:, 1], early[:, 0]] + [sb(f"m{i}", [P, DC, D]) for i in range(3, MASKS - 1)] + [early[:, 3]]
    xs = [sb(f"xs{i}", [P, D]) for i in range(MASKS)]
    xt = [sb(f"xt{i}", [P, D]) for i in range(RING)]
    ys = [sb(f"ys{i}", [P, D]) for i in range(MASKS)]
    t_steps, scale_in = sem("t_steps"), sem("scale_in")
    m_in = early_in + [sem(f"m_in{i}") for i in range(len(early_in), MASKS)]
    x_in, y_out = ([sem(f"{k}{i}") for i in range(MASKS)] for k in ("x_in", "y_out"))
    counted = ("masked", "turned", "x_copied", "y", "y_copied")
    s = {k: sem(k) for k in counted}

    def passes(eng, body):
        with eng.Fori(0, NSLOT // MASKS) as i:
            for r in range(MASKS):
                body(i * MASKS + r, r)
        for t in range(NSLOT // MASKS * MASKS, NSLOT):
            body(t, t % MASKS)

    def through(t):
        return t + RING + 1

    def freed(t):
        return t + 1

    def arrived(t, r):
        return 16 // MASKS * (t - r) + 16

    def rows(dram, t):
        return dram[bass.ds(t * P, P), :] if type(t) is not int else dram[t * P:(t + 1) * P, :]

    @block.sync
    def _(sp):
        sp.dma_start(scale[:, :], ins["scale"].broadcast_to([P, D])).then_inc(scale_in, 16)

        def mask(t, r, e):
            if type(t) is not int or t >= MASKS:
                sp.wait_ge(s["y"], t - MASKS + RING + 1)
            src = maskT[e:e + 1] if type(e) is int else maskT[bass.ds(e, 1)]
            sp.dma_start(m[r][:, :, :], src.rearrange("o (c p) n -> p (o c) n", p=P)).then_inc(m_in[r], 16)

        def tokens(t, r):
            if type(t) is not int or t >= MASKS:
                sp.wait_ge(s["turned"], t - MASKS + RING + 1)
            sp.dma_start(xs[r][:, :], rows(sorted_x, t)).then_inc(x_in[r], 16)

        for k in counted:
            sp.sem_inc(s[k], RING)
        for o in y_out:
            sp.sem_inc(o, 16)
        for t in range(len(early_in), EARLY):
            mask(t, t, t)
        sp.wait_ge(routed, 2)
        sp.wait_ge(scattered, 16 * NT)
        for t in range(MASKS):
            tokens(t, t)
            if t == RING:
                sp.wait_ge(t_steps, 2)
                mask(EARLY, EARLY, EARLY)
        with sp.Fori(0, NE // MASKS - 1) as i:
            for r in range(MASKS):
                t = (i + 1) * MASKS + r
                tokens(t, r)
                mask(t, r, t)
        for t in range(NE, NSLOT):
            tokens(t, t % MASKS)
            mask(t, t % MASKS, sp.value_load(tile_expert[0:1, t - NE:t - NE + 1], min_val=0, max_val=NE - 1))

    @block.vector
    def _(dve):
        dve.wait_ge(t_in, 16)
        nc.vector.tensor_scalar(low[:, :, :], m[MASKS - 1][:, :, :], -0.25, None, ALU.is_lt).then_inc(t_steps, 1)
        nc.vector.tensor_scalar(ternary[:, :, :], m[MASKS - 1][:, :, :], 0.25, None, ALU.is_gt).then_inc(t_steps, 1)
        dve.wait_ge(t_steps, 2)
        nc.vector.tensor_tensor(ternary[:, :, :], ternary[:, :, :], low[:, :, :], ALU.subtract).then_inc(t_steps, 1)
        dve.wait_ge(t_steps, 3)
        dve.wait_ge(scale_in, 16)
        nc.vector.tensor_tensor(ternary[:, :, :], ternary[:, :, :], scale[:, :].unsqueeze(1).broadcast_to([P, DC, D]),
                                ALU.mult).then_inc(t_steps, 1)
        dve.wait_ge(t_steps, 4)

        def body(t, r):
            dve.wait_ge(m_in[r], arrived(t, r))
            nc.vector.tensor_tensor(m[r][:, :, :], m[r][:, :, :], ternary[:, :, :], ALU.mult).then_inc(s["masked"], 1)
        passes(dve, body)

    @block.scalar
    def _(act):
        def turned_out(t, r):
            act.wait_ge(s["turned"], through(t))
            act.wait_ge(s["y"], freed(t))
            nc.scalar.activation(xt[r][:, :], bank[r][:, :], ACT.Copy).then_inc(s["x_copied"], 1)

        def y_out_of(t, r):
            act.wait_ge(s["y"], through(t))
            act.wait_ge(y_out[r], arrived(t, r))
            nc.scalar.activation(ys[r][:, :], bank[RING + r % RING][:, :], ACT.Copy).then_inc(s["y_copied"], 1)
            act.wait_ge(s["y_copied"], through(t))
            act.dma_start(rows(sorted_y, t), ys[r][:, :]).then_inc(y_out[r], 16)

        turned_out(0, 0)

        def body(t, r):
            if type(t) is not int or t < NSLOT - 1:
                turned_out(t + 1, (r + 1) % RING)
            y_out_of(t, r)
        passes(act, body)
        for r in range(MASKS):
            act.wait_ge(y_out[r], 16 * ((NSLOT - 1 - r) // MASKS + 2))

    @block.tensor
    def _(pe):
        def turn(t, r):
            pe.wait_ge(x_in[r], arrived(t, r))
            pe.wait_ge(s["x_copied"], freed(t))
            for c in range(DC):
                cols = slice(c * P, (c + 1) * P)
                mm = nc.tensor.transpose(bank[r % RING][:, cols], xs[r][:, cols], identity[:, :])
            mm.then_inc(s["turned"], 1)

        turn(0, 0)

        def body(t, r):
            if type(t) is not int or t < NSLOT - 1:
                turn(t + 1, (r + 1) % MASKS)
            pe.wait_ge(s["x_copied"], through(t))
            pe.wait_ge(s["masked"], through(t))
            pe.wait_ge(s["y_copied"], freed(t))
            for c in range(DC):
                mm = nc.tensor.matmul(bank[RING + r % RING][:, :], xt[r % RING][:, c * P:(c + 1) * P], m[r][:, c],
                                      start=c == 0, stop=c == DC - 1)
            mm.then_inc(s["y"], 1)
        passes(pe, body)


def stage_last(nc, out, acc, pos, top, sorted_y):
    with ExitStack() as held:
        def sb(name, shape, dtype=fp32):
            return held.enter_context(nc.sbuf_tensor("l_" + name, shape, dtype))

        def sem(name):
            return held.enter_context(nc.semaphore("l_" + name))

        y = sb("y", [P, NT, D])
        stats, moments = sb("stats", [P, NT, 6]), sb("moments", [P, NT, 2])
        rstd, shift, eps = sb("rstd", [P, NT]), sb("shift", [P, NT]), sb("eps", [P, 1])
        y_in = [sem(f"y_in{n}") for n in range(NT)]
        eps_set, summed, stat, moment, root, shift_made, normed, out_done = (
            sem(k) for k in ("eps_set", "summed", "stat", "moment", "root", "shift_made", "normed", "out_done"))
        block = held.enter_context(nc.Block())

        @block.gpsimd
        def _(pool):
            nc.gpsimd.memset(eps[:, :], EPS_LN).then_inc(eps_set, 1)
            for n in range(NT):
                nc.gpsimd.indirect_dma_start(
                    out=y[:, n, :], out_offset=None, in_=sorted_y,
                    in_offset=bass.IndirectOffsetOnAxis(ap=pos[:, n:n + 1], axis=0)).then_inc(y_in[n], 16)

        @block.vector
        def _(dve):
            def shift_of(n):
                dve.wait_ge(root, 2 * n + 2)
                nc.vector.scalar_tensor_tensor(shift[:, n:n + 1], moments[:, n, 0:1], -1.0, rstd[:, n:n + 1],
                                               ALU.mult, ALU.mult).then_inc(shift_made, 1)

            for n in range(NT + 2):
                if n < NT:
                    dve.wait_ge(y_in[n], 16)
                    nc.vector.scalar_tensor_tensor(acc[:, n], y[:, n], top[:, n:n + 1], acc[:, n],
                                                   ALU.mult, ALU.add).then_inc(summed, 1)
                if n >= 2:
                    dve.wait_ge(stat, n - 1)
                    nc.vector.bn_aggr(moments[:, n - 2], stats[:, n - 2]).then_inc(moment, 1)
                if 1 <= n <= NT:
                    dve.wait_ge(summed, n)
                    nc.vector.bn_stats(stats[:, n - 1], acc[:, n - 1]).then_inc(stat, 1)
                if n >= 3:
                    shift_of(n - 3)
            shift_of(NT - 1)

        @block.scalar
        def _(act):
            def finish(n):
                act.wait_ge(shift_made, n + 1)
                nc.scalar.activation(acc[:, n], acc[:, n], ACT.Identity, scale=rstd[:, n:n + 1],
                                     bias=shift[:, n:n + 1]).then_inc(normed, 1)

            act.wait_ge(eps_set, 1)
            for n in range(NT):
                act.wait_ge(moment, n + 1)
                nc.scalar.activation(rstd[:, n:n + 1], moments[:, n, 1:2], ACT.Ln, bias=eps[:, 0:1]).then_inc(root, 1)
                act.wait_ge(root, 2 * n + 1)
                nc.scalar.activation(rstd[:, n:n + 1], rstd[:, n:n + 1], ACT.Exp, scale=-0.5).then_inc(root, 1)
                if n >= 1:
                    finish(n - 1)
            finish(NT - 1)

        @block.sync
        def _(sp):
            for n in range(NT):
                sp.wait_ge(normed, n + 1)
                sp.dma_start(out[n * P:(n + 1) * P, :], acc[:, n]).then_inc(out_done, 16)
            sp.wait_ge(out_done, 16 * NT)


def build(nc, out, ins):
    with ExitStack() as held:
        def sb(name, shape, dtype=fp32):
            return held.enter_context(nc.sbuf_tensor(name, shape, dtype))

        pairs = [held.enter_context(nc.psum_tensor(f"bank{i}", [P, 2, 512], fp32)) for i in range(4)]
        bank = [pairs[i // 2][:, i % 2, :] for i in range(8)]
        acc = sb("acc", [P, NT, D])
        identity = sb("identity", [P, P])
        logits = sb("logits", [P, NT, NE])
        pos, top = sb("pos", [P, NT], u32), sb("top", [P, NT])
        tile_expert = sb("tile_expert", [1, NOVER], i32)
        sorted_x = nc.dram_tensor("sorted_x", [NSLOT * P, D], fp32, kind="Internal").ap()
        sorted_y = nc.dram_tensor("sorted_y", [NSLOT * P, D], fp32, kind="Internal").ap()

        late = held.enter_context(ExitStack())
        with ExitStack() as part:
            xyh = part.enter_context(nc.sbuf_tensor("xyh", [P, DC, T], fp32r))
            xyl = part.enter_context(nc.sbuf_tensor("xyl", [P, DC, T], fp32r))
            wh = part.enter_context(nc.sbuf_tensor("wh", [P, 3, DC, D], fp32r))
            wl = part.enter_context(nc.sbuf_tensor("wl", [P, 3, DC, D], fp32r))
            used_sems = stage_qkv(nc, ins, xyh, xyl, wh, wl, acc, bank)
            with nc.sbuf_tensor("early", [P, 4, DC, D], fp32, side="right") as early:
                pass
            wqh, wql = (late.enter_context(nc.sbuf_tensor(name, [P, DC, D], fp32r, side="right"))
                        for name in ("wqh", "wql"))
            zeros = part.enter_context(nc.sbuf_tensor("zeros", [P, D], fp32))
            stage_swiglu(nc, ins, xyh, xyl, wh, wl, acc, identity, zeros, sorted_x, wqh, wql, used_sems, bank)
        t_in = held.enter_context(nc.semaphore("t_in"))
        early_in = [held.enter_context(nc.semaphore(f"early_in{i}")) for i in range(3)]
        stage_cross(nc, ins, acc, logits, identity, wqh, wql, early, t_in, early_in, pairs)
        late.close()
        with nc.sbuf_tensor("early_kept", [P, 4, DC, D], fp32, side="right"):
            stage_experts(nc, ins, acc, logits, identity, pos, top, tile_expert, sorted_x, sorted_y, early, t_in,
                          early_in, bank)
        stage_last(nc, out, acc, pos, top, sorted_y)


def layouts(given):
    g = {name: np.asarray(a) for name, a in given.items()}

    def keys_values(w):
        w = w.reshape(w.shape[0], H, 2, HD)
        return w[:, :, 0].reshape(-1, D), w[:, :, 1].reshape(-1, D)

    def column(b):
        return b.reshape(DC, P).T

    parts = 8
    inner = g["L0_attn_w_out"].shape[1]
    wk_main, wv_main = keys_values(np.concatenate([g["L0_xattn_Wk"], g["L0_xattn_Wv"]], 1))
    bk_main, bv_main = keys_values(np.concatenate([g["L0_xattn_bk"], g["L0_xattn_bv"]])[None])
    w_last, b_last = g["L0_xattn_Wkv_dca"], g["L0_xattn_bkv_dca"]
    biases = np.zeros((P, 6, DC), np.float32)
    biases[:, 0], biases[:, 1], biases[:, 2] = column(g["L0_xattn_bq"]), column(bk_main[0]), column(b_last[:D])
    for n, name in enumerate(("kn", "kn_dca", "qn")):
        biases[:, 3 + n, 0] = np.tile(g[f"L0_xattn_{name}_w"], HC)
        biases[:, 3 + n, 1] = np.tile(g[f"L0_xattn_{name}_b"], HC)
    ins = dict(
        x=g["x"].reshape(T, D), xT=g["x"].transpose(0, 2, 1),
        wqkvT=g["L0_attn_w_qkv"].reshape(3, D, D).transpose(0, 2, 1),
        wsT=g["L0_attn_w_swiglu"].reshape(2, parts, inner // parts, DC, P).transpose(1, 4, 3, 0, 2),
        woT=g["L0_attn_w_out"].reshape(D, parts, inner // parts // P, P).transpose(1, 3, 2, 0),
        wk_main=wk_main, wv_main=wv_main, wk_last=w_last[:, :D], wv_last=w_last[:, D:],
        ctxT=g["ctx_1024"].transpose(2, 0, 1), biases=biases, bv=np.stack([bv_main[0], b_last[D:]])[None],
        wq=g["L0_xattn_Wq"], wo=g["L0_xattn_Wo"], bo=g["L0_xattn_bo"][None],
        w_ffnT=g["L0_ffn_weight"].T, scale=g["L0_ffn_scale"][None],
        maskT=g["L0_ffn_expert_masks"].transpose(0, 2, 1), routerT=g["L0_ffn_router_w"].T)
    return {name: np.ascontiguousarray(a) for name, a in ins.items()}


def kernel(**inputs):
    import concourse.bacc as bacc
    from concourse.bass_utils import run_bass_kernel_spmd

    nc = bacc.Bacc("TRN2", target_bir_lowering=False, num_devices=1)
    arrays = layouts(inputs)
    ins = {name: nc.dram_tensor(f"in_{name}_dram", a.shape, mybir.dt.from_np(a.dtype), kind="ExternalInput").ap()
           for name, a in arrays.items()}
    out = nc.dram_tensor("out_0_dram", (T, D), fp32, kind="ExternalOutput").ap()
    build(nc, out, ins)
    r = run_bass_kernel_spmd(nc, [{f"in_{name}_dram": a for name, a in arrays.items()}], core_ids=[0])
    return r.results[0]["out_0_dram"].reshape(NBATCH, S, D)
```
